# Optimizing a Trainium2 kernel written in Bass

```python
import numpy as np
import jax
import jax.numpy as jnp

def _softmax(x, axis=-1):
    return jax.nn.softmax(x, axis=axis)

def _gelu(x):
    return jax.nn.gelu(x, approximate=True)

def _silu(x):
    return jax.nn.silu(x)

def _sigmoid(x):
    return jax.nn.sigmoid(x)

def _layernorm(x, axis=-1, eps=1e-05):
    m = jnp.mean(x, axis=axis, keepdims=True)
    v = jnp.var(x, axis=axis, keepdims=True)
    return (x - m) / jnp.sqrt(v + eps)

def _scatter_add(tgt, idx, src, axis=0):
    return tgt.at[idx].add(src)

def _segment_sum(src, seg, n):
    return jax.ops.segment_sum(src, seg, n)
kernel_name = 'mk_sandwich_d1_jaxref_r8_488e34'

def setup_inputs(seed: int=0):
    np.random.seed(seed)
    _w = jnp.asarray

    def _L0_attn_setup():
        import jax, jax.numpy as jnp
        import numpy as np
        B, S, E, H, P = (2, 256, 128, 16, 256)
        HD = E // H
        key = jax.random.key(seed)
        ks = jax.random.split(key, 10)
        std = E ** (-0.5)
        x = jax.random.normal(ks[0], (B, S, E), jnp.float32)
        Wq = jax.random.normal(ks[1], (E, E), jnp.float32) * std
        Wk = jax.random.normal(ks[2], (E, E), jnp.float32) * std
        Wv = jax.random.normal(ks[3], (E, E), jnp.float32) * std
        Wo = jax.random.normal(ks[4], (E, E), jnp.float32) * std
        rel_key = jax.random.normal(ks[5], (P, HD), jnp.float32) * 0.02
        z = jnp.zeros((E,), jnp.float32)
        return {'x': x, 'Wq': Wq, 'bq': z, 'Wk': Wk, 'bk': z, 'Wv': Wv, 'bv': z, 'Wo': Wo, 'bo': z, 'rel_key': rel_key}
    _L0_attn_in = _L0_attn_setup()

    def _L0_ffn_setup():
        import jax, jax.numpy as jnp
        import numpy as np
        DIM = 128
        DEPTH = 6
        HEADS = 16
        DIM_HEAD = 64
        WINDOW = 32
        INNER = HEADS * DIM_HEAD
        DIM_INNER = int(DIM * 4 * 2 / 3)
        QK_SCALE = 8.0

        def shift_tokens(t):
            a, s = jnp.split(t, 2, -1)
            s = jnp.pad(s, ((0, 0), (1, 0), (0, 0)))[:, :-1]
            return jnp.concatenate([a, s], -1)

        def l2norm(t):
            return t / jnp.maximum(jnp.linalg.norm(t, axis=-1, keepdims=True), 1e-12)

        def rotate_half(x):
            x1, x2 = jnp.split(x, 2, -1)
            return jnp.concatenate([-x2, x1], -1)

        def rotary_tables(n):
            half = jnp.arange(0, DIM_HEAD, 2, dtype=jnp.float32)
            inv_freq = 1.0 / 10000.0 ** (half / DIM_HEAD)
            t = jnp.arange(n, dtype=jnp.float32)
            freqs = t[:, None] * inv_freq[None, :]
            freqs = jnp.concatenate([freqs, freqs], -1)
            base_scale = (half + 0.4 * DIM_HEAD) / (1.4 * DIM_HEAD)
            power = (t - n // 2) / (WINDOW // 2)
            scale = base_scale[None, :] ** power[:, None]
            scale = jnp.concatenate([scale, scale], -1)
            return (freqs, scale)

        def local_attention(q, k, v):
            b, h, n, d = q.shape
            w = WINDOW
            nw = n // w
            bq = q.reshape(b, h, nw, w, d)
            bk = k.reshape(b, h, nw, w, d)
            bv = v.reshape(b, h, nw, w, d)

            def look(t):
                p = jnp.pad(t, ((0, 0), (0, 0), (1, 0), (0, 0), (0, 0)))
                return jnp.concatenate([p[:, :, :nw], p[:, :, 1:]], axis=3)
            bk2, bv2 = (look(bk), look(bv))
            seq = jnp.arange(n).reshape(nw, w)
            seq_p = jnp.pad(seq, ((1, 0), (0, 0)), constant_values=-1)
            jt = jnp.concatenate([seq_p[:nw], seq_p[1:]], axis=1)
            it = seq[:, :, None]
            jb = jt[:, None, :]
            mask = (it < jb) | (it > jb + w) | (jb == -1)
            sim = jnp.einsum('bhwie,bhwje->bhwij', bq, bk2) * QK_SCALE
            sim = jnp.where(mask, -jnp.finfo(sim.dtype).max, sim)
            attn = jax.nn.softmax(sim, -1)
            out = jnp.einsum('bhwij,bhwje->bhwie', attn, bv2)
            return out.reshape(b, h, n, d)

        def attn_layer(x, Wqkv, qs, ksc, Wo):
            b, n, _ = x.shape
            qkv = x @ Wqkv
            q, k, v = jnp.split(qkv, 3, -1)
            sh = lambda t: t.reshape(b, n, HEADS, DIM_HEAD).transpose(0, 2, 1, 3)
            q, k, v = (sh(q), sh(k), sh(v))
            q = l2norm(q) * qs
            k = l2norm(k) * ksc
            freqs, scale = rotary_tables(n)
            cos, sin = (jnp.cos(freqs), jnp.sin(freqs))
            q = q * cos * scale + rotate_half(q) * sin * scale
            inv = 1.0 / scale
            k = k * cos * inv + rotate_half(k) * sin * inv
            out = local_attention(q, k, v)
            out = out.transpose(0, 2, 1, 3).reshape(b, n, INNER)
            return out @ Wo

        def ffn_layer(x, g, bln, W1, b1, W2, b2):
            mu = x.mean(-1, keepdims=True)
            var = ((x - mu) ** 2).mean(-1, keepdims=True)
            xn = (x - mu) / jnp.sqrt(var + 1e-05) * g + bln
            hg = xn @ W1 + b1
            a, gate = jnp.split(hg, 2, -1)
            return a * jax.nn.gelu(gate, approximate=False) @ W2 + b2
        key = jax.random.key(seed)
        ks = jax.random.split(key, 8)
        B, N = (2, 256)
        init = lambda k, shape: jax.random.normal(k, shape, jnp.float32) * 0.02
        return {'x': jax.random.normal(ks[0], (B, N, DIM), jnp.float32), 'Wqkv': init(ks[1], (DEPTH, DIM, 3 * INNER)), 'q_scale': jnp.ones((DEPTH, DIM_HEAD), jnp.float32), 'k_scale': jnp.ones((DEPTH, DIM_HEAD), jnp.float32), 'Wo': init(ks[2], (DEPTH, INNER, DIM)), 'ln_g': jnp.ones((DEPTH, DIM), jnp.float32), 'ln_b': jnp.zeros((DEPTH, DIM), jnp.float32), 'W1': init(ks[3], (DEPTH, DIM, 2 * DIM_INNER)), 'b1': jnp.zeros((DEPTH, 2 * DIM_INNER), jnp.float32), 'W2': init(ks[4], (DEPTH, DIM_INNER, DIM)), 'b2': jnp.zeros((DEPTH, DIM), jnp.float32)}
    _L0_ffn_in = _L0_ffn_setup()
    _d = {'L0_attn_x': _L0_attn_in['x'], 'L0_attn_Wq': _L0_attn_in['Wq'], 'L0_attn_bq': _L0_attn_in['bq'], 'L0_attn_Wk': _L0_attn_in['Wk'], 'L0_attn_bk': _L0_attn_in['bk'], 'L0_attn_Wv': _L0_attn_in['Wv'], 'L0_attn_bv': _L0_attn_in['bv'], 'L0_attn_Wo': _L0_attn_in['Wo'], 'L0_attn_bo': _L0_attn_in['bo'], 'L0_attn_rel_key': _L0_attn_in['rel_key'], 'L0_ffn_Wqkv': _L0_ffn_in['Wqkv'], 'L0_ffn_q_scale': _L0_ffn_in['q_scale'], 'L0_ffn_k_scale': _L0_ffn_in['k_scale'], 'L0_ffn_Wo': _L0_ffn_in['Wo'], 'L0_ffn_ln_g': _L0_ffn_in['ln_g'], 'L0_ffn_ln_b': _L0_ffn_in['ln_b'], 'L0_ffn_W1': _L0_ffn_in['W1'], 'L0_ffn_b1': _L0_ffn_in['b1'], 'L0_ffn_W2': _L0_ffn_in['W2'], 'L0_ffn_b2': _L0_ffn_in['b2']}
    _x0 = _d['L0_attn_x']
    _d['L0_attn_x'] = jax.random.normal(jax.random.fold_in(jax.random.key(seed), 1), (4, 1024, 128), dtype=_x0.dtype)
    del _x0
    return _d

def reference(L0_attn_x, L0_attn_Wq, L0_attn_bq, L0_attn_Wk, L0_attn_bk, L0_attn_Wv, L0_attn_bv, L0_attn_Wo, L0_attn_bo, L0_attn_rel_key, L0_ffn_Wqkv, L0_ffn_q_scale, L0_ffn_k_scale, L0_ffn_Wo, L0_ffn_ln_g, L0_ffn_ln_b, L0_ffn_W1, L0_ffn_b1, L0_ffn_W2, L0_ffn_b2):

    def _L0_attn_ref(x, Wq, bq, Wk, bk, Wv, bv, Wo, bo, rel_key):
        import jax, jax.numpy as jnp
        import numpy as np
        B, S, E, H, P = (2, 256, 128, 16, 256)
        HD = E // H
        b, s, e = x.shape
        p, hd = rel_key.shape
        h = e // hd
        scale = hd ** (-0.5)

        def split_heads(t):
            return t.reshape(b, s, h, hd).transpose(0, 2, 1, 3)
        q = split_heads(x @ Wq + bq)
        k = split_heads(x @ Wk + bk)
        v = split_heads(x @ Wv + bv)
        scores = jnp.einsum('bhid,bhjd->bhij', q, k)
        rel = jnp.einsum('bhid,pd->bhip', q, rel_key)
        i = jnp.arange(s)[:, None]
        j = jnp.arange(s)[None, :]
        rel_idx = jnp.clip(j - i + p - 1, 0, p - 1)
        bias = jnp.take_along_axis(rel, jnp.broadcast_to(rel_idx[None, None], (b, h, s, s)), axis=3)
        causal = j <= i
        logits = jnp.where(causal[None, None], (scores + bias) * scale, -jnp.inf)
        attn = jax.nn.softmax(logits, axis=-1)
        out = jnp.einsum('bhij,bhjd->bhid', attn, v)
        out = out.transpose(0, 2, 1, 3).reshape(b, s, e)
        return out @ Wo + bo

    def _L0_ffn_ref(x, Wqkv, q_scale, k_scale, Wo, ln_g, ln_b, W1, b1, W2, b2):
        import jax, jax.numpy as jnp
        import numpy as np
        DIM = 128
        DEPTH = 6
        HEADS = 16
        DIM_HEAD = 64
        WINDOW = 32
        INNER = HEADS * DIM_HEAD
        DIM_INNER = int(DIM * 4 * 2 / 3)
        QK_SCALE = 8.0

        def shift_tokens(t):
            a, s = jnp.split(t, 2, -1)
            s = jnp.pad(s, ((0, 0), (1, 0), (0, 0)))[:, :-1]
            return jnp.concatenate([a, s], -1)

        def l2norm(t):
            return t / jnp.maximum(jnp.linalg.norm(t, axis=-1, keepdims=True), 1e-12)

        def rotate_half(x):
            x1, x2 = jnp.split(x, 2, -1)
            return jnp.concatenate([-x2, x1], -1)

        def rotary_tables(n):
            half = jnp.arange(0, DIM_HEAD, 2, dtype=jnp.float32)
            inv_freq = 1.0 / 10000.0 ** (half / DIM_HEAD)
            t = jnp.arange(n, dtype=jnp.float32)
            freqs = t[:, None] * inv_freq[None, :]
            freqs = jnp.concatenate([freqs, freqs], -1)
            base_scale = (half + 0.4 * DIM_HEAD) / (1.4 * DIM_HEAD)
            power = (t - n // 2) / (WINDOW // 2)
            scale = base_scale[None, :] ** power[:, None]
            scale = jnp.concatenate([scale, scale], -1)
            return (freqs, scale)

        def local_attention(q, k, v):
            b, h, n, d = q.shape
            w = WINDOW
            nw = n // w
            bq = q.reshape(b, h, nw, w, d)
            bk = k.reshape(b, h, nw, w, d)
            bv = v.reshape(b, h, nw, w, d)

            def look(t):
                p = jnp.pad(t, ((0, 0), (0, 0), (1, 0), (0, 0), (0, 0)))
                return jnp.concatenate([p[:, :, :nw], p[:, :, 1:]], axis=3)
            bk2, bv2 = (look(bk), look(bv))
            seq = jnp.arange(n).reshape(nw, w)
            seq_p = jnp.pad(seq, ((1, 0), (0, 0)), constant_values=-1)
            jt = jnp.concatenate([seq_p[:nw], seq_p[1:]], axis=1)
            it = seq[:, :, None]
            jb = jt[:, None, :]
            mask = (it < jb) | (it > jb + w) | (jb == -1)
            sim = jnp.einsum('bhwie,bhwje->bhwij', bq, bk2) * QK_SCALE
            sim = jnp.where(mask, -jnp.finfo(sim.dtype).max, sim)
            attn = jax.nn.softmax(sim, -1)
            out = jnp.einsum('bhwij,bhwje->bhwie', attn, bv2)
            return out.reshape(b, h, n, d)

        def attn_layer(x, Wqkv, qs, ksc, Wo):
            b, n, _ = x.shape
            qkv = x @ Wqkv
            q, k, v = jnp.split(qkv, 3, -1)
            sh = lambda t: t.reshape(b, n, HEADS, DIM_HEAD).transpose(0, 2, 1, 3)
            q, k, v = (sh(q), sh(k), sh(v))
            q = l2norm(q) * qs
            k = l2norm(k) * ksc
            freqs, scale = rotary_tables(n)
            cos, sin = (jnp.cos(freqs), jnp.sin(freqs))
            q = q * cos * scale + rotate_half(q) * sin * scale
            inv = 1.0 / scale
            k = k * cos * inv + rotate_half(k) * sin * inv
            out = local_attention(q, k, v)
            out = out.transpose(0, 2, 1, 3).reshape(b, n, INNER)
            return out @ Wo

        def ffn_layer(x, g, bln, W1, b1, W2, b2):
            mu = x.mean(-1, keepdims=True)
            var = ((x - mu) ** 2).mean(-1, keepdims=True)
            xn = (x - mu) / jnp.sqrt(var + 1e-05) * g + bln
            hg = xn @ W1 + b1
            a, gate = jnp.split(hg, 2, -1)
            return a * jax.nn.gelu(gate, approximate=False) @ W2 + b2
        for i in range(DEPTH):
            x = attn_layer(shift_tokens(x), Wqkv[i], q_scale[i], k_scale[i], Wo[i]) + x
            x = ffn_layer(shift_tokens(x), ln_g[i], ln_b[i], W1[i], b1[i], W2[i], b2[i]) + x
        return x
    x = L0_attn_x
    x = x + _layernorm(_L0_attn_ref(_layernorm(x, axis=-1), L0_attn_Wq, L0_attn_bq, L0_attn_Wk, L0_attn_bk, L0_attn_Wv, L0_attn_bv, L0_attn_Wo, L0_attn_bo, L0_attn_rel_key), axis=-1)
    x = x + _layernorm(_L0_ffn_ref(_layernorm(x, axis=-1), L0_ffn_Wqkv, L0_ffn_q_scale, L0_ffn_k_scale, L0_ffn_Wo, L0_ffn_ln_g, L0_ffn_ln_b, L0_ffn_W1, L0_ffn_b1, L0_ffn_W2, L0_ffn_b2), axis=-1)
    return x

_drawn_inputs = setup_inputs


def setup_inputs(seed=0):
    import zlib

    import numpy as np

    out = dict(_drawn_inputs(seed))
    spreads = {'L0_attn_bq': (0.0, 0.1),
     'L0_attn_bk': (0.0, 2.0),
     'L0_attn_bv': (0.0, 0.1),
     'L0_attn_bo': (0.0, 0.1),
     'L0_ffn_q_scale': (1.0, 0.6),
     'L0_ffn_k_scale': (1.0, 0.6),
     'L0_ffn_ln_g': (1.0, 0.6),
     'L0_ffn_ln_b': (0.0, 0.8),
     'L0_ffn_b1': (0.0, 0.8),
     'L0_ffn_b2': (0.0, 0.338)}
    factors = {'L0_attn_rel_key': 7.969, 'L0_ffn_W1': 4.41, 'L0_ffn_W2': 4.301}
    for name, (base, spread) in spreads.items():
        noise = np.random.default_rng([zlib.crc32(name.encode()), seed]).standard_normal(out[name].shape)
        drawn = base * np.exp(spread * noise) if base else spread * noise
        out[name] = jnp.asarray(drawn.astype(out[name].dtype))
    for name, factor in factors.items():
        out[name] = (out[name] * factor).astype(out[name].dtype)
    return out
```

```python
from contextlib import ExitStack

import concourse.bass as bass
import numpy as np
from concourse import mybir

F32 = mybir.dt.float32
BF16 = mybir.dt.bfloat16
ALU = mybir.AluOpType
ACT = mybir.ActivationFunctionType
AX = mybir.AxisListType
ds = bass.ds

P = 128
B, S, E = 4, 1024, 128
NT = B * S // P
TB = S // P
SLOTS = B * (TB + 1)
G = 4
H_A, D_A, REL = 16, 8, 256
BAND = 3 * P
HEADS_A = B * H_A
SC_A = D_A ** -0.5
H, D = 16, 64
INNER = H * D
DEPTH, WIN = 6, 32
HID = 341
PIECES = [(c, min(P, HID - c)) for c in range(0, HID, P)]
KW = WIN + P
QK_SCALE = 8.0
NEG = -1e30
EPS = 1e-5
TILES = DEPTH * NT
ZERO_SLOT = TB + 1


def slot(m):
    return m + m // TB + 1


class Event:

    def __init__(self, sem, per=1, credit=0):
        self.sem, self.per, self.credit = sem, per, credit

    def open(self, eng):
        eng.sem_inc(self.sem, self.per * self.credit)

    def at(self, eng, n, k=None):
        v = self.per * (n + self.credit) + (self.per if k is None else k)
        if isinstance(v, int) and v <= self.per * self.credit:
            return
        eng.wait_ge(self.sem, v)


class Chain(Event):

    def start(self, eng, n, k=0):
        self.eng, self.n, self.k = eng, n, k

    def link(self, ins):
        self.k += 1
        assert self.k <= self.per
        ins.then_inc(self.sem, 1)
        self.at(self.eng, self.n, self.k)


def step_in(dve, cell):
    dve.memset(cell, 0.0)


class LayerNorm:

    def __init__(self, part, name, n, per=1):
        self.st = part.sb(name + "_stats", [P, n, 9])
        self.power = part.sb(name + "_power", [P, n, 1])
        self.power_ev = part.ev(name + "_power_ev")
        self.cell = part.sb(name + "_cell", [P, 1])
        self.chain = part.chain(name + "_chain", 2 * per)
        self.stats_ev, self.rstd_ev = part.ev(name + "_stats_ev", per), part.ev(name + "_rstd_ev", per)

    def open(self, pool):
        pool.memset(self.power[:], -0.5).then_inc(self.power_ev.sem, 1)
        self.power_ev.at(pool, 0)

    def stats(self, dve, xs):
        step_in(dve, self.cell[:])
        for j, x in enumerate(xs):
            ins = dve.bn_stats(self.st[:, j, 0:6], x)
        self.chain.link(ins)
        step_in(dve, self.cell[:])
        for j in range(len(xs)):
            ins = dve.bn_aggr(self.st[:, j, 6:8], self.st[:, j, 0:6])
        self.chain.link(ins)
        n = len(xs)
        dve.tensor_scalar(self.st[:, 0:n, 7:8], self.st[:, 0:n, 7:8], EPS, None, ALU.add)\
            .then_inc(self.stats_ev.sem, 1)

    def rstd(self, pool, n, step, k=None):
        self.stats_ev.at(pool, step, k)
        pool.tensor_tensor(self.st[:, 0:n, 8:9], self.st[:, 0:n, 7:8], self.power[:, 0:n, :], ALU.pow)\
            .then_inc(self.rstd_ev.sem, 1)

    def apply(self, dve, xs, outs, step, k=None):
        self.rstd_ev.at(dve, step, k)
        for j, x in enumerate(xs):
            ins = dve.tensor_scalar(outs[j], x, self.st[:, j, 6:7], self.st[:, j, 8:9],
                                    ALU.subtract, ALU.mult)
        return ins


def wide(ap, n):
    return ap.unsqueeze(2).to_broadcast([ap.shape[0], ap.shape[1], n])


def over(ap, n):
    return ap.unsqueeze(1).to_broadcast([ap.shape[0], n, ap.shape[1]])


class Part:

    def __init__(self, nc, name):
        self.nc, self.name, self.ctx = nc, name, ExitStack()

    def __enter__(self):
        self.ctx.__enter__()
        return self

    def __exit__(self, *a):
        return self.ctx.__exit__(*a)

    def sb(self, name, shape, dt=F32):
        return self.ctx.enter_context(self.nc.sbuf_tensor(f"{self.name}_{name}", shape, dt))

    def psum(self):
        return self.ctx.enter_context(self.nc.psum_tensor(f"{self.name}_ps", [P, 8, 512], F32))

    def sem(self, name):
        return self.ctx.enter_context(self.nc.semaphore(f"{self.name}_{name}"))

    def ev(self, name, per=1, credit=0):
        return Event(self.sem(name), per, credit)

    def chain(self, name, per):
        return Chain(self.sem(name), per)

    def block(self):
        return self.ctx.enter_context(self.nc.Block())


def build(nc, a, out):
    qt_d = nc.dram_tensor("qt_scratch", [P, B * S], F32).ap()
    kt_d = nc.dram_tensor("kt_scratch", [P, B * S], F32).ap()
    skew = nc.dram_tensor("skew_scratch", [2, TB, P * BAND], F32).ap()
    with ExitStack() as top:
        X = top.enter_context(nc.sbuf_tensor("X", [P, SLOTS, E], F32))
        X2 = top.enter_context(nc.sbuf_tensor("X2", [P, NT, E], F32))
        ident = top.enter_context(nc.sbuf_tensor("ident", [P, P], F32))
        with nc.sbuf_tensor("V", [P, NT, E], F32) as V:
            first_projections(nc, a, X, V, ident, qt_d, kt_d, skew)
            first_attention(nc, a, V, X2, ident, qt_d, kt_d, skew)
        first_output(nc, a, X, X2, ident)
        layers(nc, a, X, ident)
        last_output(nc, X, X2, out)


def first_projections(nc, a, X, V, ident, qt_d, kt_d, skew):
    STEPS = NT // G
    with Part(nc, "pr") as t:
        Wq, Wk, Wv, bv = (t.sb(n, [P, E]) for n in ("Wq", "Wk", "Wv", "bv"))
        bq, bk, r0, bkr = (t.sb(n, [P, 1]) for n in ("bq", "bk", "r0", "bkr"))
        fill = t.sb("fill", [P, BAND])
        xh, xhT = t.sb("xh", [P, G, E]), t.sb("xhT", [P, G * P])
        qf, kf = t.sb("qf", [P, G * P]), t.sb("kf", [P, G * P])
        ps = t.psum()
        s_in, s_z, s_f, s_sk, s_bk = (t.sem(n) for n in ("in", "z", "f", "sk", "bk"))
        ln = LayerNorm(t, "ln", G)
        xh_done, t_mm, xhT_done = t.ev("xh"), t.ev("t", 1, 1), t.ev("xhT", 1, 1)
        q_mm, k_mm, v_mm = t.ev("qm"), t.ev("km"), t.ev("vm", 1, 1)
        q_ev, k_ev, v_ev = (t.ev(n, 1, 1) for n in ("qe", "ke", "ve"))
        q_out, k_out = t.ev("qo", 16, 1), t.ev("ko", 16, 1)
        block = t.block()

        @block.sync
        def _(e):
            for b in range(B):
                e.dma_start(X[:, b * (TB + 1) + 1:(b + 1) * (TB + 1), :],
                            a["L0_attn_x"][b].rearrange("(t p) d -> p t d", p=P)).then_inc(s_in, 16)
            for dst, src in ((Wq, "L0_attn_Wq"), (Wk, "L0_attn_Wk"), (Wv, "L0_attn_Wv"), (ident, "c_ident")):
                e.dma_start(dst[:], a[src]).then_inc(s_in, 16)
            for dst, src in ((bq, "L0_attn_bq"), (bk, "L0_attn_bk"), (r0, "rel0")):
                e.dma_start(dst[:], a[src].rearrange("(p o) -> p o", o=1)).then_inc(s_in, 16)
            e.dma_start(bv[:], a["L0_attn_bv"].partition_broadcast(P)).then_inc(s_in, 16)
            e.wait_ge(s_f, 2)
            for par in range(2):
                for i in range(TB):
                    e.dma_start(skew[par, i].rearrange("(p c) -> p c", c=BAND), fill[:]).then_inc(s_sk, 16)
            with e.Fori(0, STEPS) as i:
                q_ev.at(e, i)
                e.dma_start(qt_d[:, ds(i * (G * P), G * P)], qf[:]).then_inc(q_out.sem, 16)
                k_ev.at(e, i)
                e.dma_start(kt_d[:, ds(i * (G * P), G * P)], kf[:]).then_inc(k_out.sem, 16)
            e.wait_ge(s_sk, 16 * 2 * TB)
            q_out.at(e, STEPS - 1)
            k_out.at(e, STEPS - 1)

        @block.gpsimd
        def _(e):
            for b in range(B):
                e.memset(X[:, b * ZERO_SLOT, :], 0.0).then_inc(s_z, 1)
            e.memset(fill[:], 0.0).then_inc(s_f, 1)
            e.wait_ge(s_f, 1)
            e.affine_select(out=fill[:], in_=fill[:], compare_op=ALU.is_ge, fill=NEG, base=REL,
                            pattern=[[-1, BAND]], channel_multiplier=1).then_inc(s_f, 1)
            ln.open(e)
            with e.Fori(0, STEPS) as i:
                ln.rstd(e, G, i)

        @block.vector
        def _(e):
            v_ev.open(e)
            k_ev.open(e)
            k_out.open(e)
            e.wait_ge(s_in, 16 * 12)
            e.tensor_tensor(bkr[:], bk[:], r0[:], ALU.add).then_inc(s_bk, 1)
            e.wait_ge(s_bk, 1)
            with e.Fori(0, STEPS) as i:
                first = i * G + i // (TB // G) + 1
                ln.chain.start(e, i)
                xs = [X[:, ds(first + g, 1), :] for g in range(G)]
                ln.stats(e, xs)
                t_mm.at(e, i - 1)
                ln.apply(e, xs, [xh[:, g, :] for g in range(G)], i).then_inc(xh_done.sem, 1)
                k_mm.at(e, i)
                k_out.at(e, i - 1)
                e.tensor_scalar(kf[:], ps[:, 2, :], bkr[:, 0:1], None, ALU.add).then_inc(k_ev.sem, 1)
                v_mm.at(e, i)
                e.tensor_tensor(V[:, ds(i * G, G), :], ps[:, 3, :].rearrange("p (g d) -> p g d", g=G),
                                over(bv[:], G), ALU.add).then_inc(v_ev.sem, 1)

        @block.scalar
        def _(e):
            xhT_done.open(e)
            q_ev.open(e)
            q_out.open(e)
            e.wait_ge(s_in, 16 * 12)
            with e.Fori(0, STEPS) as i:
                t_mm.at(e, i)
                v_mm.at(e, i - 1)
                e.activation(xhT[:], ps[:, 0, :], ACT.Copy).then_inc(xhT_done.sem, 1)
                q_mm.at(e, i)
                q_out.at(e, i - 1)
                e.activation(qf[:], ps[:, 1, :], ACT.Identity, bias=bq[:, 0:1]).then_inc(q_ev.sem, 1)

        @block.tensor
        def _(e):
            t_mm.open(e)
            v_mm.open(e)
            e.wait_ge(s_in, 16 * 12)
            with e.Fori(0, STEPS) as i:
                xh_done.at(e, i)
                xhT_done.at(e, i - 1)
                for g in range(G):
                    mm = e.transpose(ps[:, 0, g * P:(g + 1) * P], xh[:, g, :], ident[:])
                mm.then_inc(t_mm.sem, 1)
                xhT_done.at(e, i)
                q_ev.at(e, i - 1)
                e.matmul(ps[:, 1, :], Wq[:], xhT[:], start=True, stop=True).then_inc(q_mm.sem, 1)
                k_ev.at(e, i - 1)
                e.matmul(ps[:, 2, :], Wk[:], xhT[:], start=True, stop=True).then_inc(k_mm.sem, 1)
                v_ev.at(e, i - 1)
                for g in range(G):
                    mm = e.matmul(ps[:, 3, g * P:(g + 1) * P], xhT[:, g * P:(g + 1) * P], Wv[:],
                                  start=True, stop=True)
                mm.then_inc(v_mm.sem, 1)


def first_attention(nc, a, V, O, ident, qt_d, kt_d, skew):
    JJ = TB // G
    NJ = sum(G * (u + 1) for u in range(JJ))
    with Part(nc, "at") as t:
        qh, kh = t.sb("qh", [D_A, 2, S]), t.sb("kh", [D_A, 2, S])
        relT, relD = t.sb("relT", [D_A, REL]), t.sb("relD", [D_A, REL])
        vh = t.sb("vh", [P, 2, TB, WIN])
        R = t.sb("R", [P, TB, REL])
        band = t.sb("band", [P, 2, TB, BAND])
        summed = t.sb("summed", [P, 2, BAND])
        mx, nb = t.sb("mx", [P, 2 * TB]), t.sb("nb", [P, TB])
        probs = [t.sb(f"probs{u}", [P, G, G * P * (u + 1)]) for u in range(JJ)]
        pT = t.sb("pT", [P, 2, G * P])
        part, sel = t.sb("part", [P, G * P]), t.sb("sel", [P, D_A + 1])
        rc, cell = t.sb("rc", [P, G]), t.sb("cell", [P, 1])
        ps = t.psum()
        s_in, s_set, s_rel = t.sem("in"), t.sem("set"), t.sem("rel")
        qk_in = t.ev("qkin", 32)
        vh_ev = t.ev("vh")
        r_mm, r_ev = t.ev("rm", TB // 2), t.ev("re", TB // 2, 1)
        r_out, r_in = t.ev("ro", 16, 1), t.ev("ri", 16, 2)
        s_mm = t.ev("sm", TB, 2)
        nb_ev = t.ev("nb", TB, 2)
        p_ev = t.ev("pe", TB, 1)
        t_mm = t.ev("tm", NJ, 1)
        tA, tD = t.ev("tA", NJ // 2, 1), t.ev("tD", NJ // 2, 1)
        pv_mm = t.ev("pv", NJ, 2)
        o_ev, g_mm, on = t.ev("oe", JJ), t.ev("gm", JJ, 1), t.ev("on", JJ, 1)
        c_max = t.chain("cm", 2 * TB - BAND // P)
        c_on = t.chain("co", JJ)
        block = t.block()
        R_BANK, T_BANKS, O_BANK = 0, (1, 6), 7

        def width(i):
            return P * (i + 1)

        def far(i):
            return P * max(0, i + 1 - BAND // P)

        def logits(i):
            lo = 2 + 2 * (i % 2)
            return ps[:, lo:lo + 2, :].rearrange("p b n -> p (b n)")

        def load_head(e, r, par):
            s_mm.at(e, r - 2)
            hd = r % HEADS_A
            row, col = hd % H_A * D_A, hd // H_A * S
            e.dma_start(qh[:, par, :], qt_d[ds(row, D_A), ds(col, S)]).then_inc(qk_in.sem, 16)
            e.dma_start(kh[:, par, :], kt_d[ds(row, D_A), ds(col, S)]).then_inc(qk_in.sem, 16)

        def skew_head(e, r, par):
            r_ev.at(e, r)
            r_in.at(e, r - 2)
            flat = skew[par]
            dst = bass.AP(flat.tensor, flat.offset + 1, [[BAND + 1, P], [P * BAND, TB], [1, REL]])
            e.dma_start(dst, R[:]).then_inc(r_out.sem, 16)
            nb_ev.at(e, r - 2)
            r_out.at(e, r)
            e.dma_start(band[:, par, :, :], flat.rearrange("t (p c) -> p t c", c=BAND))\
                .then_inc(r_in.sem, 16)

        def band_mm(e, r, par, j):
            if j == 0:
                qk_in.at(e, r)
            r_ev.at(e, r - 1 if j == 0 else r, None if j == 0 else j)
            for i in (2 * j, 2 * j + 1):
                mm = e.matmul(ps[:, R_BANK, i % 2 * REL:(i % 2 + 1) * REL], qh[:, par, i * P:(i + 1) * P],
                              relD[:], start=True, stop=True)
            mm.then_inc(r_mm.sem, 1)

        def band_copy(e, r, j):
            r_mm.at(e, r, j + 1)
            if j == 0:
                r_out.at(e, r - 1)
            e.activation(R[:, 2 * j:2 * j + 2, :], ps[:, R_BANK, :].rearrange("p (i n) -> p i n", i=2),
                         ACT.Copy).then_inc(r_ev.sem, 1)

        def logits_mm(e, n, par, i):
            p_ev.at(e, *((n, i - 1) if i >= 2 else (n - 1, TB + i - 1)))
            w = width(i)
            for c in range(0, w, 512):
                mm = e.matmul(logits(i)[:, c:min(w, c + 512)], qh[:, par, i * P:(i + 1) * P],
                              kh[:, par, c:min(w, c + 512)], start=True, stop=True)
            mm.then_inc(s_mm.sem, 1)

        def row_max(e, n, par, i):
            s_mm.at(e, n, i + 1)
            f = far(i)
            if f:
                c_max.link(e.tensor_reduce(mx[:, 2 * i:2 * i + 1], logits(i)[:, 0:f], AX.X, ALU.max))
            if i == 0:
                r_in.at(e, n)
            p_ev.at(e, *((n, i - 1) if i >= 2 else (n - 1, TB + i - 1)))
            wb = width(i) - f
            step_in(e, cell[:])
            c_max.link(e.tensor_tensor_reduce(
                summed[:, i % 2, 0:wb], logits(i)[:, f:f + wb], band[:, par, i, BAND - wb:BAND],
                1.0, mx[:, 2 * i:2 * i + 1] if f else NEG, ALU.add, ALU.max, mx[:, 2 * i + 1:2 * i + 2]))
            e.tensor_scalar(nb[:, i:i + 1], mx[:, 2 * i + 1:2 * i + 2], -SC_A, None, ALU.mult)\
                .then_inc(nb_ev.sem, 1)

        def exps(e, n, i):
            nb_ev.at(e, n, i + 1)
            u, f, w = i // G, far(i), width(i)
            if i % G == 0:
                t_mm.at(e, n - 1, (4, NJ)[u])
            if f:
                e.activation(probs[u][:, i % G, 0:f], logits(i)[:, 0:f], ACT.Exp,
                             bias=nb[:, i:i + 1], scale=SC_A)
            e.activation(probs[u][:, i % G, f:w], summed[:, i % 2, 0:w - f], ACT.Exp,
                         bias=nb[:, i:i + 1], scale=SC_A).then_inc(p_ev.sem, 1)

        def index(u, j):
            return G * u * (u + 1) // 2 + j

        def copied(jj):
            return (tA, tD)[jj % 2], jj // 2 + 1

        def copied_before(e, n, jj):
            ev, k = copied(jj)
            ev.at(e, n - 1, NJ // 2) if k == 1 else ev.at(e, n, k - 1)

        def turn(e, n, u, j):
            jj = index(u, j)
            if j == 0:
                p_ev.at(e, n, G * (u + 1))
            copied_before(e, n, jj)
            i0 = max(j, G * u)
            for i in range(i0, G * (u + 1)):
                mm = e.transpose(ps[:, T_BANKS[jj % 2], i % G * P:(i % G + 1) * P],
                                 probs[u][:, i % G, j * P:(j + 1) * P], ident[:])
            mm.then_inc(t_mm.sem, 1)

        def turn_copy(e, n, u, j):
            jj = index(u, j)
            t_mm.at(e, n, jj + 1)
            pv_mm.at(e, *((n, jj - 1) if jj >= 2 else (n - 1, NJ + jj - 1)))
            c0 = max(0, j - G * u) * P
            src, dst = ps[:, T_BANKS[jj % 2], c0:G * P], pT[:, jj % 2, c0:G * P]
            ins = e.activation(dst, src, ACT.Copy) if jj % 2 == 0 else e.tensor_copy(dst, src)
            ins.then_inc(copied(jj)[0].sem, 1)

        def values_mm(e, n, par, u, j):
            jj = index(u, j)
            if jj == 0:
                vh_ev.at(e, n)
            if j == 0:
                on.at(e, n - 1 if u == 0 else n, JJ if u == 0 else u)
            ev, k = copied(jj)
            ev.at(e, n, k)
            c, c0 = j % G, max(0, j - G * u) * P
            e.matmul(ps[WIN * c:WIN * (c + 1), O_BANK, c0:G * P], vh[:, par, j, :],
                     pT[:, jj % 2, c0:G * P], start=(j < G), stop=(j >= G * u),
                     skip_group_check=True).then_inc(pv_mm.sem, 1)

        def part_copy(e, n, u):
            pv_mm.at(e, n, index(u, G * (u + 1)))
            g_mm.at(e, n - 1 if u == 0 else n, JJ if u == 0 else u)
            e.tensor_copy(part[:], ps[:, O_BANK, :]).then_inc(o_ev.sem, 1)

        def gather(e, n, u):
            o_ev.at(e, n, u + 1)
            for i in range(G):
                k = WIN * min(G, G * u + i + 1)
                mm = e.matmul(ps[:, O_BANK, i * (D_A + 1):(i + 1) * (D_A + 1)], part[0:k, i * P:(i + 1) * P],
                              sel[0:k, :], start=True, stop=True)
            mm.then_inc(g_mm.sem, 1)

        def normalize(e, n, u):
            g_mm.at(e, n, u + 1)
            c_on.start(e, n, u)
            o = ps[:, O_BANK, 0:G * (D_A + 1)].rearrange("p (i d) -> p i d", i=G)
            c_on.link(e.reciprocal(rc[:].unsqueeze(2), o[:, :, D_A:D_A + 1]))
            tile, col = n // H_A * TB + G * u, n % H_A * D_A
            e.tensor_tensor(O[:, ds(tile, G), ds(col, D_A)], o[:, :, 0:D_A], wide(rc[:], D_A), ALU.mult)\
                .then_inc(on.sem, 1)

        def values_in(e, r, par):
            pv_mm.at(e, r - 2)
            hd = r % HEADS_A
            e.tensor_copy(vh[:, par, :, 0:D_A], V[:, ds(hd // H_A * TB, TB), ds(hd % H_A * D_A, D_A)])\
                .then_inc(vh_ev.sem, 1)

        def head(eng, e, n, par, before, after=True):
            u1 = [(n - 1, 1 - par, 1, j) for j in range(G * JJ)] if before else []
            u0 = [(n, par, 0, j) for j in range(G)]
            if eng == "tensor":
                for i in range(G):
                    logits_mm(e, n, par, i)
                    for m, q, u, j in u1[2 * i:2 * i + 2]:
                        turn(e, m, u, j)
                        if j:
                            values_mm(e, m, q, u, j - 1)
                for i in range(G, TB):
                    logits_mm(e, n, par, i)
                    if i == G:
                        if before:
                            values_mm(e, n - 1, 1 - par, 1, TB - 1)
                    band_mm(e, n + 1, 1 - par, i - G)
                    if i == G + 1 and before:
                        gather(e, n - 1, 1)
                    turn(e, n, 0, i - G)
                    if i > G:
                        values_mm(e, n, par, 0, i - G - 1)
                values_mm(e, n, par, 0, G - 1)
                gather(e, n, 0)
            if eng == "vector":
                c_max.start(e, n)
                for i in range(TB):
                    row_max(e, n, par, i)
                    if i < G:
                        for m, q, u, j in u1[2 * i:2 * i + 2]:
                            if index(u, j) % 2:
                                turn_copy(e, m, u, j)
                    else:
                        if i == G and before:
                            part_copy(e, n - 1, 1)
                        if i == G + 1 and before:
                            normalize(e, n - 1, 1)
                        if index(0, i - G) % 2:
                            turn_copy(e, n, 0, i - G)
                part_copy(e, n, 0)
                normalize(e, n, 0)
            if eng == "scalar":
                for i in range(TB):
                    exps(e, n, i)
                    if i < G:
                        for m, q, u, j in u1[2 * i:2 * i + 2]:
                            if index(u, j) % 2 == 0:
                                turn_copy(e, m, u, j)
                    else:
                        band_copy(e, n + 1, i - G)
                        if index(0, i - G) % 2 == 0:
                            turn_copy(e, n, 0, i - G)
            if eng == "gpsimd":
                values_in(e, n + 1, 1 - par)
            if eng == "sync":
                load_head(e, n + 1, 1 - par)
                skew_head(e, n + 1, 1 - par)

        def heads(eng, e):
            if eng == "sync":
                load_head(e, 0, 0)
                skew_head(e, 0, 0)
            if eng == "gpsimd":
                values_in(e, 0, 0)
            for j in range(TB // 2):
                if eng == "tensor":
                    band_mm(e, 0, 0, j)
                if eng == "scalar":
                    band_copy(e, 0, j)
            head(eng, e, 0, 0, False)
            head(eng, e, 1, 1, True)
            with e.Fori(1, HEADS_A // 2) as pair:
                for par in range(2):
                    head(eng, e, pair * 2 + par, par, True)
            n = HEADS_A - 1
            for j in range(G * JJ):
                if eng == "tensor":
                    turn(e, n, 1, j)
                    if j:
                        values_mm(e, n, 1, 1, j - 1)
                if eng == ("scalar", "vector")[index(1, j) % 2]:
                    turn_copy(e, n, 1, j)
            if eng == "tensor":
                values_mm(e, n, 1, 1, G * JJ - 1)
                gather(e, n, 1)
            if eng == "vector":
                part_copy(e, n, 1)
                normalize(e, n, 1)

        @block.sync
        def _(e):
            e.dma_start(relT[:], a["relT"]).then_inc(s_in, 16)
            e.dma_start(sel[:], a["c_sel"]).then_inc(s_in, 16)
            r_out.open(e)
            r_in.open(e)
            heads("sync", e)
            r_in.at(e, HEADS_A)

        @block.gpsimd
        def _(e):
            e.memset(vh[:], 0.0).then_inc(s_set, 1)
            e.wait_ge(s_set, 1)
            e.memset(vh[:, :, :, D_A:D_A + 1], 1.0).then_inc(s_set, 1)
            e.wait_ge(s_set, 2)
            heads("gpsimd", e)

        @block.vector
        def _(e):
            for ev in (nb_ev, tD, on):
                ev.open(e)
            e.wait_ge(s_in, 32)
            e.tensor_scalar(relD[:], relT[:], relT[:, 0:1], None, ALU.subtract).then_inc(s_rel, 1)
            e.memset(ps[:, O_BANK, :], 0.0).then_inc(s_rel, 1)
            heads("vector", e)

        @block.scalar
        def _(e):
            for ev in (r_ev, p_ev, tA):
                ev.open(e)
            heads("scalar", e)

        @block.tensor
        def _(e):
            for ev in (s_mm, t_mm, pv_mm, g_mm):
                ev.open(e)
            e.wait_ge(s_rel, 2)
            heads("tensor", e)


def first_output(nc, a, X, X2, ident):
    STEPS = NT // G
    with Part(nc, "ou") as t:
        Wo, bo = t.sb("Wo", [P, E]), t.sb("bo", [P, E])
        oc, oT = t.sb("oc", [P, G, E]), t.sb("oT", [P, G * P])
        y, yn = t.sb("y", [P, G, E]), t.sb("yn", [P, G, E])
        ps = t.psum()
        s_in = t.sem("in")
        oc_ev, t_mm, oT_ev = t.ev("oc"), t.ev("tm", 1, 1), t.ev("oT", 1, 1)
        o_mm, y_ev = t.ev("om", 1, 1), t.ev("ye", 1, 1)
        ln = LayerNorm(t, "ln", G, 2)
        ch = t.chain("ch", 2)
        block = t.block()

        @block.sync
        def _(e):
            e.dma_start(Wo[:], a["L0_attn_Wo"]).then_inc(s_in, 16)
            e.dma_start(bo[:], a["L0_attn_bo"].partition_broadcast(P)).then_inc(s_in, 16)

        @block.gpsimd
        def _(e):
            ln.open(e)
            with e.Fori(0, STEPS) as i:
                t_mm.at(e, i - 1)
                e.tensor_copy(oc[:], X2[:, ds(i * G, G), :]).then_inc(oc_ev.sem, 1)
                ln.rstd(e, G, i, 1)
                ln.rstd(e, G, i, 2)

        @block.tensor
        def _(e):
            t_mm.open(e)
            o_mm.open(e)
            e.wait_ge(s_in, 32)
            with e.Fori(0, STEPS) as i:
                oc_ev.at(e, i)
                oT_ev.at(e, i - 1)
                for g in range(G):
                    mm = e.transpose(ps[:, 0, g * P:(g + 1) * P], oc[:, g, :], ident[:])
                mm.then_inc(t_mm.sem, 1)
                oT_ev.at(e, i)
                y_ev.at(e, i - 1)
                for g in range(G):
                    mm = e.matmul(ps[:, 1, g * P:(g + 1) * P], oT[:, g * P:(g + 1) * P], Wo[:],
                                  start=True, stop=True)
                mm.then_inc(o_mm.sem, 1)

        @block.scalar
        def _(e):
            oT_ev.open(e)
            with e.Fori(0, STEPS) as i:
                t_mm.at(e, i)
                o_mm.at(e, i - 1)
                e.activation(oT[:], ps[:, 0, :], ACT.Copy).then_inc(oT_ev.sem, 1)

        @block.vector
        def _(e):
            y_ev.open(e)
            e.wait_ge(s_in, 32)
            with e.Fori(0, STEPS) as i:
                first = i * G + i // (TB // G) + 1
                ch.start(e, i)
                ln.chain.start(e, i)
                ys = [y[:, g, :] for g in range(G)]
                o_mm.at(e, i)
                ins = e.tensor_tensor(y[:], ps[:, 1, :].rearrange("p (g d) -> p g d", g=G), over(bo[:], G),
                                      ALU.add)
                ins.then_inc(y_ev.sem, 1)
                y_ev.at(e, i)
                ln.stats(e, ys)
                ch.link(ln.apply(e, ys, [yn[:, g, :] for g in range(G)], i, 1))
                x2 = X2[:, ds(i * G, G), :]
                ch.link(e.tensor_tensor(x2, X[:, ds(first, G), :], yn[:], ALU.add))
                xs = [X2[:, ds(i * G + g, 1), :] for g in range(G)]
                ln.stats(e, xs)
                ln.apply(e, xs, [X[:, ds(first + g, 1), :] for g in range(G)], i, 2)


def layers(nc, a, X, ident):
    with Part(nc, "la") as t:
        Y = t.sb("Y", [P, SLOTS, E])
        Wqkv = t.sb("Wqkv", [P, 2, 3 * INNER])
        Wo, W1 = t.sb("Wo", [P, H * D // P, E]), t.sb("W1", [P, 2 * HID])
        W2 = t.sb("W2", [P, len(PIECES), E])
        rot, scales = t.sb("rot", [P, TB, 4 * D]), t.sb("scales", [P, DEPTH, 4 * D])
        lng, lnb, b1 = t.sb("lng", [P, DEPTH]), t.sb("lnb", [P, DEPTH]), t.sb("b1", [P, 2 * len(PIECES), DEPTH])
        b2 = t.sb("b2", [P, DEPTH, E])
        shift, last = t.sb("shift", [P, P]), t.sb("last", [P, P])
        mask, identb, mask32 = t.sb("mask", [P, TB, KW], BF16), t.sb("identb", [P, P], BF16), t.sb("mask32", [P, 2, KW])
        begins = t.sb("begins", [P, TB])
        xs, xsT = t.sb("xs", [P, E]), t.sb("xsT", [P, P])
        raw, rt, sw = t.sb("raw", [P, 2 * INNER]), t.sb("rt", [P, 2 * INNER]), t.sb("sw", [P, INNER])
        sq = t.sb("sq", [P, 2, 512])
        ssum, rn, rq = t.sb("ssum", [P, 2 * H]), t.sb("rn", [P, 2 * H]), t.sb("rq", [P, 2, H])
        tab = t.sb("tab", [P, 4, D])
        v, vp = t.sb("v", [P, 2, INNER]), t.sb("vp", [WIN, 3, INNER])
        qT, kT = t.sb("qT", [P, H // 2, 2, P]), t.sb("kT", [P, H // 2, KW])
        rmax, nb, rs, rc = t.sb("rmax", [P, H]), t.sb("nb", [P, H]), t.sb("rs", [P, H]), t.sb("rc", [P, H])
        pr, pT, pTp = t.sb("pr", [P, H, KW]), t.sb("pT", [P, H, P]), t.sb("pTp", [WIN, H, P])
        o = t.sb("o", [P, INNER])
        oT, ys, yn, ynT = t.sb("oT", [P, 8, P]), t.sb("ys", [P, E]), t.sb("yn", [P, E]), t.sb("ynT", [P, P])
        gl, gT, yb = t.sb("gl", [P, 3, P]), t.sb("gT", [P, 3, P]), t.sb("yb", [P, E])
        ps = t.psum()

        s_in, s_set, s_mask = t.sem("in"), t.sem("set"), t.sem("mask")
        w_qkv, w_o, w_1, w_2 = t.ev("wq", 16), t.ev("wo", 16), t.ev("w1", 16), t.ev("w2", 32)
        x_ev = t.ev("xe", 1, NT)
        sh_mm, sh_ev, xl_ev, xT_mm, xT_ev = t.ev("shm"), t.ev("she", 1, 1), t.ev("xle", 1, 1), t.ev("xtm", 1, 1), t.ev("xte", 1, 1)
        q_mm, q_ev, q_sq, q_ss = t.ev("qm", 6, 1), t.ev("qe", 6, 1), t.ev("qsq", 4, 1), t.ev("qss", 4, 1)
        rn_ev, rq_ev = t.ev("rn", 1, 1), t.ev("rq", 1, 1)
        tab_ev, cl_ev = t.ev("tab"), t.ev("cl")
        power = t.sb("power", [P, 2 * H])
        rc_ev, rsw_ev, rt_ev, kn_ev = t.ev("rce", 2, 1), t.ev("rsw", 2, 1), t.ev("rte", 2, 1), t.ev("kn", 1, 1)
        kc_ev, T_mm, T_ev = t.ev("kc"), t.ev("Tm", 4, 1), t.ev("Te", 4, 1)
        S_mm, m_ev, e_ev = t.ev("Sm", 8, 1), t.ev("me", 8, 1), t.ev("ee", 8, 1)
        pt_mm, pt_ev, pp_ev = t.ev("ptm", 4, 1), t.ev("pte", 4, 1), t.ev("ppe", 4, 1)
        pv_mm, o_ev = t.ev("pv", 2, 2), t.ev("oe", 2, 1)
        c_nb, c_rc = t.chain("cnb", 8), t.chain("crc", 2)
        oT_mm, oT_ev, wo_mm, y_ev = t.ev("otm", 2, 1), t.ev("ote", 2, 1), t.ev("wom", 1, 1), t.ev("ye", 1, 1)
        s2_mm, s2_ev, yl_ev = t.ev("s2m", 1, 1), t.ev("s2e", 1, 1), t.ev("yle", 1, 1)
        yn_ev, nT_mm, nT_ev = t.ev("yn", 1, 1), t.ev("ntm", 1, 1), t.ev("nte", 1, 1)
        g_mm, g_ev, a_mm, a_ev, f_mm = t.ev("gm", 1, 1), t.ev("ge", 1, 1), t.ev("am", 1, 1), t.ev("ae", 1, 1), t.ev("fm", 1, 1)
        yb_ev = t.ev("yb", 1, 1)
        ln = LayerNorm(t, "ln", 1)
        block = t.block()
        BANK_T, BANK_O, BANK_3 = 4, 5, 7

        def layer(n):
            return n // NT

        def shift_in(eng, e, n):
            cur = slot(n % NT)
            if eng == "tensor":
                x_ev.at(e, n - NT)
                q_ev.at(e, n - 1, 5)
                e.matmul(ps[:, 0, 0:E // 2], shift[:], X[:, ds(cur, 1), E // 2:E], start=True, stop=False)
                e.matmul(ps[:, 0, 0:E // 2], last[:], X[:, ds(cur - 1, 1), E // 2:E], start=False, stop=True)\
                    .then_inc(sh_mm.sem, 1)
            if eng == "scalar":
                sh_mm.at(e, n)
                xT_mm.at(e, n - 1)
                e.activation(xs[:, E // 2:E], ps[:, 0, 0:E // 2], ACT.Copy).then_inc(sh_ev.sem, 1)
            if eng == "gpsimd":
                x_ev.at(e, n - NT)
                xT_mm.at(e, n - 1)
                e.tensor_copy(xs[:, 0:E // 2], X[:, ds(cur, 1), 0:E // 2]).then_inc(xl_ev.sem, 1)

        def turn_in(eng, e, n):
            if eng == "tensor":
                sh_ev.at(e, n)
                xl_ev.at(e, n)
                q_ev.at(e, n - 1, 6)
                e.transpose(ps[:, 1, 0:P], xs[:], ident[:]).then_inc(xT_mm.sem, 1)
            if eng == "scalar":
                xT_mm.at(e, n)
                q_mm.at(e, n - 1)
                e.activation(xsT[:], ps[:, 1, 0:P], ACT.Copy).then_inc(xT_ev.sem, 1)

        def qkv(c):
            def job(eng, e, n):
                bank = c % 2
                if eng == "tensor":
                    if c == 0:
                        xT_ev.at(e, n)
                        w_qkv.at(e, layer(n))
                        sh_ev.at(e, n)
                    if c >= 2:
                        q_ev.at(e, n, c - 1)
                        if c < 6:
                            q_sq.at(e, n, c - 1)
                    e.matmul(ps[:, bank, :], xsT[:], Wqkv[:, ds(layer(n) % 2, 1), c * 512:(c + 1) * 512],
                             start=True, stop=True).then_inc(q_mm.sem, 1)
                if eng == "scalar":
                    q_mm.at(e, n, c + 1)
                    if c < 4:
                        if c % 2 == 0:
                            rsw_ev.at(e, n - 1, c // 2 + 1)
                            rc_ev.at(e, n - 1, c // 2 + 1)
                        e.activation(raw[:, c * 512:(c + 1) * 512], ps[:, bank, :], ACT.Copy)\
                            .then_inc(q_ev.sem, 1)
                        q_ss.at(e, *((n, c - 1) if c >= 2 else (n - 1, c + 3)))
                        e.activation(sq[:, c % 2, :], ps[:, bank, :], ACT.Square).then_inc(q_sq.sem, 1)
                    else:
                        pv_mm.at(e, n - 2)
                        h = slice((c - 4) * 512, (c - 3) * 512)
                        e.activation(v[:, ds(n % 2, 1), h], ps[:, bank, :], ACT.Copy)
                        e.activation(vp[:, ds(n % 3, 1), h], ps[P - WIN:P, bank, :], ACT.Copy)\
                            .then_inc(q_ev.sem, 1)
                if eng == "vector" and c < 4:
                    q_sq.at(e, n, c + 1)
                    if c == 0:
                        rn_ev.at(e, n - 1)
                    e.tensor_reduce(ssum[:, c * 8:(c + 1) * 8],
                                    sq[:, c % 2, :].rearrange("p (h d) -> p h d", d=D), AX.X, ALU.add)\
                        .then_inc(q_ss.sem, 1)
            return job

        def norms(eng, e, n):
            if eng == "vector":
                q_ss.at(e, n)
                e.tensor_scalar(ssum[:], ssum[:], 1e-24, None, ALU.max).then_inc(cl_ev.sem, 1)
            if eng == "gpsimd":
                cl_ev.at(e, n)
                rq_ev.at(e, n - 1)
                e.tensor_tensor(rn[:], ssum[:], power[:], ALU.pow).then_inc(rn_ev.sem, 1)
            if eng == "vector":
                rn_ev.at(e, n)
                e_ev.at(e, n - 2)
                e.tensor_scalar(rq[:, ds(n % 2, 1), :], rn[:, 0:H], QK_SCALE, None, ALU.mult)\
                    .then_inc(rq_ev.sem, 1)

        def tables(eng, e, n):
            if eng == "gpsimd":
                rsw_ev.at(e, n - 1)
                rc_ev.at(e, n - 1)
                e.tensor_tensor(tab[:].rearrange("p f d -> p (f d)"), rot[:, ds(n % TB, 1), :],
                                scales[:, ds(layer(n), 1), :], ALU.mult).then_inc(tab_ev.sem, 1)

        def rotate(w):
            def job(eng, e, n):
                src = raw[:, w * INNER:(w + 1) * INNER]
                dst = rt[:, w * INNER:(w + 1) * INNER]
                if eng == ("gpsimd", "vector")[w]:
                    q_ev.at(e, n, 2 * w + 2)
                    tab_ev.at(e, n)
                    T_mm.at(e, n - 1, 4)
                    e.tensor_tensor(dst.rearrange("p (h d) -> p h d", d=D),
                                    src.rearrange("p (h d) -> p h d", d=D),
                                    over(tab[:, 2 * w, :], H), ALU.mult).then_inc(rc_ev.sem, 1)
                if eng == "vector":
                    q_ev.at(e, n, 2 * w + 2)
                    tab_ev.at(e, n)
                    rt_ev.at(e, *((n, 1) if w else (n - 1, 2)))
                    s3 = src.rearrange("p (h t d) -> p h t d", h=H, t=2)
                    d3 = sw[:].rearrange("p (h t d) -> p h t d", h=H, t=2)
                    for half in range(2):
                        ins = e.tensor_tensor(d3[:, :, half, :], s3[:, :, 1 - half, :],
                                              over(tab[:, 2 * w + 1, half * 32:(half + 1) * 32], H), ALU.mult)
                    ins.then_inc(rsw_ev.sem, 1)
                if eng == "gpsimd":
                    rsw_ev.at(e, n, w + 1)
                    rc_ev.at(e, n, w + 1)
                    e.tensor_tensor(dst, dst, sw[:], ALU.add).then_inc(rt_ev.sem, 1)
                    if w:
                        rt_ev.at(e, n, 2)
                        rn_ev.at(e, n)
                        d = dst.rearrange("p (h d) -> p h d", d=D)
                        e.tensor_tensor(d, d, wide(rn[:, H:2 * H], D), ALU.mult).then_inc(kn_ev.sem, 1)
            return job

        def carry(eng, e, n):
            if eng == "gpsimd":
                S_mm.at(e, n - 1)
                flag = begins[:, ds(n % TB, 1)].unsqueeze(2).to_broadcast([P, H // 2, WIN])
                e.tensor_tensor(kT[:, :, 0:WIN], kT[:, :, P:KW], flag, ALU.mult)\
                    .then_inc(kc_ev.sem, 1)

        def turn_qk(u):
            w, half = u % 2, u // 2
            def job(eng, e, n):
                if eng == "tensor":
                    kn_ev.at(e, n) if w else rt_ev.at(e, n, 1)
                    if u == 0:
                        pt_ev.at(e, n - 1)
                    else:
                        T_ev.at(e, n, u)
                    for j in range(4):
                        c = w * INNER + (4 * half + j) * P
                        mm = e.transpose(ps[:, BANK_T, j * P:(j + 1) * P], rt[:, c:c + P], ident[:])
                    mm.then_inc(T_mm.sem, 1)
                if eng == "scalar":
                    T_mm.at(e, n, u + 1)
                    pairs = slice(4 * half, 4 * half + 4)
                    src = ps[:, BANK_T, :].rearrange("p (j t) -> p j t", j=4)
                    if w:
                        kc_ev.at(e, n)
                        e.activation(kT[:, pairs, WIN:KW], src, ACT.Copy).then_inc(T_ev.sem, 1)
                    else:
                        S_mm.at(e, n - 1)
                        e.activation(qT[0:D, pairs, 0, :], src[0:D], ACT.Copy)
                        e.activation(qT[D:P, pairs, 1, :], src[D:P], ACT.Copy).then_inc(T_ev.sem, 1)
            return job

        def scores(p):
            bank = 2 + p % 2
            def job(eng, e, n):
                both = ps[:, bank, 0:2 * KW].rearrange("p (h k) -> p h k", h=2)
                if eng == "tensor":
                    e_ev.at(e, *((n, p - 1) if p >= 2 else (n - 1, p + 7)))
                    T_ev.at(e, n, 2 + 2 * (p // 4))
                    e.matmul(both, identb[:], mask[:, ds(n % TB, 1), :].to_broadcast([P, 2, KW]),
                             start=True, stop=True)
                    for h in range(2):
                        mm = e.matmul(both[:, h, :], qT[:, p, h, :], kT[:, p, :], start=False, stop=True,
                                      skip_group_check=True)
                    mm.then_inc(S_mm.sem, 1)
                if eng == "vector":
                    S_mm.at(e, n, p + 1)
                    if p == 0:
                        c_nb.start(e, n)
                        e_ev.at(e, n - 1)
                    hs = slice(2 * p, 2 * p + 2)
                    c_nb.link(e.tensor_reduce(rmax[:, hs], both, AX.X, ALU.max, negate=True))
                    rq_ev.at(e, n)
                    e.tensor_tensor(nb[:, hs], rmax[:, hs], rq[:, ds(n % 2, 1), hs], ALU.mult)\
                        .then_inc(m_ev.sem, 1)
                if eng == "scalar":
                    m_ev.at(e, n, p + 1)
                    if p == 0:
                        pt_mm.at(e, n - 1)
                        pp_ev.at(e, n - 1)
                        o_ev.at(e, n - 1)
                    for h in range(2):
                        hh = 2 * p + h
                        ins = e.activation(pr[:, hh, :], both[:, h, :], ACT.Exp, bias=nb[:, hh:hh + 1],
                                           scale=rq[:, ds(n % 2, 1), hh:hh + 1], accum_out=rs[:, hh:hh + 1])
                    ins.then_inc(e_ev.sem, 1)
            return job

        def turn_p(u):
            def job(eng, e, n):
                hs = slice(4 * u, 4 * u + 4)
                if eng == "tensor":
                    e_ev.at(e, n, 2 * u + 2)
                    T_ev.at(e, n) if u == 0 else pt_ev.at(e, n, u)
                    for j in range(4):
                        mm = e.transpose(ps[:, BANK_T, j * P:(j + 1) * P], pr[:, 4 * u + j, WIN:KW], ident[:])
                    mm.then_inc(pt_mm.sem, 1)
                if eng == "vector":
                    e_ev.at(e, n, 2 * u + 2)
                    if u == 0:
                        pv_mm.at(e, n - 1)
                    e.transpose(pTp[:, hs, 0:WIN], pr[0:WIN, hs, 0:WIN]).then_inc(pp_ev.sem, 1)
                    pt_mm.at(e, n, u + 1)
                    e.tensor_copy(pT[:, hs, :], ps[:, BANK_T, :].rearrange("p (j t) -> p j t", j=4))\
                        .then_inc(pt_ev.sem, 1)
            return job

        def values(u):
            def job(eng, e, n):
                bank = BANK_O + u
                if eng == "tensor":
                    pt_ev.at(e, n, 2 * u + 2)
                    pp_ev.at(e, n, 2 * u + 2)
                    q_ev.at(e, n)
                    o_ev.at(e, n - 1, u + 1)
                    for j in range(8):
                        h = 8 * u + j
                        e.matmul(ps[:, bank, j * D:(j + 1) * D], pT[:, h, :],
                                 v[:, ds(n % 2, 1), h * D:(h + 1) * D], start=(j == 0), stop=True,
                                 skip_group_check=True)
                    for j in range(8):
                        h = 8 * u + j
                        mm = e.matmul(ps[:, bank, j * D:(j + 1) * D], pTp[:, h, :],
                                      vp[:, ds((n + 2) % 3, 1), h * D:(h + 1) * D], start=False, stop=True,
                                      skip_group_check=True)
                    mm.then_inc(pv_mm.sem, 1)
                if eng == "vector":
                    e_ev.at(e, n, 4 * u + 4)
                    c_rc.start(e, n, u)
                    c_rc.link(e.reciprocal(rc[:, 8 * u:8 * u + 8], rs[:, 8 * u:8 * u + 8]))
                    if u == 0:
                        oT_mm.at(e, n - 1)
                    pv_mm.at(e, n, u + 1)
                    e.tensor_tensor(o[:, u * 512:(u + 1) * 512].rearrange("p (h d) -> p h d", d=D),
                                    ps[:, bank, :].rearrange("p (h d) -> p h d", d=D),
                                    wide(rc[:, 8 * u:8 * u + 8], D), ALU.mult).then_inc(o_ev.sem, 1)
            return job

        def turn_o(u):
            def job(eng, e, n):
                if eng == "tensor":
                    o_ev.at(e, n, u + 1)
                    oT_ev.at(e, n, 1) if u else x_ev.at(e, n - 1)
                    for j in range(4):
                        mm = e.transpose(ps[:, BANK_3, j * P:(j + 1) * P], o[:, (4 * u + j) * P:(4 * u + j + 1) * P],
                                         ident[:])
                    mm.then_inc(oT_mm.sem, 1)
                if eng == "scalar":
                    oT_mm.at(e, n, u + 1)
                    if u == 0:
                        wo_mm.at(e, n - 1)
                    e.activation(oT[:, 4 * u:4 * u + 4, :], ps[:, BANK_3, :].rearrange("p (j t) -> p j t", j=4),
                                 ACT.Copy).then_inc(oT_ev.sem, 1)
            return job

        def project(eng, e, n):
            cur = slot(n % NT)
            if eng == "tensor":
                oT_ev.at(e, n)
                w_o.at(e, layer(n))
                for j in range(8):
                    mm = e.matmul(ps[:, BANK_3, 0:E], oT[:, j, :], Wo[:, j, :], start=(j == 0), stop=(j == 7))
                mm.then_inc(wo_mm.sem, 1)
            if eng == "vector":
                wo_mm.at(e, n)
                e.tensor_tensor(Y[:, ds(cur, 1), :], ps[:, BANK_3, 0:E], X[:, ds(cur, 1), :], ALU.add)\
                    .then_inc(y_ev.sem, 1)

        def shift_y(eng, e, n):
            cur = slot(n % NT)
            if eng == "tensor":
                y_ev.at(e, n)
                e.matmul(ps[:, BANK_3, 0:E // 2], shift[:], Y[:, ds(cur, 1), E // 2:E], start=True, stop=False)
                e.matmul(ps[:, BANK_3, 0:E // 2], last[:], Y[:, ds(cur - 1, 1), E // 2:E], start=False, stop=True)\
                    .then_inc(s2_mm.sem, 1)
            if eng == "scalar":
                s2_mm.at(e, n)
                yn_ev.at(e, n - 1)
                e.activation(ys[:, E // 2:E], ps[:, BANK_3, 0:E // 2], ACT.Copy).then_inc(s2_ev.sem, 1)
            if eng == "gpsimd":
                y_ev.at(e, n)
                yn_ev.at(e, n - 1)
                e.tensor_copy(ys[:, 0:E // 2], Y[:, ds(cur, 1), 0:E // 2]).then_inc(yl_ev.sem, 1)
                x_ev.at(e, n - 1)
                e.tensor_tensor(yb[:], Y[:, ds(cur, 1), :], b2[:, ds(layer(n), 1), :], ALU.add)\
                    .then_inc(yb_ev.sem, 1)
                ln.rstd(e, 1, n)
            if eng == "vector":
                s2_ev.at(e, n)
                yl_ev.at(e, n)
                nT_mm.at(e, n - 1)
                ln.chain.start(e, n)
                ln.stats(e, [ys[:]])
                ln.apply(e, [ys[:]], [yn[:]], n).then_inc(yn_ev.sem, 1)

        def turn_y(eng, e, n):
            if eng == "tensor":
                yn_ev.at(e, n)
                e.transpose(ps[:, BANK_3, 0:P], yn[:], ident[:]).then_inc(nT_mm.sem, 1)
            if eng == "scalar":
                nT_mm.at(e, n)
                a_mm.at(e, n - 1)
                e.activation(ynT[:], ps[:, BANK_3, 0:P], ACT.Identity, bias=lnb[:, ds(layer(n), 1)],
                             scale=lng[:, ds(layer(n), 1)]).then_inc(nT_ev.sem, 1)

        def gate(eng, e, n):
            if eng == "tensor":
                nT_ev.at(e, n)
                w_1.at(e, layer(n))
                for j, (c, w) in enumerate(PIECES):
                    mm = e.matmul(ps[0:w, BANK_3, j * P:(j + 1) * P], W1[:, HID + c:HID + c + w], ynT[:],
                                  start=True, stop=True)
                mm.then_inc(g_mm.sem, 1)
            if eng == "scalar":
                g_mm.at(e, n)
                a_ev.at(e, n - 1)
                for j, (c, w) in enumerate(PIECES):
                    ins = e.activation(gl[0:w, j, :], ps[0:w, BANK_3, j * P:(j + 1) * P], ACT.Gelu,
                                       bias=b1[0:w, 3 + j, ds(layer(n), 1)])
                ins.then_inc(g_ev.sem, 1)

        def gated(eng, e, n):
            if eng == "tensor":
                g_ev.at(e, n)
                for j, (c, w) in enumerate(PIECES):
                    mm = e.matmul(ps[0:w, BANK_3, j * P:(j + 1) * P], W1[:, c:c + w], ynT[:],
                                  start=True, stop=True)
                mm.then_inc(a_mm.sem, 1)
            if eng == "vector":
                a_mm.at(e, n)
                g_ev.at(e, n)
                f_mm.at(e, n - 1)
                for j, (c, w) in enumerate(PIECES):
                    ins = e.scalar_tensor_tensor(gT[0:w, j, :], ps[0:w, BANK_3, j * P:(j + 1) * P],
                                                 b1[0:w, j, ds(layer(n), 1)], gl[0:w, j, :], ALU.add, ALU.mult)
                ins.then_inc(a_ev.sem, 1)

        def down(eng, e, n):
            if eng == "tensor":
                a_ev.at(e, n)
                w_2.at(e, layer(n))
                for j, (c, w) in enumerate(PIECES):
                    mm = e.matmul(ps[:, BANK_3, 0:E], gT[0:w, j, :], W2[0:w, j, :], start=(j == 0), stop=(j == 2))
                mm.then_inc(f_mm.sem, 1)
            if eng == "vector":
                f_mm.at(e, n)
                yb_ev.at(e, n)
                if not isinstance(n, int) or n < TILES - 1:
                    sh_mm.at(e, n + 1)
                e.tensor_tensor(X[:, ds(slot(n % NT), 1), :], ps[:, BANK_3, 0:E], yb[:], ALU.add)\
                    .then_inc(x_ev.sem, 1)

        ORDER = [
            (2, carry), (1, tables), (2, turn_qk(0)), (3, turn_o(0)), (1, shift_in), (2, turn_qk(1)),
            (3, turn_o(1)), (2, scores(0)), (1, turn_in), (3, project), (2, scores(1)), (2, turn_qk(2)),
            (1, qkv(0)), (2, turn_qk(3)), (3, shift_y), (2, scores(2)), (1, qkv(1)), (1, rotate(0)),
            (2, turn_p(0)), (2, scores(3)), (1, qkv(2)), (3, turn_y), (2, scores(4)), (2, turn_p(1)),
            (1, qkv(3)), (1, norms), (1, rotate(1)), (3, gate), (2, scores(5)), (1, qkv(4)), (2, values(0)),
            (3, gated), (2, scores(6)), (2, turn_p(2)), (1, qkv(5)), (2, scores(7)), (3, down), (2, turn_p(3)),
            (2, values(1)),
        ]

        def tile(eng, e, g, stages):
            for s, job in ORDER:
                if s in stages:
                    job(eng, e, g - (s - 1))

        def tiles(eng, e):
            tile(eng, e, 0, (1,))
            tile(eng, e, 1, (1, 2))
            with e.Fori(2, TILES) as g:
                tile(eng, e, g, (1, 2, 3))
            tile(eng, e, TILES, (2, 3))
            tile(eng, e, TILES + 1, (3,))

        N_IN = 11

        @block.sync
        def _(e):
            def small(l):
                e.dma_start(Wo[:], a["L0_ffn_Wo"][l].rearrange("(c p) d -> p c d", p=P)).then_inc(w_o.sem, 16)
            def qkv_in(l):
                e.dma_start(Wqkv[:, ds(l % 2, 1), :], a["L0_ffn_Wqkv"][ds(l, 1)].rearrange("l p n -> p l n"))\
                    .then_inc(w_qkv.sem, 16)
            def o_in(l):
                e.dma_start(Wo[:], a["L0_ffn_Wo"][ds(l, 1)].rearrange("l (c p) d -> p (l c) d", p=P))\
                    .then_inc(w_o.sem, 16)
            def w1_in(l):
                e.dma_start(W1[:], a["L0_ffn_W1"][ds(l, 1)].rearrange("l p n -> p (l n)")).then_inc(w_1.sem, 16)
            def w2_in(l):
                w2 = a["L0_ffn_W2"][ds(l, 1)]
                e.dma_start(W2[:, 0:2, :], w2[:, 0:2 * P, :].rearrange("l (c p) d -> p (l c) d", p=P))\
                    .then_inc(w_2.sem, 16)
                e.dma_start(W2[0:HID - 2 * P, 2, :], w2[:, 2 * P:HID, :].rearrange("l p d -> p (l d)"))\
                    .then_inc(w_2.sem, 16)
            qkv_in(0)
            e.dma_start(rot[:], a["c_rot"]).then_inc(s_in, 16)
            e.dma_start(scales[:], a["scales"].partition_broadcast(P)).then_inc(s_in, 16)
            e.dma_start(b2[:], a["L0_ffn_b2"].partition_broadcast(P)).then_inc(s_in, 16)
            for dst, src in ((lng, "lngT"), (lnb, "lnbT"), (b1, "b1T"), (shift, "c_shift"), (last, "c_last"),
                             (begins, "c_begins"), (mask32, "c_mask")):
                e.dma_start(dst[:], a[src]).then_inc(s_in, 16)
            e.dma_start(sq[:, 0, 0:P], a["c_ident"]).then_inc(s_in, 16)
            o_in(0)
            w1_in(0)
            w2_in(0)
            qkv_in(1)

            def refill(l):
                wo_mm.at(e, l * NT - 1)
                o_in(l)
                a_mm.at(e, l * NT - 1)
                w1_in(l)
                f_mm.at(e, l * NT - 1)
                w2_in(l)
            with e.Fori(1, DEPTH - 1) as l:
                refill(l)
                qkv_in(l + 1)
            refill(DEPTH - 1)

        @block.gpsimd
        def _(e):
            xl_ev.open(e)
            rt_ev.open(e)
            kn_ev.open(e)
            yl_ev.open(e)
            yb_ev.open(e)
            rn_ev.open(e)
            for b in range(B):
                e.memset(Y[:, b * ZERO_SLOT, :], 0.0)
            ln.open(e)
            e.memset(power[:], -0.5)
            e.memset(pTp[:].rearrange("p a b -> p (a b)"), 0.0)
            e.memset(qT[:].rearrange("p a b c -> p (a b c)"), 0.0)
            e.memset(kT[:].rearrange("p a b -> p (a b)"), 0.0)
            e.memset(vp[:].rearrange("p a b -> p (a b)"), 0.0).then_inc(s_set, 1)
            e.wait_ge(s_in, 16 * N_IN)
            e.wait_ge(s_set, 1)
            tiles("gpsimd", e)

        @block.vector
        def _(e):
            for ev in (x_ev, q_ss, rq_ev, rc_ev, rsw_ev, m_ev, pt_ev, pp_ev, o_ev, y_ev, yn_ev, a_ev):
                ev.open(e)
            e.wait_ge(s_in, 16 * N_IN)
            e.tensor_copy(mask[:, 0, :], mask32[:, 0, :])
            for i in range(1, TB):
                e.tensor_copy(mask[:, i, :], mask32[:, 1, :])
            e.tensor_copy(identb[:], sq[:, 0, 0:P]).then_inc(s_mask, 1)
            e.wait_ge(s_mask, 1)
            e.wait_ge(s_set, 1)
            tiles("vector", e)

        @block.scalar
        def _(e):
            for ev in (sh_ev, xT_ev, q_ev, q_sq, T_ev, e_ev, oT_ev, s2_ev, nT_ev, g_ev):
                ev.open(e)
            e.wait_ge(s_in, 16 * N_IN)
            e.wait_ge(s_set, 1)
            e.wait_ge(s_mask, 1)
            tiles("scalar", e)

        @block.tensor
        def _(e):
            for ev in (xT_mm, q_mm, T_mm, S_mm, pt_mm, pv_mm, oT_mm, wo_mm, s2_mm, nT_mm, g_mm, a_mm, f_mm):
                ev.open(e)
            e.wait_ge(s_in, 16 * N_IN)
            e.wait_ge(s_set, 1)
            e.wait_ge(s_mask, 1)
            tiles("tensor", e)


def last_output(nc, X, X2, out):
    STEPS = NT // G
    with Part(nc, "fi") as t:
        yn, res = t.sb("yn", [P, G, E]), t.sb("res", [P, 2, G, E])
        yn_ev, res_ev = t.ev("yn"), t.ev("re", 1, 1)
        sent = [t.ev(f"sent{u}", 16, 1) for u in range(2)]
        ln = LayerNorm(t, "ln", G)
        block = t.block()
        rows = out.rearrange("b (t p) d -> p (b t) d", p=P)

        @block.vector
        def _(e):
            res_ev.open(e)
            with e.Fori(0, STEPS // 2) as pair:
                for u in range(2):
                    i = pair * 2 + u
                    first = i * G + i // (TB // G) + 1
                    ln.chain.start(e, i)
                    xs = [X[:, ds(first + g, 1), :] for g in range(G)]
                    ln.stats(e, xs)
                    ln.apply(e, xs, [yn[:, g, :] for g in range(G)], i).then_inc(yn_ev.sem, 1)
                    yn_ev.at(e, i)
                    sent[u].at(e, pair - 1)
                    e.tensor_tensor(res[:, u, :, :], X2[:, ds(i * G, G), :], yn[:], ALU.add)\
                        .then_inc(res_ev.sem, 1)

        @block.gpsimd
        def _(e):
            ln.open(e)
            with e.Fori(0, STEPS) as i:
                ln.rstd(e, G, i)

        @block.sync
        def _(e):
            for u in range(2):
                sent[u].open(e)
            with e.Fori(0, STEPS // 2) as pair:
                for u in range(2):
                    i = pair * 2 + u
                    res_ev.at(e, i)
                    e.dma_start(rows[:, ds(i * G, G), :], res[:, u, :, :]).then_inc(sent[u].sem, 16)
            for u in range(2):
                sent[u].at(e, STEPS // 2 - 1)


def constants():
    r = np.arange(P)
    half = np.arange(0, D, 2, dtype=np.float32)
    inv_freq = (1.0 / np.float32(10000.0) ** (half / np.float32(D))).astype(np.float32)
    pos = np.arange(S, dtype=np.float32)
    freqs = pos[:, None] * inv_freq[None, :]
    base = (half + np.float32(0.4 * D)) / np.float32(1.4 * D)
    scale = base[None, :] ** ((pos - S // 2) / np.float32(WIN // 2))[:, None]
    cos, sin = np.cos(freqs), np.sin(freqs)
    tabs = []
    for s in (scale, 1.0 / scale):
        tabs += [np.concatenate([cos * s, cos * s], 1), np.concatenate([-sin * s, sin * s], 1)]
    rot = np.stack(tabs, 1).astype(np.float32)
    q, k = WIN + r[:, None], np.arange(KW)[None, :]
    seen = (k <= q) & (q - k <= WIN) & (k // WIN >= q // WIN - 1)
    masks = np.where(np.stack([seen & (k >= WIN), seen], 1), 0.0, NEG).astype(np.float32)
    begins = np.ones((P, TB), np.float32)
    begins[:, 0] = 0.0
    sel = np.zeros((P, D_A + 1), np.float32)
    for c in range(G):
        sel[WIN * c + np.arange(D_A + 1), np.arange(D_A + 1)] = 1.0
    return {
        "c_ident": np.eye(P, dtype=np.float32),
        "c_shift": np.eye(P, k=1, dtype=np.float32),
        "c_last": ((r[:, None] == P - 1) & (r[None, :] == 0)).astype(np.float32),
        "c_rot": np.ascontiguousarray(rot.reshape(TB, P, 4 * D).transpose(1, 0, 2)),
        "c_mask": np.ascontiguousarray(masks), "c_begins": begins, "c_sel": sel,
    }


_INS = ["L0_attn_x", "L0_attn_Wq", "L0_attn_bq", "L0_attn_Wk", "L0_attn_bk", "L0_attn_Wv", "L0_attn_bv",
        "L0_attn_Wo", "L0_attn_bo", "L0_ffn_Wqkv", "L0_ffn_Wo", "L0_ffn_W1", "L0_ffn_W2", "L0_ffn_b2"]


def layout(x):
    arrays = {n: np.ascontiguousarray(x[n]) for n in _INS}
    rel = np.asarray(x["L0_attn_rel_key"])
    arrays["relT"] = np.ascontiguousarray(rel.T)
    arrays["rel0"] = np.ascontiguousarray(np.tile(rel[0], H_A))
    qs, ks = np.asarray(x["L0_ffn_q_scale"]), np.asarray(x["L0_ffn_k_scale"])
    swap = lambda s: np.concatenate([s[:, D // 2:], s[:, :D // 2]], 1)
    arrays["scales"] = np.ascontiguousarray(np.concatenate([qs, swap(qs), ks, swap(ks)], 1))
    arrays["lngT"] = np.ascontiguousarray(np.asarray(x["L0_ffn_ln_g"]).T)
    arrays["lnbT"] = np.ascontiguousarray(np.asarray(x["L0_ffn_ln_b"]).T)
    b1 = np.asarray(x["L0_ffn_b1"])
    b1t = np.zeros((P, 2 * len(PIECES), DEPTH), b1.dtype)
    for half in range(2):
        for j, (c, w) in enumerate(PIECES):
            b1t[0:w, half * len(PIECES) + j, :] = b1[:, half * HID + c:half * HID + c + w].T
    arrays["b1T"] = b1t
    arrays.update(constants())
    return arrays


def kernel(**inputs):
    import concourse.bacc as bacc
    from concourse.bass_utils import run_bass_kernel_spmd

    nc = bacc.Bacc("TRN2", target_bir_lowering=False, num_devices=1)
    arrays = layout(inputs)
    aps = {n: nc.dram_tensor(f"in_{n}", v.shape, mybir.dt.from_np(v.dtype), kind="ExternalInput").ap()
           for n, v in arrays.items()}
    out = nc.dram_tensor("out", (B, S, E), F32, kind="ExternalOutput").ap()
    build(nc, aps, out)
    r = run_bass_kernel_spmd(nc, [{f"in_{n}": v for n, v in arrays.items()}], core_ids=[0])
    return r.results[0]["out"]
```

```python
from contextlib import ExitStack

import concourse.bass as bass
import numpy as np
from concourse import mybir

F32 = mybir.dt.float32
BF16 = mybir.dt.bfloat16
ALU = mybir.AluOpType
ACT = mybir.ActivationFunctionType
AX = mybir.AxisListType
ds = bass.ds

P = 128
B, S, E = 4, 1024, 128
NT = B * S // P
TB = S // P
SLOTS = B * (TB + 1)
G = 4
H_A, D_A, REL = 16, 8, 256
BAND = 3 * P
HEADS_A = B * H_A
SC_A = D_A ** -0.5
H, D = 16, 64
INNER = H * D
DEPTH, WIN = 6, 32
HID = 341
PIECES = [(c, min(P, HID - c)) for c in range(0, HID, P)]
KW = WIN + P
QK_SCALE = 8.0
NEG = -1e30
EPS = 1e-5
TILES = DEPTH * NT
ZERO_SLOT = TB + 1
RING = 3

ORDER = {
    "tensor": [("turn_p1", 2), ("shift_in", 0), ("scores6", 2), ("values0", 2), ("turn_in", 0),
              ("scores7", 2), ("turn_qk1", 1), ("qkv0", 0), ("qkv1", 0), ("scores0", 1),
              ("turn_p2", 2), ("scores1", 1), ("turn_qk2", 1), ("qkv2", 0), ("turn_y", 3),
              ("qkv3", 0), ("turn_p3", 2), ("turn_qk3", 1), ("scores2", 1), ("qkv4", 0),
              ("values1", 2), ("gate", 3), ("scores3", 1), ("scores4", 1), ("project", 2),
              ("turn_p0", 1), ("gated", 3), ("turn_qk0", 0), ("qkv5", 0), ("shift_y", 2),
              ("down", 3), ("scores5", 1)],
    "vector": [("scores5", 2), ("turn_p1", 2), ("scores6", 2), ("statistics", 3), ("scores7", 2),
              ("over_sum2", 2), ("scale_q", 1), ("over_sum3", 2), ("normalize", 3), ("turn_p2", 2),
              ("qkv0", 0), ("scores0", 1), ("qkv1", 0), ("swap0", 0), ("scores1", 1), ("turn_p3", 2),
              ("scores2", 1), ("qkv2", 0), ("qkv3", 0), ("norms", 0), ("swap1", 0), ("over_sum0", 1),
              ("scores3", 1), ("straight1", 0), ("project", 2), ("turn_p0", 1), ("gated", 3),
              ("scores4", 1), ("over_sum1", 1), ("down", 3)],
    "scalar": [("qkv5", 1), ("turn_qk0", 1), ("scores5", 2), ("shift_in", 0), ("shift_y", 3),
              ("turn_in", 0), ("scores6", 2), ("turn_qk1", 1), ("scores7", 2), ("values0", 2),
              ("qkv0", 0), ("qkv1", 0), ("turn_qk2", 1), ("scores0", 1), ("qkv2", 0), ("turn_y", 3),
              ("turn_qk3", 1), ("qkv3", 0), ("scores1", 1), ("scores2", 1), ("values1", 2),
              ("gate", 3), ("scores3", 1), ("qkv4", 0), ("scores4", 1)],
    "gpsimd": [("shift_in", 0), ("norms", 1), ("rotated1", 1), ("shift_y", 3), ("residual", 3),
              ("tables", 0), ("carry", 1), ("statistics", 3), ("straight0", 0), ("rotated0", 0)],
}


def slot(m):
    return m + m // TB + 1


class Event:

    def __init__(self, sem, per=1, credit=0):
        self.sem, self.per, self.credit = sem, per, credit

    def open(self, eng):
        eng.sem_inc(self.sem, self.per * self.credit)

    def at(self, eng, n, k=None):
        v = self.per * (n + self.credit) + (self.per if k is None else k)
        if isinstance(v, int) and v <= self.per * self.credit:
            return
        eng.wait_ge(self.sem, v)


class Chain(Event):

    def start(self, eng, n, k=0):
        self.eng, self.n, self.k = eng, n, k

    def link(self, ins):
        self.k += 1
        assert self.k <= self.per
        ins.then_inc(self.sem, 1)
        self.at(self.eng, self.n, self.k)


def step_in(dve, cell):
    dve.memset(cell, 0.0)


class LayerNorm:

    def __init__(self, part, name, n, per=1):
        self.st = part.sb(name + "_stats", [P, n, 9])
        self.power = part.sb(name + "_power", [P, n, 1])
        self.power_ev = part.ev(name + "_power_ev")
        self.cell = part.sb(name + "_cell", [P, 1])
        self.chain = part.chain(name + "_chain", 2 * per)
        self.stats_ev, self.rstd_ev = part.ev(name + "_stats_ev", per), part.ev(name + "_rstd_ev", per)

    def open(self, pool):
        pool.memset(self.power[:], -0.5).then_inc(self.power_ev.sem, 1)
        self.power_ev.at(pool, 0)

    def stats(self, dve, xs):
        step_in(dve, self.cell[:])
        for j, x in enumerate(xs):
            ins = dve.bn_stats(self.st[:, j, 0:6], x)
        self.chain.link(ins)
        step_in(dve, self.cell[:])
        for j in range(len(xs)):
            ins = dve.bn_aggr(self.st[:, j, 6:8], self.st[:, j, 0:6])
        self.chain.link(ins)
        n = len(xs)
        dve.tensor_scalar(self.st[:, 0:n, 7:8], self.st[:, 0:n, 7:8], EPS, None, ALU.add)\
            .then_inc(self.stats_ev.sem, 1)

    def rstd(self, pool, n, step, k=None):
        self.stats_ev.at(pool, step, k)
        pool.tensor_tensor(self.st[:, 0:n, 8:9], self.st[:, 0:n, 7:8], self.power[:, 0:n, :], ALU.pow)\
            .then_inc(self.rstd_ev.sem, 1)

    def apply(self, dve, xs, outs, step, k=None):
        self.rstd_ev.at(dve, step, k)
        for j, x in enumerate(xs):
            ins = dve.tensor_scalar(outs[j], x, self.st[:, j, 6:7], self.st[:, j, 8:9],
                                    ALU.subtract, ALU.mult)
        return ins


def wide(ap, n):
    return ap.unsqueeze(2).to_broadcast([ap.shape[0], ap.shape[1], n])


def over(ap, n):
    return ap.unsqueeze(1).to_broadcast([ap.shape[0], n, ap.shape[1]])


class Part:

    def __init__(self, nc, name):
        self.nc, self.name, self.ctx = nc, name, ExitStack()

    def __enter__(self):
        self.ctx.__enter__()
        return self

    def __exit__(self, *a):
        return self.ctx.__exit__(*a)

    def sb(self, name, shape, dt=F32):
        return self.ctx.enter_context(self.nc.sbuf_tensor(f"{self.name}_{name}", shape, dt))

    def psum(self):
        return self.ctx.enter_context(self.nc.psum_tensor(f"{self.name}_ps", [P, 8, 512], F32))

    def sem(self, name):
        return self.ctx.enter_context(self.nc.semaphore(f"{self.name}_{name}"))

    def ev(self, name, per=1, credit=0):
        return Event(self.sem(name), per, credit)

    def chain(self, name, per):
        return Chain(self.sem(name), per)

    def block(self):
        return self.ctx.enter_context(self.nc.Block())


def build(nc, a, out):
    qt_d = nc.dram_tensor("qt_scratch", [P, B * S], F32).ap()
    kt_d = nc.dram_tensor("kt_scratch", [P, B * S], F32).ap()
    skew = nc.dram_tensor("skew_scratch", [2, TB, P * BAND], F32).ap()
    with ExitStack() as top:
        X = top.enter_context(nc.sbuf_tensor("X", [P, SLOTS, E], F32))
        X2 = top.enter_context(nc.sbuf_tensor("X2", [P, NT, E], F32))
        ident = top.enter_context(nc.sbuf_tensor("ident", [P, P], F32))
        with nc.sbuf_tensor("V", [P, NT, E], F32) as V:
            first_projections(nc, a, X, V, ident, qt_d, kt_d, skew)
            first_attention(nc, a, V, X2, ident, qt_d, kt_d, skew)
        first_output(nc, a, X, X2, ident)
        layers(nc, a, X, ident)
        last_output(nc, X, X2, out)


def first_projections(nc, a, X, V, ident, qt_d, kt_d, skew):
    STEPS = NT // G
    with Part(nc, "pr") as t:
        Wq, Wk, Wv, bv = (t.sb(n, [P, E]) for n in ("Wq", "Wk", "Wv", "bv"))
        bq, bk, r0, bkr = (t.sb(n, [P, 1]) for n in ("bq", "bk", "r0", "bkr"))
        fill = t.sb("fill", [P, BAND])
        xh, xhT = t.sb("xh", [P, G, E]), t.sb("xhT", [P, G * P])
        qf, kf = t.sb("qf", [P, G * P]), t.sb("kf", [P, G * P])
        ps = t.psum()
        s_in, s_z, s_f, s_sk, s_bk = (t.sem(n) for n in ("in", "z", "f", "sk", "bk"))
        ln = LayerNorm(t, "ln", G)
        xh_done, t_mm, xhT_done = t.ev("xh"), t.ev("t", 1, 1), t.ev("xhT", 1, 1)
        q_mm, k_mm, v_mm = t.ev("qm"), t.ev("km"), t.ev("vm", 1, 1)
        q_ev, k_ev, v_ev = (t.ev(n, 1, 1) for n in ("qe", "ke", "ve"))
        q_out, k_out = t.ev("qo", 16, 1), t.ev("ko", 16, 1)
        block = t.block()

        @block.sync
        def _(e):
            for b in range(B):
                e.dma_start(X[:, b * (TB + 1) + 1:(b + 1) * (TB + 1), :],
                            a["L0_attn_x"][b].rearrange("(t p) d -> p t d", p=P)).then_inc(s_in, 16)
            for dst, src in ((Wq, "L0_attn_Wq"), (Wk, "L0_attn_Wk"), (Wv, "L0_attn_Wv"), (ident, "c_ident")):
                e.dma_start(dst[:], a[src]).then_inc(s_in, 16)
            for dst, src in ((bq, "L0_attn_bq"), (bk, "L0_attn_bk"), (r0, "rel0")):
                e.dma_start(dst[:], a[src].rearrange("(p o) -> p o", o=1)).then_inc(s_in, 16)
            e.dma_start(bv[:], a["L0_attn_bv"].partition_broadcast(P)).then_inc(s_in, 16)
            e.wait_ge(s_f, 2)
            for par in range(2):
                for i in range(TB):
                    e.dma_start(skew[par, i].rearrange("(p c) -> p c", c=BAND), fill[:]).then_inc(s_sk, 16)
            with e.Fori(0, STEPS) as i:
                q_ev.at(e, i)
                e.dma_start(qt_d[:, ds(i * (G * P), G * P)], qf[:]).then_inc(q_out.sem, 16)
                k_ev.at(e, i)
                e.dma_start(kt_d[:, ds(i * (G * P), G * P)], kf[:]).then_inc(k_out.sem, 16)
            e.wait_ge(s_sk, 16 * 2 * TB)
            q_out.at(e, STEPS - 1)
            k_out.at(e, STEPS - 1)

        @block.gpsimd
        def _(e):
            for b in range(B):
                e.memset(X[:, b * ZERO_SLOT, :], 0.0).then_inc(s_z, 1)
            e.memset(fill[:], 0.0).then_inc(s_f, 1)
            e.wait_ge(s_f, 1)
            e.affine_select(out=fill[:], in_=fill[:], compare_op=ALU.is_ge, fill=NEG, base=REL,
                            pattern=[[-1, BAND]], channel_multiplier=1).then_inc(s_f, 1)
            ln.open(e)
            with e.Fori(0, STEPS) as i:
                ln.rstd(e, G, i)

        @block.vector
        def _(e):
            v_ev.open(e)
            k_ev.open(e)
            k_out.open(e)
            e.wait_ge(s_in, 16 * 12)
            e.tensor_tensor(bkr[:], bk[:], r0[:], ALU.add).then_inc(s_bk, 1)
            e.wait_ge(s_bk, 1)
            with e.Fori(0, STEPS) as i:
                first = i * G + i // (TB // G) + 1
                ln.chain.start(e, i)
                xs = [X[:, ds(first + g, 1), :] for g in range(G)]
                ln.stats(e, xs)
                t_mm.at(e, i - 1)
                ln.apply(e, xs, [xh[:, g, :] for g in range(G)], i).then_inc(xh_done.sem, 1)
                k_mm.at(e, i)
                k_out.at(e, i - 1)
                e.tensor_scalar(kf[:], ps[:, 2, :], bkr[:, 0:1], None, ALU.add).then_inc(k_ev.sem, 1)
                v_mm.at(e, i)
                e.tensor_tensor(V[:, ds(i * G, G), :], ps[:, 3, :].rearrange("p (g d) -> p g d", g=G),
                                over(bv[:], G), ALU.add).then_inc(v_ev.sem, 1)

        @block.scalar
        def _(e):
            xhT_done.open(e)
            q_ev.open(e)
            q_out.open(e)
            e.wait_ge(s_in, 16 * 12)
            with e.Fori(0, STEPS) as i:
                t_mm.at(e, i)
                v_mm.at(e, i - 1)
                e.activation(xhT[:], ps[:, 0, :], ACT.Copy).then_inc(xhT_done.sem, 1)
                q_mm.at(e, i)
                q_out.at(e, i - 1)
                e.activation(qf[:], ps[:, 1, :], ACT.Identity, bias=bq[:, 0:1]).then_inc(q_ev.sem, 1)

        @block.tensor
        def _(e):
            t_mm.open(e)
            v_mm.open(e)
            e.wait_ge(s_in, 16 * 12)
            with e.Fori(0, STEPS) as i:
                xh_done.at(e, i)
                xhT_done.at(e, i - 1)
                for g in range(G):
                    mm = e.transpose(ps[:, 0, g * P:(g + 1) * P], xh[:, g, :], ident[:])
                mm.then_inc(t_mm.sem, 1)
                xhT_done.at(e, i)
                q_ev.at(e, i - 1)
                e.matmul(ps[:, 1, :], Wq[:], xhT[:], start=True, stop=True).then_inc(q_mm.sem, 1)
                k_ev.at(e, i - 1)
                e.matmul(ps[:, 2, :], Wk[:], xhT[:], start=True, stop=True).then_inc(k_mm.sem, 1)
                v_ev.at(e, i - 1)
                for g in range(G):
                    mm = e.matmul(ps[:, 3, g * P:(g + 1) * P], xhT[:, g * P:(g + 1) * P], Wv[:],
                                  start=True, stop=True)
                mm.then_inc(v_mm.sem, 1)


def first_attention(nc, a, V, O, ident, qt_d, kt_d, skew):
    JJ = TB // G
    NJ = sum(G * (u + 1) for u in range(JJ))
    with Part(nc, "at") as t:
        qh, kh = t.sb("qh", [D_A, 2, S]), t.sb("kh", [D_A, 2, S])
        relT, relD = t.sb("relT", [D_A, REL]), t.sb("relD", [D_A, REL])
        vh = t.sb("vh", [P, 2, TB, WIN])
        R = t.sb("R", [P, TB, REL])
        band = t.sb("band", [P, 2, TB, BAND])
        summed = t.sb("summed", [P, 2, BAND])
        mx, nb = t.sb("mx", [P, 2 * TB]), t.sb("nb", [P, TB])
        probs = [t.sb(f"probs{u}", [P, G, G * P * (u + 1)]) for u in range(JJ)]
        pT = t.sb("pT", [P, 2, G * P])
        part, sel = t.sb("part", [P, G * P]), t.sb("sel", [P, D_A + 1])
        rc, cell = t.sb("rc", [P, G]), t.sb("cell", [P, 1])
        ps = t.psum()
        s_in, s_set, s_rel = t.sem("in"), t.sem("set"), t.sem("rel")
        qk_in = t.ev("qkin", 32)
        vh_ev = t.ev("vh")
        r_mm, r_ev = t.ev("rm", TB // 2), t.ev("re", TB // 2, 1)
        r_out, r_in = t.ev("ro", 16, 1), t.ev("ri", 16, 2)
        s_mm = t.ev("sm", TB, 2)
        nb_ev = t.ev("nb", TB, 2)
        p_ev = t.ev("pe", TB, 1)
        t_mm = t.ev("tm", NJ, 1)
        tA, tD = t.ev("tA", NJ // 2, 1), t.ev("tD", NJ // 2, 1)
        pv_mm = t.ev("pv", NJ, 2)
        o_ev, g_mm, on = t.ev("oe", JJ), t.ev("gm", JJ, 1), t.ev("on", JJ, 1)
        c_max = t.chain("cm", 2 * TB - BAND // P)
        c_on = t.chain("co", JJ)
        block = t.block()
        R_BANK, T_BANKS, O_BANK = 0, (1, 6), 7

        def width(i):
            return P * (i + 1)

        def far(i):
            return P * max(0, i + 1 - BAND // P)

        def logits(i):
            lo = 2 + 2 * (i % 2)
            return ps[:, lo:lo + 2, :].rearrange("p b n -> p (b n)")

        def load_head(e, r, par):
            s_mm.at(e, r - 2)
            hd = r % HEADS_A
            row, col = hd % H_A * D_A, hd // H_A * S
            e.dma_start(qh[:, par, :], qt_d[ds(row, D_A), ds(col, S)]).then_inc(qk_in.sem, 16)
            e.dma_start(kh[:, par, :], kt_d[ds(row, D_A), ds(col, S)]).then_inc(qk_in.sem, 16)

        def skew_head(e, r, par):
            r_ev.at(e, r)
            r_in.at(e, r - 2)
            flat = skew[par]
            dst = bass.AP(flat.tensor, flat.offset + 1, [[BAND + 1, P], [P * BAND, TB], [1, REL]])
            e.dma_start(dst, R[:]).then_inc(r_out.sem, 16)
            nb_ev.at(e, r - 2)
            r_out.at(e, r)
            e.dma_start(band[:, par, :, :], flat.rearrange("t (p c) -> p t c", c=BAND))\
                .then_inc(r_in.sem, 16)

        def band_mm(e, r, par, j):
            if j == 0:
                qk_in.at(e, r)
            r_ev.at(e, r - 1 if j == 0 else r, None if j == 0 else j)
            for i in (2 * j, 2 * j + 1):
                mm = e.matmul(ps[:, R_BANK, i % 2 * REL:(i % 2 + 1) * REL], qh[:, par, i * P:(i + 1) * P],
                              relD[:], start=True, stop=True)
            mm.then_inc(r_mm.sem, 1)

        def band_copy(e, r, j):
            r_mm.at(e, r, j + 1)
            if j == 0:
                r_out.at(e, r - 1)
            e.activation(R[:, 2 * j:2 * j + 2, :], ps[:, R_BANK, :].rearrange("p (i n) -> p i n", i=2),
                         ACT.Copy).then_inc(r_ev.sem, 1)

        def logits_mm(e, n, par, i):
            p_ev.at(e, *((n, i - 1) if i >= 2 else (n - 1, TB + i - 1)))
            w = width(i)
            for c in range(0, w, 512):
                mm = e.matmul(logits(i)[:, c:min(w, c + 512)], qh[:, par, i * P:(i + 1) * P],
                              kh[:, par, c:min(w, c + 512)], start=True, stop=True)
            mm.then_inc(s_mm.sem, 1)

        def row_max(e, n, par, i):
            s_mm.at(e, n, i + 1)
            f = far(i)
            if f:
                c_max.link(e.tensor_reduce(mx[:, 2 * i:2 * i + 1], logits(i)[:, 0:f], AX.X, ALU.max))
            if i == 0:
                r_in.at(e, n)
            p_ev.at(e, *((n, i - 1) if i >= 2 else (n - 1, TB + i - 1)))
            wb = width(i) - f
            step_in(e, cell[:])
            c_max.link(e.tensor_tensor_reduce(
                summed[:, i % 2, 0:wb], logits(i)[:, f:f + wb], band[:, par, i, BAND - wb:BAND],
                1.0, mx[:, 2 * i:2 * i + 1] if f else NEG, ALU.add, ALU.max, mx[:, 2 * i + 1:2 * i + 2]))
            e.tensor_scalar(nb[:, i:i + 1], mx[:, 2 * i + 1:2 * i + 2], -SC_A, None, ALU.mult)\
                .then_inc(nb_ev.sem, 1)

        def exps(e, n, i):
            nb_ev.at(e, n, i + 1)
            u, f, w = i // G, far(i), width(i)
            if i % G == 0:
                t_mm.at(e, n - 1, (4, NJ)[u])
            if f:
                e.activation(probs[u][:, i % G, 0:f], logits(i)[:, 0:f], ACT.Exp,
                             bias=nb[:, i:i + 1], scale=SC_A)
            e.activation(probs[u][:, i % G, f:w], summed[:, i % 2, 0:w - f], ACT.Exp,
                         bias=nb[:, i:i + 1], scale=SC_A).then_inc(p_ev.sem, 1)

        def index(u, j):
            return G * u * (u + 1) // 2 + j

        def copied(jj):
            return (tA, tD)[jj % 2], jj // 2 + 1

        def copied_before(e, n, jj):
            ev, k = copied(jj)
            ev.at(e, n - 1, NJ // 2) if k == 1 else ev.at(e, n, k - 1)

        def turn(e, n, u, j):
            jj = index(u, j)
            if j == 0:
                p_ev.at(e, n, G * (u + 1))
            copied_before(e, n, jj)
            i0 = max(j, G * u)
            for i in range(i0, G * (u + 1)):
                mm = e.transpose(ps[:, T_BANKS[jj % 2], i % G * P:(i % G + 1) * P],
                                 probs[u][:, i % G, j * P:(j + 1) * P], ident[:])
            mm.then_inc(t_mm.sem, 1)

        def turn_copy(e, n, u, j):
            jj = index(u, j)
            t_mm.at(e, n, jj + 1)
            pv_mm.at(e, *((n, jj - 1) if jj >= 2 else (n - 1, NJ + jj - 1)))
            c0 = max(0, j - G * u) * P
            src, dst = ps[:, T_BANKS[jj % 2], c0:G * P], pT[:, jj % 2, c0:G * P]
            ins = e.activation(dst, src, ACT.Copy) if jj % 2 == 0 else e.tensor_copy(dst, src)
            ins.then_inc(copied(jj)[0].sem, 1)

        def values_mm(e, n, par, u, j):
            jj = index(u, j)
            if jj == 0:
                vh_ev.at(e, n)
            if j == 0:
                on.at(e, n - 1 if u == 0 else n, JJ if u == 0 else u)
            ev, k = copied(jj)
            ev.at(e, n, k)
            c, c0 = j % G, max(0, j - G * u) * P
            e.matmul(ps[WIN * c:WIN * (c + 1), O_BANK, c0:G * P], vh[:, par, j, :],
                     pT[:, jj % 2, c0:G * P], start=(j < G), stop=(j >= G * u),
                     skip_group_check=True).then_inc(pv_mm.sem, 1)

        def part_copy(e, n, u):
            pv_mm.at(e, n, index(u, G * (u + 1)))
            g_mm.at(e, n - 1 if u == 0 else n, JJ if u == 0 else u)
            e.tensor_copy(part[:], ps[:, O_BANK, :]).then_inc(o_ev.sem, 1)

        def gather(e, n, u):
            o_ev.at(e, n, u + 1)
            for i in range(G):
                k = WIN * min(G, G * u + i + 1)
                mm = e.matmul(ps[:, O_BANK, i * (D_A + 1):(i + 1) * (D_A + 1)], part[0:k, i * P:(i + 1) * P],
                              sel[0:k, :], start=True, stop=True)
            mm.then_inc(g_mm.sem, 1)

        def normalize(e, n, u):
            g_mm.at(e, n, u + 1)
            c_on.start(e, n, u)
            o = ps[:, O_BANK, 0:G * (D_A + 1)].rearrange("p (i d) -> p i d", i=G)
            c_on.link(e.reciprocal(rc[:].unsqueeze(2), o[:, :, D_A:D_A + 1]))
            tile, col = n // H_A * TB + G * u, n % H_A * D_A
            e.tensor_tensor(O[:, ds(tile, G), ds(col, D_A)], o[:, :, 0:D_A], wide(rc[:], D_A), ALU.mult)\
                .then_inc(on.sem, 1)

        def values_in(e, r, par):
            pv_mm.at(e, r - 2)
            hd = r % HEADS_A
            e.tensor_copy(vh[:, par, :, 0:D_A], V[:, ds(hd // H_A * TB, TB), ds(hd % H_A * D_A, D_A)])\
                .then_inc(vh_ev.sem, 1)

        def head(eng, e, n, par, before, after=True):
            u1 = [(n - 1, 1 - par, 1, j) for j in range(G * JJ)] if before else []
            u0 = [(n, par, 0, j) for j in range(G)]
            if eng == "tensor":
                for i in range(G):
                    logits_mm(e, n, par, i)
                    for m, q, u, j in u1[2 * i:2 * i + 2]:
                        turn(e, m, u, j)
                        if j:
                            values_mm(e, m, q, u, j - 1)
                for i in range(G, TB):
                    logits_mm(e, n, par, i)
                    if i == G:
                        if before:
                            values_mm(e, n - 1, 1 - par, 1, TB - 1)
                    band_mm(e, n + 1, 1 - par, i - G)
                    if i == G + 1 and before:
                        gather(e, n - 1, 1)
                    turn(e, n, 0, i - G)
                    if i > G:
                        values_mm(e, n, par, 0, i - G - 1)
                values_mm(e, n, par, 0, G - 1)
                gather(e, n, 0)
            if eng == "vector":
                c_max.start(e, n)
                for i in range(TB):
                    row_max(e, n, par, i)
                    if i < G:
                        for m, q, u, j in u1[2 * i:2 * i + 2]:
                            if index(u, j) % 2:
                                turn_copy(e, m, u, j)
                    else:
                        if i == G and before:
                            part_copy(e, n - 1, 1)
                        if i == G + 1 and before:
                            normalize(e, n - 1, 1)
                        if index(0, i - G) % 2:
                            turn_copy(e, n, 0, i - G)
                part_copy(e, n, 0)
                normalize(e, n, 0)
            if eng == "scalar":
                for i in range(TB):
                    exps(e, n, i)
                    if i < G:
                        for m, q, u, j in u1[2 * i:2 * i + 2]:
                            if index(u, j) % 2 == 0:
                                turn_copy(e, m, u, j)
                    else:
                        band_copy(e, n + 1, i - G)
                        if index(0, i - G) % 2 == 0:
                            turn_copy(e, n, 0, i - G)
            if eng == "gpsimd":
                values_in(e, n + 1, 1 - par)
            if eng == "sync":
                load_head(e, n + 1, 1 - par)
                skew_head(e, n + 1, 1 - par)

        def heads(eng, e):
            if eng == "sync":
                load_head(e, 0, 0)
                skew_head(e, 0, 0)
            if eng == "gpsimd":
                values_in(e, 0, 0)
            for j in range(TB // 2):
                if eng == "tensor":
                    band_mm(e, 0, 0, j)
                if eng == "scalar":
                    band_copy(e, 0, j)
            head(eng, e, 0, 0, False)
            head(eng, e, 1, 1, True)
            with e.Fori(1, HEADS_A // 2) as pair:
                for par in range(2):
                    head(eng, e, pair * 2 + par, par, True)
            n = HEADS_A - 1
            for j in range(G * JJ):
                if eng == "tensor":
                    turn(e, n, 1, j)
                    if j:
                        values_mm(e, n, 1, 1, j - 1)
                if eng == ("scalar", "vector")[index(1, j) % 2]:
                    turn_copy(e, n, 1, j)
            if eng == "tensor":
                values_mm(e, n, 1, 1, G * JJ - 1)
                gather(e, n, 1)
            if eng == "vector":
                part_copy(e, n, 1)
                normalize(e, n, 1)

        @block.sync
        def _(e):
            e.dma_start(relT[:], a["relT"]).then_inc(s_in, 16)
            e.dma_start(sel[:], a["c_sel"]).then_inc(s_in, 16)
            r_out.open(e)
            r_in.open(e)
            heads("sync", e)
            r_in.at(e, HEADS_A)

        @block.gpsimd
        def _(e):
            e.memset(vh[:], 0.0).then_inc(s_set, 1)
            e.wait_ge(s_set, 1)
            e.memset(vh[:, :, :, D_A:D_A + 1], 1.0).then_inc(s_set, 1)
            e.wait_ge(s_set, 2)
            heads("gpsimd", e)

        @block.vector
        def _(e):
            for ev in (nb_ev, tD, on):
                ev.open(e)
            e.wait_ge(s_in, 32)
            e.tensor_scalar(relD[:], relT[:], relT[:, 0:1], None, ALU.subtract).then_inc(s_rel, 1)
            e.memset(ps[:, O_BANK, :], 0.0).then_inc(s_rel, 1)
            heads("vector", e)

        @block.scalar
        def _(e):
            for ev in (r_ev, p_ev, tA):
                ev.open(e)
            heads("scalar", e)

        @block.tensor
        def _(e):
            for ev in (s_mm, t_mm, pv_mm, g_mm):
                ev.open(e)
            e.wait_ge(s_rel, 2)
            heads("tensor", e)


def first_output(nc, a, X, X2, ident):
    STEPS = NT // G
    with Part(nc, "ou") as t:
        Wo, bo = t.sb("Wo", [P, E]), t.sb("bo", [P, E])
        oc, oT = t.sb("oc", [P, G, E]), t.sb("oT", [P, G * P])
        y, yn = t.sb("y", [P, G, E]), t.sb("yn", [P, G, E])
        ps = t.psum()
        s_in = t.sem("in")
        oc_ev, t_mm, oT_ev = t.ev("oc"), t.ev("tm", 1, 1), t.ev("oT", 1, 1)
        o_mm, y_ev = t.ev("om", 1, 1), t.ev("ye", 1, 1)
        ln = LayerNorm(t, "ln", G, 2)
        ch = t.chain("ch", 2)
        block = t.block()

        @block.sync
        def _(e):
            e.dma_start(Wo[:], a["L0_attn_Wo"]).then_inc(s_in, 16)
            e.dma_start(bo[:], a["L0_attn_bo"].partition_broadcast(P)).then_inc(s_in, 16)

        @block.gpsimd
        def _(e):
            ln.open(e)
            with e.Fori(0, STEPS) as i:
                t_mm.at(e, i - 1)
                e.tensor_copy(oc[:], X2[:, ds(i * G, G), :]).then_inc(oc_ev.sem, 1)
                ln.rstd(e, G, i, 1)
                ln.rstd(e, G, i, 2)

        @block.tensor
        def _(e):
            t_mm.open(e)
            o_mm.open(e)
            e.wait_ge(s_in, 32)
            with e.Fori(0, STEPS) as i:
                oc_ev.at(e, i)
                oT_ev.at(e, i - 1)
                for g in range(G):
                    mm = e.transpose(ps[:, 0, g * P:(g + 1) * P], oc[:, g, :], ident[:])
                mm.then_inc(t_mm.sem, 1)
                oT_ev.at(e, i)
                y_ev.at(e, i - 1)
                for g in range(G):
                    mm = e.matmul(ps[:, 1, g * P:(g + 1) * P], oT[:, g * P:(g + 1) * P], Wo[:],
                                  start=True, stop=True)
                mm.then_inc(o_mm.sem, 1)

        @block.scalar
        def _(e):
            oT_ev.open(e)
            with e.Fori(0, STEPS) as i:
                t_mm.at(e, i)
                o_mm.at(e, i - 1)
                e.activation(oT[:], ps[:, 0, :], ACT.Copy).then_inc(oT_ev.sem, 1)

        @block.vector
        def _(e):
            y_ev.open(e)
            e.wait_ge(s_in, 32)
            with e.Fori(0, STEPS) as i:
                first = i * G + i // (TB // G) + 1
                ch.start(e, i)
                ln.chain.start(e, i)
                ys = [y[:, g, :] for g in range(G)]
                o_mm.at(e, i)
                ins = e.tensor_tensor(y[:], ps[:, 1, :].rearrange("p (g d) -> p g d", g=G), over(bo[:], G),
                                      ALU.add)
                ins.then_inc(y_ev.sem, 1)
                y_ev.at(e, i)
                ln.stats(e, ys)
                ch.link(ln.apply(e, ys, [yn[:, g, :] for g in range(G)], i, 1))
                x2 = X2[:, ds(i * G, G), :]
                ch.link(e.tensor_tensor(x2, X[:, ds(first, G), :], yn[:], ALU.add))
                xs = [X2[:, ds(i * G + g, 1), :] for g in range(G)]
                ln.stats(e, xs)
                ln.apply(e, xs, [X[:, ds(first + g, 1), :] for g in range(G)], i, 2)


def layers(nc, a, X, ident):
    with Part(nc, "la") as t:
        Y = t.sb("Y", [P, SLOTS, E])
        Wqkv = t.sb("Wqkv", [P, 2, 3 * INNER])
        Wo, W1 = t.sb("Wo", [P, H * D // P, E]), t.sb("W1", [P, 2 * HID])
        W2 = t.sb("W2", [P, len(PIECES), E])
        rot, scales = t.sb("rot", [P, TB, 4 * D]), t.sb("scales", [P, DEPTH, 4 * D])
        lng, lnb, b1 = t.sb("lng", [P, DEPTH]), t.sb("lnb", [P, DEPTH]), t.sb("b1", [P, 2 * len(PIECES), DEPTH])
        b2 = t.sb("b2", [P, DEPTH, E])
        shift, last = t.sb("shift", [P, P]), t.sb("last", [P, P])
        mask, identb, mask32 = t.sb("mask", [P, TB, KW], BF16), t.sb("identb", [P, P], BF16), t.sb("mask32", [P, 2, KW])
        begins = t.sb("begins", [P, TB])
        xs, xsT = t.sb("xs", [P, E]), t.sb("xsT", [P, RING, P])
        raw, rt, sw = t.sb("raw", [P, 2 * INNER]), t.sb("rt", [P, 2 * INNER]), t.sb("sw", [P, 2 * INNER])
        sq = t.sb("sq", [P, 2, 512])
        ssum, rn, rq = t.sb("ssum", [P, 2 * H]), t.sb("rn", [P, RING, 2 * H]), t.sb("rq", [P, RING, H])
        tab = t.sb("tab", [P, RING, 4, D])
        v = t.sb("v", [P, RING, INNER])
        qT, kT = t.sb("qT", [P, H // 2, 2, P]), t.sb("kT", [P, RING, H // 2, KW])
        rmax, nb, rs, rc = t.sb("rmax", [P, H]), t.sb("nb", [P, H]), t.sb("rs", [P, H]), t.sb("rc", [P, H])
        pr, pT, pTp = t.sb("pr", [P, H, KW]), t.sb("pT", [P, H, P]), t.sb("pTp", [P, H, WIN])
        oT, ys, yn, ynT = t.sb("oT", [P, 8, P]), t.sb("ys", [P, E]), t.sb("yn", [P, E]), t.sb("ynT", [P, RING, P])
        gl, gT, yb = t.sb("gl", [P, 3, P]), t.sb("gT", [P, 3, P]), t.sb("yb", [P, RING, E])
        ps = t.psum()

        s_in, s_set, s_mask = t.sem("in"), t.sem("set"), t.sem("mask")
        w_qkv, w_o, w_1, w_2 = t.ev("wq", 16), t.ev("wo", 16), t.ev("w1", 16), t.ev("w2", 32)
        x_ev = t.ev("xe", 1, NT)
        sh_mm, sh_ev, xl_ev, xT_mm, xT_ev = t.ev("shm"), t.ev("she", 1, 1), t.ev("xle", 1, 1), t.ev("xtm", 1, 1), t.ev("xte", 1, 1)
        q_mm, q_ev, q_sq, q_ss = t.ev("qm", 6, 1), t.ev("qe", 6, 1), t.ev("qsq", 4, 1), t.ev("qss", 4, 1)
        rn_ev, rq_ev = t.ev("rn", 1, 1), t.ev("rq", 1, RING)
        tab_ev, cl_ev = t.ev("tab"), t.ev("cl")
        power = t.sb("power", [P, 2 * H])
        rc_ev = [t.ev("rcq", 1, RING), t.ev("rck", 1, RING)]
        rsw_ev, rt_ev, kn_ev = t.ev("rsw", 2, RING), t.ev("rte", 2, 1), t.ev("kn", 1, 1)
        kc_ev, T_mm, T_ev = t.ev("kc"), t.ev("Tm", 4, 1), t.ev("Te", 4, 1)
        S_mm, m_ev, e_ev = t.ev("Sm", 8, RING), t.ev("me", 8, 1), t.ev("ee", 8, RING)
        pt_mm, pt_ev, pp_ev = t.ev("ptm", 4, 1), t.ev("pte", 4, 1), t.ev("ppe", 4, 1)
        nm_ev, pv_mm = t.ev("nme", 4, 1), t.ev("pv", 2, 2)
        c_nb, c_rc = t.chain("cnb", 8), t.chain("crc", 4)
        oT_ev, wo_mm, y_ev = t.ev("ote", 2, 1), t.ev("wom", 1, 1), t.ev("ye", 1, 1)
        s2_mm, s2_ev, yl_ev = t.ev("s2m", 1, 1), t.ev("s2e", 1, 1), t.ev("yle", 1, 1)
        yn_ev, nT_mm, nT_ev = t.ev("yn", 1, 1), t.ev("ntm", 1, 1), t.ev("nte", 1, 1)
        g_mm, g_ev, a_mm, a_ev, f_mm = t.ev("gm", 1, 1), t.ev("ge", 1, 1), t.ev("am", 1, RING), t.ev("ae", 1, 1), t.ev("fm", 1, 1)
        yb_ev = t.ev("yb", 1, 1)
        ln = LayerNorm(t, "ln", 1)
        block = t.block()
        BANK_T, BANK_O, BANK_G, BANK_Y = 4, 5, 6, 7

        def layer(n):
            return n // NT


        def shift_in(eng, e, n, m):
            cur = slot(n % NT)
            if eng == "tensor":
                x_ev.at(e, n - NT)
                q_ev.at(e, n - 1, 5)
                e.matmul(ps[:, 0, 0:E // 2], shift[:], X[:, ds(cur, 1), E // 2:E], start=True, stop=False)
                e.matmul(ps[:, 0, 0:E // 2], last[:], X[:, ds(cur - 1, 1), E // 2:E], start=False, stop=True)\
                    .then_inc(sh_mm.sem, 1)
            if eng == "scalar":
                sh_mm.at(e, n)
                xT_mm.at(e, n - 1)
                e.activation(xs[:, E // 2:E], ps[:, 0, 0:E // 2], ACT.Copy).then_inc(sh_ev.sem, 1)
            if eng == "gpsimd":
                x_ev.at(e, n - NT)
                xT_mm.at(e, n - 1)
                e.tensor_copy(xs[:, 0:E // 2], X[:, ds(cur, 1), 0:E // 2]).then_inc(xl_ev.sem, 1)

        def turn_in(eng, e, n, m):
            if eng == "tensor":
                sh_ev.at(e, n)
                xl_ev.at(e, n)
                q_ev.at(e, n - 1, 6)
                e.transpose(ps[:, 1, 0:P], xs[:], ident[:]).then_inc(xT_mm.sem, 1)
            if eng == "scalar":
                xT_mm.at(e, n)
                q_mm.at(e, n - 1)
                e.activation(xsT[:, m, :], ps[:, 1, 0:P], ACT.Copy).then_inc(xT_ev.sem, 1)

        def qkv(c):
            def job(eng, e, n, m):
                bank = c % 2
                if eng == "tensor":
                    if c == 0:
                        xT_ev.at(e, n)
                        w_qkv.at(e, layer(n))
                        sh_ev.at(e, n)
                    if c >= 2:
                        q_ev.at(e, n, c - 1)
                        q_sq.at(e, n, min(c - 1, 4))
                    e.matmul(ps[:, bank, :], xsT[:, m, :], Wqkv[:, ds(layer(n) % 2, 1), c * 512:(c + 1) * 512],
                             start=True, stop=True).then_inc(q_mm.sem, 1)
                if eng == "scalar":
                    q_mm.at(e, n, c + 1)
                    if c < 4:
                        if c % 2 == 0:
                            rsw_ev.at(e, n - 1, c // 2 + 1)
                            rc_ev[c // 2].at(e, n - 1)
                        e.activation(raw[:, c * 512:(c + 1) * 512], ps[:, bank, :], ACT.Copy)\
                            .then_inc(q_ev.sem, 1)
                        q_ss.at(e, *((n, c - 1) if c >= 2 else (n - 1, c + 3)))
                        e.activation(sq[:, c % 2, :], ps[:, bank, :], ACT.Square).then_inc(q_sq.sem, 1)
                    else:
                        pv_mm.at(e, n - 2)
                        e.activation(v[:, m, (c - 4) * 512:(c - 3) * 512], ps[:, bank, :], ACT.Copy)\
                            .then_inc(q_ev.sem, 1)
                if eng == "vector" and c < 4:
                    q_sq.at(e, n, c + 1)
                    if c == 0:
                        rn_ev.at(e, n - 1)
                    e.tensor_reduce(ssum[:, c * 8:(c + 1) * 8],
                                    sq[:, c % 2, :].rearrange("p (h d) -> p h d", d=D), AX.X, ALU.add)\
                        .then_inc(q_ss.sem, 1)
            return job

        def norms(eng, e, n, m):
            if eng == "vector":
                q_ss.at(e, n)
                e.tensor_scalar(ssum[:], ssum[:], 1e-24, None, ALU.max).then_inc(cl_ev.sem, 1)
            if eng == "gpsimd":
                cl_ev.at(e, n)
                rq_ev.at(e, n - RING)
                e.tensor_tensor(rn[:, m, :], ssum[:], power[:], ALU.pow).then_inc(rn_ev.sem, 1)

        def scale_q(eng, e, n, m):
            if eng == "vector":
                rn_ev.at(e, n)
                e_ev.at(e, n - RING)
                e.tensor_scalar(rq[:, m, :], rn[:, m, 0:H], QK_SCALE, None, ALU.mult).then_inc(rq_ev.sem, 1)

        def tables(eng, e, n, m):
            if eng == "gpsimd":
                rsw_ev.at(e, n - RING)
                rc_ev[1].at(e, n - RING)
                e.tensor_tensor(tab[:, m].rearrange("p f d -> p (f d)"), rot[:, ds(n % TB, 1), :],
                                scales[:, ds(layer(n), 1), :], ALU.mult).then_inc(tab_ev.sem, 1)

        def swap(w):
            def job(eng, e, n, m):
                if eng == "vector":
                    q_ev.at(e, n, 2 * w + 2)
                    tab_ev.at(e, n)
                    rt_ev.at(e, n - 1, w + 1)
                    s3 = raw[:, w * INNER:(w + 1) * INNER].rearrange("p (h t d) -> p h t d", h=H, t=2)
                    d3 = sw[:, w * INNER:(w + 1) * INNER].rearrange("p (h t d) -> p h t d", h=H, t=2)
                    for half in range(2):
                        ins = e.tensor_tensor(d3[:, :, half, :], s3[:, :, 1 - half, :],
                                              over(tab[:, m, 2 * w + 1, half * 32:(half + 1) * 32], H), ALU.mult)
                    ins.then_inc(rsw_ev.sem, 1)
            return job

        def straight(w):
            def job(eng, e, n, m):
                if eng == ("gpsimd", "vector")[w]:
                    q_ev.at(e, n, 2 * w + 2)
                    tab_ev.at(e, n)
                    T_mm.at(e, n - 1, 3 + w)
                    e.tensor_tensor(rt[:, w * INNER:(w + 1) * INNER].rearrange("p (h d) -> p h d", d=D),
                                    raw[:, w * INNER:(w + 1) * INNER].rearrange("p (h d) -> p h d", d=D),
                                    over(tab[:, m, 2 * w, :], H), ALU.mult).then_inc(rc_ev[w].sem, 1)
            return job

        def rotated(w):
            def job(eng, e, n, m):
                if eng == "gpsimd":
                    dst = rt[:, w * INNER:(w + 1) * INNER]
                    rsw_ev.at(e, n, w + 1)
                    rc_ev[w].at(e, n)
                    e.tensor_tensor(dst, dst, sw[:, w * INNER:(w + 1) * INNER], ALU.add).then_inc(rt_ev.sem, 1)
                    if w:
                        rt_ev.at(e, n, 2)
                        rn_ev.at(e, n)
                        d = dst.rearrange("p (h d) -> p h d", d=D)
                        e.tensor_tensor(d, d, wide(rn[:, m, H:2 * H], D), ALU.mult).then_inc(kn_ev.sem, 1)
            return job

        def carry(eng, e, n, m):
            if eng == "gpsimd":
                T_ev.at(e, n - 1)
                S_mm.at(e, n - RING)
                flag = begins[:, ds(n % TB, 1)].unsqueeze(2).to_broadcast([P, H // 2, WIN])
                e.tensor_tensor(kT[:, m, :, 0:WIN], kT[:, (m - 1) % RING, :, P:KW], flag, ALU.mult)\
                    .then_inc(kc_ev.sem, 1)

        def turn_qk(u):
            w, half = u % 2, u // 2
            def job(eng, e, n, m):
                if eng == "tensor":
                    kn_ev.at(e, n) if w else rt_ev.at(e, n, 1)
                    T_ev.at(e, *((n, u) if u else (n - 1, 4)))
                    for j in range(4):
                        c = w * INNER + (4 * half + j) * P
                        mm = e.transpose(ps[:, BANK_T, j * P:(j + 1) * P], rt[:, c:c + P], ident[:])
                    mm.then_inc(T_mm.sem, 1)
                if eng == "scalar":
                    T_mm.at(e, n, u + 1)
                    pairs = slice(4 * half, 4 * half + 4)
                    src = ps[:, BANK_T, :].rearrange("p (j t) -> p j t", j=4)
                    if w:
                        S_mm.at(e, n - RING)
                        e.activation(kT[:, m, pairs, WIN:KW], src, ACT.Copy).then_inc(T_ev.sem, 1)
                    else:
                        S_mm.at(e, n - 1, 4 * half + 4)
                        e.activation(qT[0:D, pairs, 0, :], src[0:D], ACT.Copy)
                        e.activation(qT[D:P, pairs, 1, :], src[D:P], ACT.Copy).then_inc(T_ev.sem, 1)
            return job

        def scores(p):
            bank = 2 + p % 2
            def job(eng, e, n, m):
                both = ps[:, bank, 0:2 * KW].rearrange("p (h k) -> p h k", h=2)
                if eng == "tensor":
                    e_ev.at(e, *((n, p - 1) if p >= 2 else (n - 1, p + 7)))
                    T_ev.at(e, n, 2 + 2 * (p // 4))
                    if p == 0:
                        kc_ev.at(e, n)
                    e.matmul(both, identb[:], mask[:, ds(n % TB, 1), :].to_broadcast([P, 2, KW]),
                             start=True, stop=True)
                    for h in range(2):
                        mm = e.matmul(both[:, h, :], qT[:, p, h, :], kT[:, m, p, :], start=False, stop=True,
                                      skip_group_check=True)
                    mm.then_inc(S_mm.sem, 1)
                if eng == "vector":
                    S_mm.at(e, n, p + 1)
                    c_nb.start(e, n, p)
                    if p == 0:
                        rq_ev.at(e, n)
                    hs = slice(2 * p, 2 * p + 2)
                    c_nb.link(e.tensor_reduce(rmax[:, hs], both, AX.X, ALU.max, negate=True))
                    e_ev.at(e, n - 1, p + 1)
                    e.tensor_tensor(nb[:, hs], rmax[:, hs], rq[:, m, hs], ALU.mult).then_inc(m_ev.sem, 1)
                if eng == "scalar":
                    m_ev.at(e, n, p + 1)
                    nm_ev.at(e, n - 1, p // 2 + 1)
                    pt_mm.at(e, n - 1, p // 2 + 1)
                    pp_ev.at(e, n - 1, p // 2 + 1)
                    for h in range(2):
                        hh = 2 * p + h
                        ins = e.activation(pr[:, hh, :], both[:, h, :], ACT.Exp, bias=nb[:, hh:hh + 1],
                                           scale=rq[:, m, hh:hh + 1], accum_out=rs[:, hh:hh + 1])
                    ins.then_inc(e_ev.sem, 1)
            return job

        def over_sum(u):
            hs = slice(4 * u, 4 * u + 4)
            def job(eng, e, n, m):
                if eng == "vector":
                    e_ev.at(e, n, 2 * u + 2)
                    c_rc.start(e, n, u)
                    c_rc.link(e.reciprocal(rc[:, hs], rs[:, hs]))
                    e.tensor_tensor(pr[:, hs, :], pr[:, hs, :], wide(rc[:, hs], KW), ALU.mult)\
                        .then_inc(nm_ev.sem, 1)
                    nm_ev.at(e, n, u + 1)
                    pv_mm.at(e, n - 1, u // 2 + 1)
                    e.transpose(pTp[P - WIN:P, hs, :], pr[0:WIN, hs, 0:WIN]).then_inc(pp_ev.sem, 1)
            return job

        def turn_p(u):
            hs = slice(4 * u, 4 * u + 4)
            def job(eng, e, n, m):
                if eng == "tensor":
                    nm_ev.at(e, n, u + 1)
                    pt_ev.at(e, n, u) if u % 2 else oT_ev.at(e, *((n, 1) if u else (n - 1, 2)))
                    for j in range(4):
                        mm = e.transpose(ps[:, BANK_O, j * P:(j + 1) * P], pr[:, 4 * u + j, WIN:KW], ident[:])
                    mm.then_inc(pt_mm.sem, 1)
                if eng == "vector":
                    pt_mm.at(e, n, u + 1)
                    pv_mm.at(e, n - 1, u // 2 + 1)
                    e.tensor_copy(pT[:, hs, :], ps[:, BANK_O, :].rearrange("p (j t) -> p j t", j=4))\
                        .then_inc(pt_ev.sem, 1)
            return job

        def values(u):
            def job(eng, e, n, m):
                if eng == "tensor":
                    pt_ev.at(e, n, 2 * u + 2)
                    pp_ev.at(e, n, 2 * u + 2)
                    q_ev.at(e, n)
                    for before in range(2):
                        for j in range(8):
                            h = 8 * u + j
                            row, col = h % 2 * D, j // 2 * P
                            src, p = ((m - 1) % RING, pTp) if before else (m, pT)
                            mm = e.matmul(ps[row:row + D, BANK_O, col:col + (WIN if before else P)],
                                          v[:, src, h * D:(h + 1) * D], p[:, h, :],
                                          start=(not before and j < 2), stop=True, skip_group_check=True)
                    mm.then_inc(pv_mm.sem, 1)
                if eng == "scalar":
                    pv_mm.at(e, n, u + 1)
                    if u == 0:
                        wo_mm.at(e, n - 1)
                    e.activation(oT[:, 4 * u:4 * u + 4, :], ps[:, BANK_O, :].rearrange("p (j t) -> p j t", j=4),
                                 ACT.Copy).then_inc(oT_ev.sem, 1)
            return job

        def project(eng, e, n, m):
            cur = slot(n % NT)
            if eng == "tensor":
                oT_ev.at(e, n)
                w_o.at(e, layer(n))
                nT_ev.at(e, n - 1)
                for j in range(8):
                    mm = e.matmul(ps[:, BANK_Y, 0:E], oT[:, j, :], Wo[:, j, :], start=(j == 0), stop=(j == 7))
                mm.then_inc(wo_mm.sem, 1)
            if eng == "vector":
                wo_mm.at(e, n)
                e.tensor_tensor(Y[:, ds(cur, 1), :], ps[:, BANK_Y, 0:E], X[:, ds(cur, 1), :], ALU.add)\
                    .then_inc(y_ev.sem, 1)

        def shift_y(eng, e, n, m):
            cur = slot(n % NT)
            out = ps[:, BANK_Y, 0:E // 2]
            if eng == "tensor":
                y_ev.at(e, n)
                e.matmul(out, shift[:], Y[:, ds(cur, 1), E // 2:E], start=True, stop=False)
                e.matmul(out, last[:], Y[:, ds(cur - 1, 1), E // 2:E], start=False, stop=True)\
                    .then_inc(s2_mm.sem, 1)
            if eng == "scalar":
                s2_mm.at(e, n)
                yn_ev.at(e, n - 1)
                e.activation(ys[:, E // 2:E], out, ACT.Copy).then_inc(s2_ev.sem, 1)
            if eng == "gpsimd":
                y_ev.at(e, n)
                yn_ev.at(e, n - 1)
                e.tensor_copy(ys[:, 0:E // 2], Y[:, ds(cur, 1), 0:E // 2]).then_inc(yl_ev.sem, 1)

        def residual(eng, e, n, m):
            if eng == "gpsimd":
                y_ev.at(e, n)
                x_ev.at(e, n - RING)
                e.tensor_tensor(yb[:, m, :], Y[:, ds(slot(n % NT), 1), :], b2[:, ds(layer(n), 1), :], ALU.add)\
                    .then_inc(yb_ev.sem, 1)

        def statistics(eng, e, n, m):
            if eng == "vector":
                s2_ev.at(e, n)
                yl_ev.at(e, n)
                ln.chain.start(e, n)
                ln.stats(e, [ys[:]])
            if eng == "gpsimd":
                ln.rstd(e, 1, n)

        def normalize(eng, e, n, m):
            if eng == "vector":
                nT_mm.at(e, n - 1)
                ln.apply(e, [ys[:]], [yn[:]], n).then_inc(yn_ev.sem, 1)

        def turn_y(eng, e, n, m):
            if eng == "tensor":
                yn_ev.at(e, n)
                e.transpose(ps[:, BANK_Y, 0:E], yn[:], ident[:]).then_inc(nT_mm.sem, 1)
            if eng == "scalar":
                nT_mm.at(e, n)
                a_mm.at(e, n - RING)
                e.activation(ynT[:, m, :], ps[:, BANK_Y, 0:E], ACT.Identity, bias=lnb[:, ds(layer(n), 1)],
                             scale=lng[:, ds(layer(n), 1)]).then_inc(nT_ev.sem, 1)

        def gate(eng, e, n, m):
            if eng == "tensor":
                nT_ev.at(e, n)
                w_1.at(e, layer(n))
                x_ev.at(e, n - 1)
                for j, (c, w) in enumerate(PIECES):
                    mm = e.matmul(ps[0:w, BANK_G, j * P:(j + 1) * P], W1[:, HID + c:HID + c + w], ynT[:, m, :],
                                  start=True, stop=True)
                mm.then_inc(g_mm.sem, 1)
            if eng == "scalar":
                g_mm.at(e, n)
                a_ev.at(e, n - 1)
                for j, (c, w) in enumerate(PIECES):
                    ins = e.activation(gl[0:w, j, :], ps[0:w, BANK_G, j * P:(j + 1) * P], ACT.Gelu,
                                       bias=b1[0:w, 3 + j, ds(layer(n), 1)])
                ins.then_inc(g_ev.sem, 1)

        def gated(eng, e, n, m):
            if eng == "tensor":
                g_ev.at(e, n)
                for j, (c, w) in enumerate(PIECES):
                    mm = e.matmul(ps[0:w, BANK_G, j * P:(j + 1) * P], W1[:, c:c + w], ynT[:, m, :],
                                  start=True, stop=True)
                mm.then_inc(a_mm.sem, 1)
            if eng == "vector":
                a_mm.at(e, n)
                g_ev.at(e, n)
                f_mm.at(e, n - 1)
                for j, (c, w) in enumerate(PIECES):
                    ins = e.scalar_tensor_tensor(gT[0:w, j, :], ps[0:w, BANK_G, j * P:(j + 1) * P],
                                                 b1[0:w, j, ds(layer(n), 1)], gl[0:w, j, :], ALU.add, ALU.mult)
                ins.then_inc(a_ev.sem, 1)

        def down(eng, e, n, m):
            if eng == "tensor":
                a_ev.at(e, n)
                w_2.at(e, layer(n))
                for j, (c, w) in enumerate(PIECES):
                    mm = e.matmul(ps[:, BANK_G, 0:E], gT[0:w, j, :], W2[0:w, j, :], start=(j == 0), stop=(j == 2))
                mm.then_inc(f_mm.sem, 1)
            if eng == "vector":
                f_mm.at(e, n)
                yb_ev.at(e, n)
                if not isinstance(n, int) or n < TILES - 1:
                    sh_mm.at(e, n + 1)
                e.tensor_tensor(X[:, ds(slot(n % NT), 1), :], ps[:, BANK_G, 0:E], yb[:, m, :], ALU.add)\
                    .then_inc(x_ev.sem, 1)

        JOBS = {"carry": carry, "tables": tables, "shift_in": shift_in, "turn_in": turn_in, "norms": norms,
                "scale_q": scale_q, "project": project, "shift_y": shift_y, "residual": residual,
                "statistics": statistics, "normalize": normalize, "turn_y": turn_y, "gate": gate,
                "gated": gated, "down": down}
        for kind, count in ((qkv, 6), (swap, 2), (straight, 2), (rotated, 2), (turn_qk, 4), (scores, 8),
                            (over_sum, 4), (turn_p, 4), (values, 2)):
            for c in range(count):
                JOBS[f"{kind.__name__}{c}"] = kind(c)

        def tile(eng, e, g, place, first=0, end=TILES):
            for name, lag in ORDER[eng]:
                if isinstance(g, int) and not first <= g - lag < end:
                    continue
                JOBS[name](eng, e, g - lag, (place - lag) % RING)

        def tiles(eng, e):
            for g in range(RING):
                tile(eng, e, g, g)
            with e.Fori(1, TILES // RING) as turn:
                for place in range(RING):
                    tile(eng, e, turn * RING + place, place)
            for g in range(TILES, TILES + RING):
                tile(eng, e, g, g)

        N_IN = 11

        @block.sync
        def _(e):
            def small(l):
                e.dma_start(Wo[:], a["L0_ffn_Wo"][l].rearrange("(c p) d -> p c d", p=P)).then_inc(w_o.sem, 16)
            def qkv_in(l):
                e.dma_start(Wqkv[:, ds(l % 2, 1), :], a["L0_ffn_Wqkv"][ds(l, 1)].rearrange("l p n -> p l n"))\
                    .then_inc(w_qkv.sem, 16)
            def o_in(l):
                e.dma_start(Wo[:], a["L0_ffn_Wo"][ds(l, 1)].rearrange("l (c p) d -> p (l c) d", p=P))\
                    .then_inc(w_o.sem, 16)
            def w1_in(l):
                e.dma_start(W1[:], a["L0_ffn_W1"][ds(l, 1)].rearrange("l p n -> p (l n)")).then_inc(w_1.sem, 16)
            def w2_in(l):
                w2 = a["L0_ffn_W2"][ds(l, 1)]
                e.dma_start(W2[:, 0:2, :], w2[:, 0:2 * P, :].rearrange("l (c p) d -> p (l c) d", p=P))\
                    .then_inc(w_2.sem, 16)
                e.dma_start(W2[0:HID - 2 * P, 2, :], w2[:, 2 * P:HID, :].rearrange("l p d -> p (l d)"))\
                    .then_inc(w_2.sem, 16)
            qkv_in(0)
            e.dma_start(rot[:], a["c_rot"]).then_inc(s_in, 16)
            e.dma_start(scales[:], a["scales"].partition_broadcast(P)).then_inc(s_in, 16)
            e.dma_start(b2[:], a["L0_ffn_b2"].partition_broadcast(P)).then_inc(s_in, 16)
            for dst, src in ((lng, "lngT"), (lnb, "lnbT"), (b1, "b1T"), (shift, "c_shift"), (last, "c_last"),
                             (begins, "c_begins"), (mask32, "c_mask")):
                e.dma_start(dst[:], a[src]).then_inc(s_in, 16)
            e.dma_start(sq[:, 0, 0:P], a["c_ident"]).then_inc(s_in, 16)
            o_in(0)
            w1_in(0)
            w2_in(0)
            qkv_in(1)

            def refill(l):
                wo_mm.at(e, l * NT - 1)
                o_in(l)
                a_mm.at(e, l * NT - 1)
                w1_in(l)
                f_mm.at(e, l * NT - 1)
                w2_in(l)
            with e.Fori(1, DEPTH - 1) as l:
                refill(l)
                qkv_in(l + 1)
            refill(DEPTH - 1)

        @block.gpsimd
        def _(e):
            xl_ev.open(e)
            rc_ev[0].open(e)
            rt_ev.open(e)
            kn_ev.open(e)
            yl_ev.open(e)
            yb_ev.open(e)
            rn_ev.open(e)
            for b in range(B):
                e.memset(Y[:, b * ZERO_SLOT, :], 0.0)
            ln.open(e)
            e.memset(power[:], -0.5)
            e.memset(pTp[:].rearrange("p a b -> p (a b)"), 0.0)
            e.memset(qT[:].rearrange("p a b c -> p (a b c)"), 0.0)
            e.memset(kT[:].rearrange("p r a b -> p (r a b)"), 0.0)
            e.memset(v[:].rearrange("p a b -> p (a b)"), 0.0).then_inc(s_set, 1)
            e.wait_ge(s_in, 16 * N_IN)
            e.wait_ge(s_set, 1)
            tiles("gpsimd", e)

        @block.vector
        def _(e):
            for ev in (x_ev, q_ss, rq_ev, rc_ev[1], rsw_ev, m_ev, pt_ev, pp_ev, y_ev, yn_ev, a_ev, nm_ev):
                ev.open(e)
            e.wait_ge(s_in, 16 * N_IN)
            e.tensor_copy(mask[:, 0, :], mask32[:, 0, :])
            for i in range(1, TB):
                e.tensor_copy(mask[:, i, :], mask32[:, 1, :])
            e.tensor_copy(identb[:], sq[:, 0, 0:P]).then_inc(s_mask, 1)
            e.wait_ge(s_mask, 1)
            e.wait_ge(s_set, 1)
            tiles("vector", e)

        @block.scalar
        def _(e):
            for ev in (sh_ev, xT_ev, q_ev, q_sq, T_ev, e_ev, oT_ev, s2_ev, nT_ev, g_ev):
                ev.open(e)
            e.wait_ge(s_in, 16 * N_IN)
            e.wait_ge(s_set, 1)
            e.wait_ge(s_mask, 1)
            tiles("scalar", e)

        @block.tensor
        def _(e):
            for ev in (xT_mm, q_mm, T_mm, S_mm, pt_mm, pv_mm, wo_mm, s2_mm, nT_mm, g_mm, a_mm, f_mm):
                ev.open(e)
            e.wait_ge(s_in, 16 * N_IN)
            e.wait_ge(s_set, 1)
            e.wait_ge(s_mask, 1)
            tiles("tensor", e)


def last_output(nc, X, X2, out):
    STEPS = NT // G
    with Part(nc, "fi") as t:
        yn, res = t.sb("yn", [P, G, E]), t.sb("res", [P, 2, G, E])
        yn_ev, res_ev = t.ev("yn"), t.ev("re", 1, 1)
        sent = [t.ev(f"sent{u}", 16, 1) for u in range(2)]
        ln = LayerNorm(t, "ln", G)
        block = t.block()
        rows = out.rearrange("b (t p) d -> p (b t) d", p=P)

        @block.vector
        def _(e):
            res_ev.open(e)
            with e.Fori(0, STEPS // 2) as pair:
                for u in range(2):
                    i = pair * 2 + u
                    first = i * G + i // (TB // G) + 1
                    ln.chain.start(e, i)
                    xs = [X[:, ds(first + g, 1), :] for g in range(G)]
                    ln.stats(e, xs)
                    ln.apply(e, xs, [yn[:, g, :] for g in range(G)], i).then_inc(yn_ev.sem, 1)
                    yn_ev.at(e, i)
                    sent[u].at(e, pair - 1)
                    e.tensor_tensor(res[:, u, :, :], X2[:, ds(i * G, G), :], yn[:], ALU.add)\
                        .then_inc(res_ev.sem, 1)

        @block.gpsimd
        def _(e):
            ln.open(e)
            with e.Fori(0, STEPS) as i:
                ln.rstd(e, G, i)

        @block.sync
        def _(e):
            for u in range(2):
                sent[u].open(e)
            with e.Fori(0, STEPS // 2) as pair:
                for u in range(2):
                    i = pair * 2 + u
                    res_ev.at(e, i)
                    e.dma_start(rows[:, ds(i * G, G), :], res[:, u, :, :]).then_inc(sent[u].sem, 16)
            for u in range(2):
                sent[u].at(e, STEPS // 2 - 1)


def constants():
    r = np.arange(P)
    half = np.arange(0, D, 2, dtype=np.float32)
    inv_freq = (1.0 / np.float32(10000.0) ** (half / np.float32(D))).astype(np.float32)
    pos = np.arange(S, dtype=np.float32)
    freqs = pos[:, None] * inv_freq[None, :]
    base = (half + np.float32(0.4 * D)) / np.float32(1.4 * D)
    scale = base[None, :] ** ((pos - S // 2) / np.float32(WIN // 2))[:, None]
    cos, sin = np.cos(freqs), np.sin(freqs)
    tabs = []
    for s in (scale, 1.0 / scale):
        tabs += [np.concatenate([cos * s, cos * s], 1), np.concatenate([-sin * s, sin * s], 1)]
    rot = np.stack(tabs, 1).astype(np.float32)
    q, k = WIN + r[:, None], np.arange(KW)[None, :]
    seen = (k <= q) & (q - k <= WIN) & (k // WIN >= q // WIN - 1)
    masks = np.where(np.stack([seen & (k >= WIN), seen], 1), 0.0, NEG).astype(np.float32)
    begins = np.ones((P, TB), np.float32)
    begins[:, 0] = 0.0
    sel = np.zeros((P, D_A + 1), np.float32)
    for c in range(G):
        sel[WIN * c + np.arange(D_A + 1), np.arange(D_A + 1)] = 1.0
    return {
        "c_ident": np.eye(P, dtype=np.float32),
        "c_shift": np.eye(P, k=1, dtype=np.float32),
        "c_last": ((r[:, None] == P - 1) & (r[None, :] == 0)).astype(np.float32),
        "c_rot": np.ascontiguousarray(rot.reshape(TB, P, 4 * D).transpose(1, 0, 2)),
        "c_mask": np.ascontiguousarray(masks), "c_begins": begins, "c_sel": sel,
    }


_INS = ["L0_attn_x", "L0_attn_Wq", "L0_attn_bq", "L0_attn_Wk", "L0_attn_bk", "L0_attn_Wv", "L0_attn_bv",
        "L0_attn_Wo", "L0_attn_bo", "L0_ffn_Wqkv", "L0_ffn_Wo", "L0_ffn_W1", "L0_ffn_W2", "L0_ffn_b2"]


def layout(x):
    arrays = {n: np.ascontiguousarray(x[n]) for n in _INS}
    rel = np.asarray(x["L0_attn_rel_key"])
    arrays["relT"] = np.ascontiguousarray(rel.T)
    arrays["rel0"] = np.ascontiguousarray(np.tile(rel[0], H_A))
    qs, ks = np.asarray(x["L0_ffn_q_scale"]), np.asarray(x["L0_ffn_k_scale"])
    swap = lambda s: np.concatenate([s[:, D // 2:], s[:, :D // 2]], 1)
    arrays["scales"] = np.ascontiguousarray(np.concatenate([qs, swap(qs), ks, swap(ks)], 1))
    arrays["lngT"] = np.ascontiguousarray(np.asarray(x["L0_ffn_ln_g"]).T)
    arrays["lnbT"] = np.ascontiguousarray(np.asarray(x["L0_ffn_ln_b"]).T)
    b1 = np.asarray(x["L0_ffn_b1"])
    b1t = np.zeros((P, 2 * len(PIECES), DEPTH), b1.dtype)
    for half in range(2):
        for j, (c, w) in enumerate(PIECES):
            b1t[0:w, half * len(PIECES) + j, :] = b1[:, half * HID + c:half * HID + c + w].T
    arrays["b1T"] = b1t
    arrays.update(constants())
    return arrays


def kernel(**inputs):
    import concourse.bacc as bacc
    from concourse.bass_utils import run_bass_kernel_spmd

    nc = bacc.Bacc("TRN2", target_bir_lowering=False, num_devices=1)
    arrays = layout(inputs)
    aps = {n: nc.dram_tensor(f"in_{n}", v.shape, mybir.dt.from_np(v.dtype), kind="ExternalInput").ap()
           for n, v in arrays.items()}
    out = nc.dram_tensor("out", (B, S, E), F32, kind="ExternalOutput").ap()
    build(nc, aps, out)
    r = run_bass_kernel_spmd(nc, [{f"in_{n}": v for n, v in arrays.items()}], core_ids=[0])
    return r.results[0]["out"]
```

```python
from contextlib import ExitStack

import concourse.bass as bass
import numpy as np
from concourse import mybir

F32 = mybir.dt.float32
BF16 = mybir.dt.bfloat16
ALU = mybir.AluOpType
ACT = mybir.ActivationFunctionType
AX = mybir.AxisListType
ds = bass.ds

P = 128
B, S, E = 4, 1024, 128
NT = B * S // P
TB = S // P
SLOTS = B * (TB + 1)
G = 4
H_A, D_A, REL = 16, 8, 256
BAND = 3 * P
HEADS_A = B * H_A
PARTS = 3
KP = PARTS * PARTS * D_A
RING_A = 4
SC_A = D_A ** -0.5
H, D = 16, 64
INNER = H * D
DEPTH, WIN = 6, 32
HID = 341
PIECES = [(c, min(P, HID - c)) for c in range(0, HID, P)]
KW = WIN + P
QK_SCALE = 8.0
NEG = -1e30
EPS = 1e-5
TILES = DEPTH * NT
ZERO_SLOT = TB + 1
RING = 3

ORDER_A = {
    "tensor": [("bands1", 1), ("rows0", 2), ("gather1", 4), ("turn1", 3), ("turn2", 3),
              ("values0", 3), ("turn3", 3), ("values1", 3), ("rows1", 2), ("bands2", 1),
              ("rows2", 2), ("values2", 3), ("values3", 3), ("turn4", 3), ("bands3", 1),
              ("gather0", 3), ("rows3", 2), ("turn5", 3), ("turn6", 3), ("rows4", 2), ("values4", 3),
              ("turn7", 3), ("values5", 3), ("rows5", 2), ("values6", 3), ("turn8", 3), ("turn9", 3),
              ("bands0", 0), ("values7", 3), ("rows6", 2), ("turn10", 3), ("values8", 3),
              ("turn11", 3), ("values9", 3), ("values10", 3), ("values11", 3), ("rows7", 2),
              ("turn0", 2)],
    "vector": [("drain1", 4), ("rows7", 3), ("gather1", 4), ("turn1", 3), ("rows0", 2), ("turn3", 3),
              ("rows1", 2), ("drain0", 3), ("rows2", 2), ("gather0", 3), ("rows3", 2), ("turn5", 3),
              ("rows4", 2), ("turn7", 3), ("rows5", 2), ("turn9", 3), ("rows6", 2), ("turn11", 3)],
    "scalar": [("turn0", 3), ("bands1", 1), ("rows7", 3), ("rows0", 2), ("turn2", 3), ("bands2", 1),
              ("rows1", 2), ("turn4", 3), ("bands3", 1), ("rows2", 2), ("rows3", 2), ("turn6", 3),
              ("rows4", 2), ("turn8", 3), ("bands0", 0), ("rows5", 2), ("turn10", 3), ("rows6", 2)],
    "gpsimd": [("values_in", 0)],
    "sync": [("load", 0), ("store", 1), ("fetch", 1)],
}

ORDER = {
    "tensor": [("shift_in", 0), ("scores5", 2), ("scores6", 2), ("turn_in", 0), ("turn_qk0", 1),
              ("shift_y", 3), ("turn_p1", 2), ("qkv0", 0), ("qkv1", 0), ("scores7", 2),
              ("turn_qk1", 1), ("values0", 2), ("scores0", 1), ("turn_qk2", 1), ("qkv2", 0),
              ("scores1", 1), ("turn_y", 3), ("turn_p2", 2), ("scores2", 1), ("qkv3", 0),
              ("qkv4", 0), ("turn_p3", 2), ("turn_qk3", 1), ("gate", 3), ("qkv5", 0), ("scores3", 1),
              ("values1", 2), ("scores4", 1), ("gated", 3), ("project", 2), ("turn_p0", 1),
              ("down", 3)],
    "vector": [("over_sum1", 2), ("scores5", 2), ("scale_q", 1), ("scores6", 2), ("statistics", 3),
              ("turn_p1", 2), ("over_sum2", 2), ("scores7", 2), ("qkv0", 0), ("normalize", 3),
              ("scores0", 1), ("over_sum3", 2), ("qkv1", 0), ("scores1", 1), ("turn_p2", 2),
              ("scores2", 1), ("swap0", 0), ("qkv2", 0), ("turn_p3", 2), ("qkv3", 0), ("norms", 0),
              ("swap1", 0), ("scores3", 1), ("over_sum0", 1), ("scores4", 1), ("gated", 3),
              ("straight1", 0), ("project", 2), ("turn_p0", 1), ("down", 3)],
    "scalar": [("scores4", 2), ("shift_in", 0), ("turn_in", 0), ("turn_qk0", 1), ("shift_y", 3),
              ("scores5", 2), ("qkv0", 0), ("scores6", 2), ("turn_qk1", 1), ("values0", 2),
              ("scores7", 2), ("qkv1", 0), ("scores0", 1), ("turn_y", 3), ("qkv2", 0),
              ("turn_qk2", 1), ("qkv3", 0), ("scores1", 1), ("scores2", 1), ("turn_qk3", 1),
              ("gate", 3), ("values1", 2), ("scores3", 1), ("qkv4", 0), ("qkv5", 0)],
    "gpsimd": [("straight0", 1), ("tables", 0), ("shift_in", 0), ("rotated0", 1), ("norms", 1),
              ("shift_y", 3), ("rotated1", 1), ("residual", 3), ("statistics", 3), ("carry", 1)],
}


def slot(m):
    return m + m // TB + 1


class Event:

    def __init__(self, sem, per=1, credit=0):
        self.sem, self.per, self.credit = sem, per, credit

    def open(self, eng):
        eng.sem_inc(self.sem, self.per * self.credit)

    def at(self, eng, n, k=None):
        v = self.per * (n + self.credit) + (self.per if k is None else k)
        if isinstance(v, int) and v <= self.per * self.credit:
            return
        eng.wait_ge(self.sem, v)


class Chain(Event):

    def start(self, eng, n, k=0):
        self.eng, self.n, self.k = eng, n, k

    def link(self, ins):
        self.k += 1
        assert self.k <= self.per
        ins.then_inc(self.sem, 1)
        self.at(self.eng, self.n, self.k)


def step_in(dve, cell):
    dve.memset(cell, 0.0)


class LayerNorm:

    def __init__(self, part, name, n, per=1):
        self.st = part.sb(name + "_stats", [P, n, 9])
        self.power = part.sb(name + "_power", [P, n, 1])
        self.power_ev = part.ev(name + "_power_ev")
        self.cell = part.sb(name + "_cell", [P, 1])
        self.chain = part.chain(name + "_chain", 2 * per)
        self.stats_ev, self.rstd_ev = part.ev(name + "_stats_ev", per), part.ev(name + "_rstd_ev", per)

    def open(self, pool):
        pool.memset(self.power[:], -0.5).then_inc(self.power_ev.sem, 1)
        self.power_ev.at(pool, 0)

    def stats(self, dve, xs):
        step_in(dve, self.cell[:])
        for j, x in enumerate(xs):
            ins = dve.bn_stats(self.st[:, j, 0:6], x)
        self.chain.link(ins)
        step_in(dve, self.cell[:])
        for j in range(len(xs)):
            ins = dve.bn_aggr(self.st[:, j, 6:8], self.st[:, j, 0:6])
        self.chain.link(ins)
        n = len(xs)
        dve.tensor_scalar(self.st[:, 0:n, 7:8], self.st[:, 0:n, 7:8], EPS, None, ALU.add)\
            .then_inc(self.stats_ev.sem, 1)

    def rstd(self, pool, n, step, k=None):
        self.stats_ev.at(pool, step, k)
        pool.tensor_tensor(self.st[:, 0:n, 8:9], self.st[:, 0:n, 7:8], self.power[:, 0:n, :], ALU.pow)\
            .then_inc(self.rstd_ev.sem, 1)

    def apply(self, dve, xs, outs, step, k=None):
        self.rstd_ev.at(dve, step, k)
        for j, x in enumerate(xs):
            ins = dve.tensor_scalar(outs[j], x, self.st[:, j, 6:7], self.st[:, j, 8:9],
                                    ALU.subtract, ALU.mult)
        return ins


def wide(ap, n):
    return ap.unsqueeze(2).to_broadcast([ap.shape[0], ap.shape[1], n])


def over(ap, n):
    return ap.unsqueeze(1).to_broadcast([ap.shape[0], n, ap.shape[1]])


def rounds(eng, e, order, jobs, count, ring):
    def one(g, place):
        for name, lag in order[eng]:
            if isinstance(g, int) and not 0 <= g - lag < count:
                continue
            jobs[name](eng, e, g - lag, (place - lag) % ring)
    for g in range(ring):
        one(g, g)
    with e.Fori(1, count // ring) as turn:
        for place in range(ring):
            one(turn * ring + place, place)
    for g in range(count, count + max(lag for _, lag in order[eng])):
        one(g, g % ring)


class Part:

    def __init__(self, nc, name):
        self.nc, self.name, self.ctx = nc, name, ExitStack()

    def __enter__(self):
        self.ctx.__enter__()
        return self

    def __exit__(self, *a):
        return self.ctx.__exit__(*a)

    def sb(self, name, shape, dt=F32):
        return self.ctx.enter_context(self.nc.sbuf_tensor(f"{self.name}_{name}", shape, dt))

    def psum(self):
        return self.ctx.enter_context(self.nc.psum_tensor(f"{self.name}_ps", [P, 8, 512], F32))

    def sem(self, name):
        return self.ctx.enter_context(self.nc.semaphore(f"{self.name}_{name}"))

    def ev(self, name, per=1, credit=0):
        return Event(self.sem(name), per, credit)

    def chain(self, name, per):
        return Chain(self.sem(name), per)

    def block(self):
        return self.ctx.enter_context(self.nc.Block())


def build(nc, a, out):
    qt_d = nc.dram_tensor("qt_scratch", [PARTS, PARTS, P, B * S], BF16).ap()
    kt_d = nc.dram_tensor("kt_scratch", [PARTS, PARTS, P, B * S], BF16).ap()
    rel_d = nc.dram_tensor("rel_scratch", [PARTS, D_A, REL], BF16).ap()
    skew = nc.dram_tensor("skew_scratch", [2, TB, P * BAND], F32).ap()
    with ExitStack() as top:
        X = top.enter_context(nc.sbuf_tensor("X", [P, SLOTS, E], F32))
        X2 = top.enter_context(nc.sbuf_tensor("X2", [P, NT, E], F32))
        ident = top.enter_context(nc.sbuf_tensor("ident", [P, P], F32))
        with nc.sbuf_tensor("V", [P, NT, E], F32) as V:
            first_projections(nc, a, X, V, ident, qt_d, kt_d, rel_d, skew)
            first_attention(nc, a, V, X2, ident, qt_d, kt_d, rel_d, skew)
        first_output(nc, a, X, X2, ident)
        layers(nc, a, X, ident)
        last_output(nc, X, X2, out)


def first_projections(nc, a, X, V, ident, qt_d, kt_d, rel_d, skew):
    STEPS = NT // G
    with Part(nc, "pr") as t:
        Wq, Wk, Wv, bv = (t.sb(n, [P, E]) for n in ("Wq", "Wk", "Wv", "bv"))
        bq, bk, r0, bkr = (t.sb(n, [P, 1]) for n in ("bq", "bk", "r0", "bkr"))
        fill = t.sb("fill", [P, BAND])
        xh, xhT = t.sb("xh", [P, G, E]), t.sb("xhT", [P, G * P])
        qf, kf = t.sb("qf", [P, G * P]), t.sb("kf", [P, G * P])
        q3, k3 = t.sb("q3", [P, PARTS, G * P], BF16), t.sb("k3", [P, PARTS, G * P], BF16)
        relT, relD, rel3 = t.sb("relT", [D_A, REL]), t.sb("relD", [D_A, REL]), t.sb("rel3", [D_A, PARTS, REL], BF16)
        ps = t.psum()
        s_in, s_z, s_f, s_sk, s_bk = (t.sem(n) for n in ("in", "z", "f", "sk", "bk"))
        ln = LayerNorm(t, "ln", G)
        xh_done, t_mm, xhT_done = t.ev("xh"), t.ev("t", 1, 1), t.ev("xhT", 1, 1)
        q_mm, k_mm, v_mm = t.ev("qm"), t.ev("km"), t.ev("vm", 1, 1)
        q_ev, k_ev, v_ev = (t.ev(n, 1, 1) for n in ("qe", "ke", "ve"))
        q3_ev, k3_ev, rel3_ev = t.ev("q3", 1, 1), t.ev("k3"), t.ev("r3")
        q_out, k_out, rel_out = t.ev("qo", 16 * PARTS, 1), t.ev("ko", 16 * PARTS, 1), t.ev("ro", 16)
        c_q, c_k, c_rel = (t.chain(n, 2 * PARTS - 2) for n in ("cq", "ck", "cr"))
        block = t.block()

        def split(dve, chain, step, x, parts, done):
            chain.start(dve, step)
            for p in range(PARTS - 1):
                chain.link(dve.tensor_copy(parts[:, p, :], x))
                chain.link(dve.tensor_tensor(x, x, parts[:, p, :], ALU.subtract))
            dve.tensor_copy(parts[:, PARTS - 1, :], x).then_inc(done.sem, 1)

        def tiles_of(i):
            first = i * G + i // (TB // G) + 1
            return [X[:, ds(first + g, 1), :] for g in range(G)]

        def stats(eng, e, i, m):
            if eng == "vector":
                ln.chain.start(e, i)
                ln.stats(e, tiles_of(i))
            if eng == "gpsimd":
                ln.rstd(e, G, i)

        def turn(eng, e, i, m):
            if eng == "vector":
                t_mm.at(e, i - 1)
                ln.apply(e, tiles_of(i), [xh[:, g, :] for g in range(G)], i).then_inc(xh_done.sem, 1)
            if eng == "tensor":
                xh_done.at(e, i)
                xhT_done.at(e, i - 1)
                for g in range(G):
                    mm = e.transpose(ps[:, 0, g * P:(g + 1) * P], xh[:, g, :], ident[:])
                mm.then_inc(t_mm.sem, 1)
            if eng == "scalar":
                t_mm.at(e, i)
                v_mm.at(e, i - 1)
                e.activation(xhT[:], ps[:, 0, :], ACT.Copy).then_inc(xhT_done.sem, 1)

        def project(eng, e, i, m):
            if eng == "tensor":
                xhT_done.at(e, i)
                q_ev.at(e, i - 1)
                e.matmul(ps[:, 1, :], Wq[:], xhT[:], start=True, stop=True).then_inc(q_mm.sem, 1)
                k_ev.at(e, i - 1)
                e.matmul(ps[:, 2, :], Wk[:], xhT[:], start=True, stop=True).then_inc(k_mm.sem, 1)
                v_ev.at(e, i - 1)
                for g in range(G):
                    mm = e.matmul(ps[:, 3, g * P:(g + 1) * P], xhT[:, g * P:(g + 1) * P], Wv[:],
                                  start=True, stop=True)
                mm.then_inc(v_mm.sem, 1)
            if eng == "scalar":
                q_mm.at(e, i)
                q3_ev.at(e, i - 1)
                e.activation(qf[:], ps[:, 1, :], ACT.Identity, bias=bq[:, 0:1]).then_inc(q_ev.sem, 1)
            if eng == "vector":
                k_mm.at(e, i)
                e.tensor_scalar(kf[:], ps[:, 2, :], bkr[:, 0:1], None, ALU.add).then_inc(k_ev.sem, 1)
                v_mm.at(e, i)
                e.tensor_tensor(V[:, ds(i * G, G), :], ps[:, 3, :].rearrange("p (g d) -> p g d", g=G),
                                over(bv[:], G), ALU.add).then_inc(v_ev.sem, 1)

        def parts(eng, e, i, m):
            cols = ds(i * (G * P), G * P)
            if eng == "vector":
                k_ev.at(e, i)
                k_out.at(e, i - 1)
                split(e, c_k, i, kf[:], k3, k3_ev)
                q_ev.at(e, i)
                q_out.at(e, i - 1)
                split(e, c_q, i, qf[:], q3, q3_ev)
            if eng == "sync":
                k3_ev.at(e, i)
                for p in range(PARTS):
                    e.dma_start(kt_d[p, :, :, cols].rearrange("a p c -> p a c"), k3[:]).then_inc(k_out.sem, 16)
                q3_ev.at(e, i)
                for p in range(PARTS):
                    e.dma_start(qt_d[:, p, :, cols].rearrange("a p c -> p a c"), q3[:]).then_inc(q_out.sem, 16)

        JOBS = {"stats": stats, "turn": turn, "project": project, "parts": parts}
        order = {"sync": [("parts", 2)], "gpsimd": [("stats", 0)], "tensor": [("turn", 1), ("project", 1)],
                 "scalar": [("turn", 1), ("project", 1)],
                 "vector": [("turn", 1), ("stats", 0), ("parts", 2), ("project", 1)]}

        def steps(eng, e):
            rounds(eng, e, order, JOBS, STEPS, 2)

        @block.sync
        def _(e):
            for b in range(B):
                e.dma_start(X[:, b * (TB + 1) + 1:(b + 1) * (TB + 1), :],
                            a["L0_attn_x"][b].rearrange("(t p) d -> p t d", p=P)).then_inc(s_in, 16)
            for dst, src in ((Wq, "L0_attn_Wq"), (Wk, "L0_attn_Wk"), (Wv, "L0_attn_Wv"), (ident, "c_ident")):
                e.dma_start(dst[:], a[src]).then_inc(s_in, 16)
            for dst, src in ((bq, "L0_attn_bq"), (bk, "L0_attn_bk"), (r0, "rel0")):
                e.dma_start(dst[:], a[src].rearrange("(p o) -> p o", o=1)).then_inc(s_in, 16)
            e.dma_start(bv[:], a["L0_attn_bv"].partition_broadcast(P)).then_inc(s_in, 16)
            e.dma_start(relT[:], a["relT"]).then_inc(s_in, 16)
            rel3_ev.at(e, 0)
            e.dma_start(rel_d.rearrange("a p c -> p a c"), rel3[:]).then_inc(rel_out.sem, 16)
            e.wait_ge(s_f, 2)
            for par in range(2):
                for i in range(TB):
                    e.dma_start(skew[par, i].rearrange("(p c) -> p c", c=BAND), fill[:]).then_inc(s_sk, 16)
            steps("sync", e)
            e.wait_ge(s_sk, 16 * 2 * TB)
            q_out.at(e, STEPS - 1)
            k_out.at(e, STEPS - 1)
            rel_out.at(e, 0)

        @block.gpsimd
        def _(e):
            for b in range(B):
                e.memset(X[:, b * ZERO_SLOT, :], 0.0).then_inc(s_z, 1)
            e.memset(fill[:], 0.0).then_inc(s_f, 1)
            e.wait_ge(s_f, 1)
            e.affine_select(out=fill[:], in_=fill[:], compare_op=ALU.is_ge, fill=NEG, base=REL,
                            pattern=[[-1, BAND]], channel_multiplier=1).then_inc(s_f, 1)
            ln.open(e)
            steps("gpsimd", e)

        @block.vector
        def _(e):
            v_ev.open(e)
            k_ev.open(e)
            k_out.open(e)
            q_out.open(e)
            q3_ev.open(e)
            e.wait_ge(s_in, 16 * 13)
            e.tensor_tensor(bkr[:], bk[:], r0[:], ALU.add).then_inc(s_bk, 1)
            e.wait_ge(s_bk, 1)
            e.tensor_scalar(relD[:], relT[:], relT[:, 0:1], None, ALU.subtract).then_inc(s_bk, 1)
            e.wait_ge(s_bk, 2)
            split(e, c_rel, 0, relD[:], rel3, rel3_ev)
            steps("vector", e)

        @block.scalar
        def _(e):
            xhT_done.open(e)
            q_ev.open(e)
            e.wait_ge(s_in, 16 * 13)
            steps("scalar", e)

        @block.tensor
        def _(e):
            t_mm.open(e)
            v_mm.open(e)
            e.wait_ge(s_in, 16 * 13)
            steps("tensor", e)


def first_attention(nc, a, V, O, ident, qt_d, kt_d, rel_d, skew):
    JJ = TB // G
    NJ = sum(G * (u + 1) for u in range(JJ))
    with Part(nc, "at") as t:
        qh, kh = t.sb("qh", [KP, RING_A, S], BF16), t.sb("kh", [KP, RING_A, S], BF16)
        relD = t.sb("relD", [KP, REL], BF16)
        vh = t.sb("vh", [P, RING_A, TB, WIN])
        R = t.sb("R", [P, 2, TB, REL])
        band = t.sb("band", [P, 2, TB, BAND])
        summed = t.sb("summed", [P, 2, BAND])
        mx, nb = t.sb("mx", [P, 2 * TB]), t.sb("nb", [P, TB])
        probs = [t.sb(f"probs{u}", [P, 2, G, G * P * (u + 1)]) for u in range(JJ)]
        pT = t.sb("pT", [P, 2, G * P])
        part, sel = t.sb("part", [P, G * P]), t.sb("sel", [P, D_A + 1])
        rc, cell = t.sb("rc", [P, G]), t.sb("cell", [P, 1])
        ps = t.psum()
        s_in, s_set, s_zero = t.sem("in"), t.sem("set"), t.sem("zero")
        qk_in = [t.ev(f"qkin{u}", 32) for u in range(2)]
        vh_ev = t.ev("vh")
        r_mm, r_ev = t.ev("rm", TB // 2), t.ev("re", TB // 2, 1)
        r_out, r_in = [[t.ev(f"{n}{u}", 16, 1) for u in range(2)] for n in ("ro", "ri")]
        s_mm = t.ev("sm", TB, RING_A)
        nb_ev = t.ev("nb", TB, 2)
        p_ev = t.ev("pe", TB, 1)
        t_mm = t.ev("tm", NJ, 2)
        tA, tD = t.ev("tA", NJ // 2, 1), t.ev("tD", NJ // 2, 1)
        pv_mm = t.ev("pv", NJ, RING_A)
        o_ev, g_mm, on = t.ev("oe", JJ), t.ev("gm", JJ, 1), t.ev("on", JJ, 1)
        c_max = t.chain("cm", TB)
        c_on = t.chain("co", JJ)
        block = t.block()
        R_BANK, T_BANKS, O_BANK = 0, (1, 6), 7

        def width(i):
            return P * (i + 1)

        def far(i):
            return P * max(0, i + 1 - BAND // P)

        def logits(i):
            lo = 2 + 2 * (i % 2)
            return ps[:, lo:lo + 2, :].rearrange("p b n -> p (b n)")


        def load(eng, e, n, m):
            s_mm.at(e, n - RING_A)
            hd = n % HEADS_A
            row, col = ds(hd % H_A * D_A, D_A), ds(hd // H_A * S, S)
            for dst, src in ((qh, qt_d), (kh, kt_d)):
                e.dma_start(dst[:, m, :], src.rearrange("a b p c -> (a b) p c")[:, row, col])\
                    .then_inc(qk_in[m % 2].sem, 16)

        def store(eng, e, n, m):
            r_ev.at(e, n)
            r_in[m % 2].at(e, n // 2 - 1)
            flat = skew[m % 2]
            dst = bass.AP(flat.tensor, flat.offset + 1, [[BAND + 1, P], [P * BAND, TB], [1, REL]])
            e.dma_start(dst, R[:, m % 2]).then_inc(r_out[m % 2].sem, 16)

        def fetch(eng, e, n, m):
            nb_ev.at(e, n - 2)
            r_out[m % 2].at(e, n // 2)
            e.dma_start(band[:, m % 2, :, :], skew[m % 2].rearrange("t (p c) -> p t c", c=BAND))\
                .then_inc(r_in[m % 2].sem, 16)

        def bands(j):
            def job(eng, e, n, m):
                if eng == "tensor":
                    if j == 0:
                        qk_in[m % 2].at(e, n // 2)
                    r_ev.at(e, *((n, j) if j else (n - 1, TB // 2)))
                    for i in (2 * j, 2 * j + 1):
                        mm = e.matmul(ps[:, R_BANK, i % 2 * REL:(i % 2 + 1) * REL],
                                      qh[:, m, i * P:(i + 1) * P], relD[:], start=True, stop=True)
                    mm.then_inc(r_mm.sem, 1)
                if eng == "scalar":
                    r_mm.at(e, n, j + 1)
                    if j == 0:
                        r_out[m % 2].at(e, n // 2 - 1)
                    e.activation(R[:, m % 2, 2 * j:2 * j + 2, :],
                                 ps[:, R_BANK, :].rearrange("p (i n) -> p i n", i=2), ACT.Copy)\
                        .then_inc(r_ev.sem, 1)
            return job

        def rows(i):
            def job(eng, e, n, m):
                f, w = far(i), width(i)
                if eng == "tensor":
                    if i == 0:
                        qk_in[m % 2].at(e, n // 2)
                    p_ev.at(e, *((n, i - 1) if i >= 2 else (n - 1, TB + i - 1)))
                    for c in range(0, w, 512):
                        mm = e.matmul(logits(i)[:, c:min(w, c + 512)], qh[:, m, i * P:(i + 1) * P],
                                      kh[:, m, c:min(w, c + 512)], start=True, stop=True)
                    mm.then_inc(s_mm.sem, 1)
                if eng == "vector":
                    s_mm.at(e, n, i + 1)
                    c_max.start(e, n, i)
                    if i == 0:
                        r_in[m % 2].at(e, n // 2)
                    p_ev.at(e, *((n, i - 1) if i >= 2 else (n - 1, TB + i - 1)))
                    step_in(e, cell[:])
                    ins = e.tensor_tensor_reduce(
                        summed[:, i % 2, 0:w - f], logits(i)[:, f:w], band[:, m % 2, i, BAND - w + f:BAND],
                        1.0, NEG, ALU.add, ALU.max, mx[:, 2 * i:2 * i + 1])
                    if f:
                        ins = e.tensor_reduce(mx[:, 2 * i + 1:2 * i + 2], logits(i)[:, 0:f], AX.X, ALU.max)
                    c_max.link(ins)
                    e.tensor_scalar(nb[:, i:i + 1], mx[:, 2 * i:2 * i + 1],
                                    mx[:, 2 * i + 1:2 * i + 2] if f else NEG, -SC_A, ALU.max, ALU.mult)\
                        .then_inc(nb_ev.sem, 1)
                if eng == "scalar":
                    nb_ev.at(e, n, i + 1)
                    u = i // G
                    if i % G == 0:
                        t_mm.at(e, n - 2, (4, NJ)[u])
                    if f:
                        e.activation(probs[u][:, m % 2, i % G, 0:f], logits(i)[:, 0:f], ACT.Exp,
                                     bias=nb[:, i:i + 1], scale=SC_A)
                    e.activation(probs[u][:, m % 2, i % G, f:w], summed[:, i % 2, 0:w - f], ACT.Exp,
                                 bias=nb[:, i:i + 1], scale=SC_A).then_inc(p_ev.sem, 1)
            return job

        def place(jj):
            return (0, jj) if jj < G else (1, jj - G)

        def copied(jj):
            return (tA, tD)[jj % 2], jj // 2 + 1

        def turn(jj):
            u, j = place(jj)
            bank = T_BANKS[jj % 2]
            ev, k = copied(jj)
            def job(eng, e, n, m):
                if eng == "tensor":
                    if j == 0:
                        p_ev.at(e, n, G * (u + 1))
                    ev.at(e, *((n - 1, NJ // 2) if k == 1 else (n, k - 1)))
                    for i in range(max(j, G * u), G * (u + 1)):
                        mm = e.transpose(ps[:, bank, i % G * P:(i % G + 1) * P],
                                         probs[u][:, m % 2, i % G, j * P:(j + 1) * P], ident[:])
                    mm.then_inc(t_mm.sem, 1)
                if eng == ("scalar", "vector")[jj % 2]:
                    t_mm.at(e, n, jj + 1)
                    pv_mm.at(e, *((n, jj - 1) if jj >= 2 else (n - 1, NJ + jj - 1)))
                    c0 = max(0, j - G * u) * P
                    src, dst = ps[:, bank, c0:G * P], pT[:, jj % 2, c0:G * P]
                    ins = e.activation(dst, src, ACT.Copy) if jj % 2 == 0 else e.tensor_copy(dst, src)
                    ins.then_inc(ev.sem, 1)
            return job

        def values(jj):
            u, j = place(jj)
            ev, k = copied(jj)
            def job(eng, e, n, m):
                if jj == 0:
                    vh_ev.at(e, n)
                if j == 0:
                    on.at(e, *((n, u) if u else (n - 1, JJ)))
                ev.at(e, n, k)
                c, c0 = j % G, max(0, j - G * u) * P
                e.matmul(ps[WIN * c:WIN * (c + 1), O_BANK, c0:G * P], vh[:, m, j, :],
                         pT[:, jj % 2, c0:G * P], start=(j < G), stop=(j >= G * u),
                         skip_group_check=True).then_inc(pv_mm.sem, 1)
            return job

        def drain(u):
            def job(eng, e, n, m):
                pv_mm.at(e, n, G * (u + 1) * (u + 2) // 2)
                g_mm.at(e, *((n, u) if u else (n - 1, JJ)))
                e.tensor_copy(part[:], ps[:, O_BANK, :]).then_inc(o_ev.sem, 1)
            return job

        def gather(u):
            def job(eng, e, n, m):
                if eng == "tensor":
                    o_ev.at(e, n, u + 1)
                    for i in range(G):
                        k = WIN * min(G, G * u + i + 1)
                        mm = e.matmul(ps[:, O_BANK, i * (D_A + 1):(i + 1) * (D_A + 1)],
                                      part[0:k, i * P:(i + 1) * P], sel[0:k, :], start=True, stop=True)
                    mm.then_inc(g_mm.sem, 1)
                if eng == "vector":
                    g_mm.at(e, n, u + 1)
                    c_on.start(e, n, u)
                    o = ps[:, O_BANK, 0:G * (D_A + 1)].rearrange("p (i d) -> p i d", i=G)
                    c_on.link(e.reciprocal(rc[:].unsqueeze(2), o[:, :, D_A:D_A + 1]))
                    tile, col = n // H_A * TB + G * u, n % H_A * D_A
                    e.tensor_tensor(O[:, ds(tile, G), ds(col, D_A)], o[:, :, 0:D_A], wide(rc[:], D_A),
                                    ALU.mult).then_inc(on.sem, 1)
            return job

        def values_in(eng, e, n, m):
            pv_mm.at(e, n - RING_A)
            e.tensor_copy(vh[:, m, :, 0:D_A], V[:, ds(n // H_A * TB, TB), ds(n % H_A * D_A, D_A)])\
                .then_inc(vh_ev.sem, 1)

        JOBS = {"load": load, "store": store, "fetch": fetch, "values_in": values_in}
        for kind, count in ((bands, TB // 2), (rows, TB), (turn, NJ), (values, NJ), (drain, JJ), (gather, JJ)):
            for c in range(count):
                JOBS[f"{kind.__name__}{c}"] = kind(c)

        def heads(eng, e):
            rounds(eng, e, ORDER_A, JOBS, HEADS_A, RING_A)

        @block.sync
        def _(e):
            for p in range(PARTS):
                rows_p = slice(p * PARTS * D_A, (p + 1) * PARTS * D_A)
                e.dma_start(relD[rows_p, :], rel_d.rearrange("b p c -> (b p) c")).then_inc(s_in, 16)
            e.dma_start(sel[:], a["c_sel"]).then_inc(s_in, 16)
            for ev in r_out + r_in:
                ev.open(e)
            heads("sync", e)

        @block.gpsimd
        def _(e):
            e.memset(vh[:], 0.0).then_inc(s_set, 1)
            e.wait_ge(s_set, 1)
            e.memset(vh[:, :, :, D_A:D_A + 1], 1.0).then_inc(s_set, 1)
            e.wait_ge(s_set, 2)
            heads("gpsimd", e)

        @block.vector
        def _(e):
            for ev in (nb_ev, tD, on):
                ev.open(e)
            e.memset(ps[:, O_BANK, :], 0.0).then_inc(s_zero, 1)
            heads("vector", e)

        @block.scalar
        def _(e):
            for ev in (r_ev, p_ev, tA):
                ev.open(e)
            heads("scalar", e)

        @block.tensor
        def _(e):
            for ev in (s_mm, t_mm, pv_mm, g_mm):
                ev.open(e)
            e.wait_ge(s_in, 16 * (PARTS + 1))
            e.wait_ge(s_zero, 1)
            heads("tensor", e)


def first_output(nc, a, X, X2, ident):
    STEPS = NT // G
    with Part(nc, "ou") as t:
        Wo, bo = t.sb("Wo", [P, E]), t.sb("bo", [P, E])
        oc, oT = t.sb("oc", [P, G, E]), t.sb("oT", [P, G * P])
        y, yn = t.sb("y", [P, G, E]), t.sb("yn", [P, G, E])
        ps = t.psum()
        s_in = t.sem("in")
        oc_ev, t_mm, oT_ev = t.ev("oc"), t.ev("tm", 1, 1), t.ev("oT", 1, 1)
        o_mm, y_ev = t.ev("om", 1, 1), t.ev("ye", 1, 1)
        ln1, ln2 = LayerNorm(t, "ln1", G), LayerNorm(t, "ln2", G)
        ch = t.chain("ch", 2)
        block = t.block()

        def x2_tiles(i):
            return [X2[:, ds(i * G + g, 1), :] for g in range(G)]

        def project(eng, e, i, m):
            if eng == "gpsimd":
                t_mm.at(e, i - 1)
                e.tensor_copy(oc[:], X2[:, ds(i * G, G), :]).then_inc(oc_ev.sem, 1)
            if eng == "tensor":
                oc_ev.at(e, i)
                oT_ev.at(e, i - 1)
                for g in range(G):
                    mm = e.transpose(ps[:, 0, g * P:(g + 1) * P], oc[:, g, :], ident[:])
                mm.then_inc(t_mm.sem, 1)
                oT_ev.at(e, i)
                y_ev.at(e, i - 1)
                for g in range(G):
                    mm = e.matmul(ps[:, 1, g * P:(g + 1) * P], oT[:, g * P:(g + 1) * P], Wo[:],
                                  start=True, stop=True)
                mm.then_inc(o_mm.sem, 1)
            if eng == "scalar":
                t_mm.at(e, i)
                o_mm.at(e, i - 1)
                e.activation(oT[:], ps[:, 0, :], ACT.Copy).then_inc(oT_ev.sem, 1)
            if eng == "vector":
                ln1.chain.start(e, i)
                o_mm.at(e, i)
                e.tensor_tensor(y[:], ps[:, 1, :].rearrange("p (g d) -> p g d", g=G), over(bo[:], G),
                                ALU.add).then_inc(y_ev.sem, 1)
                y_ev.at(e, i)
                ln1.stats(e, [y[:, g, :] for g in range(G)])

        def rstd1(eng, e, i, m):
            ln1.rstd(e, G, i)

        def add(eng, e, i, m):
            if eng == "vector":
                first = i * G + i // (TB // G) + 1
                ch.start(e, i)
                ch.link(ln1.apply(e, [y[:, g, :] for g in range(G)], [yn[:, g, :] for g in range(G)], i))
                ch.link(e.tensor_tensor(X2[:, ds(i * G, G), :], X[:, ds(first, G), :], yn[:], ALU.add))
                ln2.chain.start(e, i)
                ln2.stats(e, x2_tiles(i))
            if eng == "gpsimd":
                ln2.rstd(e, G, i)

        def finish(eng, e, i, m):
            first = i * G + i // (TB // G) + 1
            ln2.apply(e, x2_tiles(i), [X[:, ds(first + g, 1), :] for g in range(G)], i)

        JOBS = {"project": project, "rstd1": rstd1, "add": add, "finish": finish}
        order = {"gpsimd": [("project", 0), ("add", 1), ("rstd1", 0)], "tensor": [("project", 0)],
                 "scalar": [("project", 0)], "vector": [("finish", 2), ("add", 1), ("project", 0)]}

        def steps(eng, e):
            rounds(eng, e, order, JOBS, STEPS, 2)

        @block.sync
        def _(e):
            e.dma_start(Wo[:], a["L0_attn_Wo"]).then_inc(s_in, 16)
            e.dma_start(bo[:], a["L0_attn_bo"].partition_broadcast(P)).then_inc(s_in, 16)

        @block.gpsimd
        def _(e):
            ln1.open(e)
            ln2.open(e)
            steps("gpsimd", e)

        @block.tensor
        def _(e):
            t_mm.open(e)
            o_mm.open(e)
            e.wait_ge(s_in, 32)
            steps("tensor", e)

        @block.scalar
        def _(e):
            oT_ev.open(e)
            steps("scalar", e)

        @block.vector
        def _(e):
            y_ev.open(e)
            e.wait_ge(s_in, 32)
            steps("vector", e)


def layers(nc, a, X, ident):
    with Part(nc, "la") as t:
        Y = t.sb("Y", [P, SLOTS, E])
        Wqkv = t.sb("Wqkv", [P, 2, 3 * INNER])
        Wo, W1 = t.sb("Wo", [P, H * D // P, E]), t.sb("W1", [P, 2 * HID])
        W2 = t.sb("W2", [P, len(PIECES), E])
        rot, scales = t.sb("rot", [P, TB, 4 * D]), t.sb("scales", [P, DEPTH, 4 * D])
        lng, lnb, b1 = t.sb("lng", [P, DEPTH]), t.sb("lnb", [P, DEPTH]), t.sb("b1", [P, 2 * len(PIECES), DEPTH])
        b2 = t.sb("b2", [P, DEPTH, E])
        shift, last = t.sb("shift", [P, P]), t.sb("last", [P, P])
        mask, identb, mask32 = t.sb("mask", [P, TB, KW], BF16), t.sb("identb", [P, P], BF16), t.sb("mask32", [P, 2, KW])
        begins = t.sb("begins", [P, TB])
        xs, xsT = t.sb("xs", [P, E]), t.sb("xsT", [P, RING, P])
        raw, rt, sw = t.sb("raw", [P, 2 * INNER]), t.sb("rt", [P, 2 * INNER]), t.sb("sw", [P, 2 * INNER])
        sq = t.sb("sq", [P, 2, 512])
        ssum, rn, rq = t.sb("ssum", [P, 2 * H]), t.sb("rn", [P, RING, 2 * H]), t.sb("rq", [P, RING, H])
        tab = t.sb("tab", [P, RING, 4, D])
        v = t.sb("v", [P, RING, INNER])
        qT, kT = t.sb("qT", [P, H // 2, 2, P]), t.sb("kT", [P, RING, H // 2, KW])
        rmax, nb, rs, rc = t.sb("rmax", [P, H]), t.sb("nb", [P, H]), t.sb("rs", [P, H]), t.sb("rc", [P, H])
        pr, pT, pTp = t.sb("pr", [P, H, KW]), t.sb("pT", [P, H, P]), t.sb("pTp", [P, H, WIN])
        oT, ys, yn, ynT = t.sb("oT", [P, 8, P]), t.sb("ys", [P, E]), t.sb("yn", [P, E]), t.sb("ynT", [P, RING, P])
        gl, gT, yb = t.sb("gl", [P, 3, P]), t.sb("gT", [P, 3, P]), t.sb("yb", [P, RING, E])
        ps = t.psum()

        s_in, s_tab, s_set, s_mask = t.sem("in"), t.sem("tables"), t.sem("set"), t.sem("mask")
        w_qkv, w_o, w_1, w_2 = t.ev("wq", 16), t.ev("wo", 16), t.ev("w1", 16), t.ev("w2", 32)
        x_ev = t.ev("xe", 1, NT)
        sh_mm, sh_ev, xl_ev, xT_mm, xT_ev = t.ev("shm"), t.ev("she", 1, 1), t.ev("xle", 1, 1), t.ev("xtm", 1, 1), t.ev("xte", 1, 1)
        q_mm, q_ev, q_sq, q_ss = t.ev("qm", 6, 1), t.ev("qe", 6, 1), t.ev("qsq", 4, 1), t.ev("qss", 4, 1)
        rn_ev, rq_ev = t.ev("rn", 1, 1), t.ev("rq", 1, RING)
        tab_ev, cl_ev = t.ev("tab"), t.ev("cl")
        power = t.sb("power", [P, 2 * H])
        rc_ev = [t.ev("rcq", 1, RING), t.ev("rck", 1, RING)]
        rsw_ev, rt_ev, kn_ev = t.ev("rsw", 2, RING), t.ev("rte", 2, 1), t.ev("kn", 1, 1)
        kc_ev, T_mm, T_ev = t.ev("kc"), t.ev("Tm", 4, 1), t.ev("Te", 4, 1)
        S_mm, m_ev, e_ev = t.ev("Sm", 8, RING), t.ev("me", 8, 1), t.ev("ee", 8, RING)
        pt_mm, pt_ev, pp_ev = t.ev("ptm", 4, 1), t.ev("pte", 4, 1), t.ev("ppe", 4, 1)
        nm_ev, pv_mm = t.ev("nme", 4, 1), t.ev("pv", 2, 2)
        c_nb, c_rc = t.chain("cnb", 8), t.chain("crc", 4)
        oT_ev, wo_mm, y_ev = t.ev("ote", 2, 1), t.ev("wom", 1, 1), t.ev("ye", 1, 1)
        s2_mm, s2_ev, yl_ev = t.ev("s2m", 1, 1), t.ev("s2e", 1, 1), t.ev("yle", 1, 1)
        yn_ev, nT_mm, nT_ev = t.ev("yn", 1, 1), t.ev("ntm", 1, 1), t.ev("nte", 1, 1)
        g_mm, g_ev, a_mm, a_ev, f_mm = t.ev("gm", 1, 1), t.ev("ge", 1, 1), t.ev("am", 1, RING), t.ev("ae", 1, 1), t.ev("fm", 1, 1)
        yb_ev = t.ev("yb", 1, 1)
        ln = LayerNorm(t, "ln", 1)
        block = t.block()
        BANK_T, BANK_O, BANK_G, BANK_Y = 4, 5, 6, 7

        def layer(n):
            return n // NT


        def shift_in(eng, e, n, m):
            cur = slot(n % NT)
            if eng == "tensor":
                x_ev.at(e, n - NT)
                q_ev.at(e, n - 1, 5)
                e.matmul(ps[:, 0, 0:E // 2], shift[:], X[:, ds(cur, 1), E // 2:E], start=True, stop=False)
                e.matmul(ps[:, 0, 0:E // 2], last[:], X[:, ds(cur - 1, 1), E // 2:E], start=False, stop=True)\
                    .then_inc(sh_mm.sem, 1)
            if eng == "scalar":
                sh_mm.at(e, n)
                xT_mm.at(e, n - 1)
                e.activation(xs[:, E // 2:E], ps[:, 0, 0:E // 2], ACT.Copy).then_inc(sh_ev.sem, 1)
            if eng == "gpsimd":
                x_ev.at(e, n - NT)
                xT_mm.at(e, n - 1)
                e.tensor_copy(xs[:, 0:E // 2], X[:, ds(cur, 1), 0:E // 2]).then_inc(xl_ev.sem, 1)

        def turn_in(eng, e, n, m):
            if eng == "tensor":
                sh_ev.at(e, n)
                xl_ev.at(e, n)
                q_ev.at(e, n - 1, 6)
                e.transpose(ps[:, 1, 0:P], xs[:], ident[:]).then_inc(xT_mm.sem, 1)
            if eng == "scalar":
                xT_mm.at(e, n)
                q_mm.at(e, n - 1)
                e.activation(xsT[:, m, :], ps[:, 1, 0:P], ACT.Copy).then_inc(xT_ev.sem, 1)

        def qkv(c):
            def job(eng, e, n, m):
                bank = c % 2
                if eng == "tensor":
                    if c == 0:
                        xT_ev.at(e, n)
                        w_qkv.at(e, layer(n))
                        sh_ev.at(e, n)
                    if c >= 2:
                        q_ev.at(e, n, c - 1)
                        q_sq.at(e, n, min(c - 1, 4))
                    e.matmul(ps[:, bank, :], xsT[:, m, :], Wqkv[:, ds(layer(n) % 2, 1), c * 512:(c + 1) * 512],
                             start=True, stop=True).then_inc(q_mm.sem, 1)
                if eng == "scalar":
                    q_mm.at(e, n, c + 1)
                    if c < 4:
                        if c % 2 == 0:
                            rsw_ev.at(e, n - 1, c // 2 + 1)
                            rc_ev[c // 2].at(e, n - 1)
                        e.activation(raw[:, c * 512:(c + 1) * 512], ps[:, bank, :], ACT.Copy)\
                            .then_inc(q_ev.sem, 1)
                        q_ss.at(e, *((n, c - 1) if c >= 2 else (n - 1, c + 3)))
                        e.activation(sq[:, c % 2, :], ps[:, bank, :], ACT.Square).then_inc(q_sq.sem, 1)
                    else:
                        pv_mm.at(e, n - 2)
                        e.activation(v[:, m, (c - 4) * 512:(c - 3) * 512], ps[:, bank, :], ACT.Copy)\
                            .then_inc(q_ev.sem, 1)
                if eng == "vector" and c < 4:
                    q_sq.at(e, n, c + 1)
                    if c == 0:
                        rn_ev.at(e, n - 1)
                    e.tensor_reduce(ssum[:, c * 8:(c + 1) * 8],
                                    sq[:, c % 2, :].rearrange("p (h d) -> p h d", d=D), AX.X, ALU.add)\
                        .then_inc(q_ss.sem, 1)
            return job

        def norms(eng, e, n, m):
            if eng == "vector":
                q_ss.at(e, n)
                e.tensor_scalar(ssum[:], ssum[:], 1e-24, None, ALU.max).then_inc(cl_ev.sem, 1)
            if eng == "gpsimd":
                cl_ev.at(e, n)
                rq_ev.at(e, n - RING)
                e.tensor_tensor(rn[:, m, :], ssum[:], power[:], ALU.pow).then_inc(rn_ev.sem, 1)

        def scale_q(eng, e, n, m):
            if eng == "vector":
                rn_ev.at(e, n)
                e_ev.at(e, n - RING)
                e.tensor_scalar(rq[:, m, :], rn[:, m, 0:H], QK_SCALE, None, ALU.mult).then_inc(rq_ev.sem, 1)

        def tables(eng, e, n, m):
            if eng == "gpsimd":
                rsw_ev.at(e, n - RING)
                rc_ev[1].at(e, n - RING)
                e.tensor_tensor(tab[:, m].rearrange("p f d -> p (f d)"), rot[:, ds(n % TB, 1), :],
                                scales[:, ds(layer(n), 1), :], ALU.mult).then_inc(tab_ev.sem, 1)

        def swap(w):
            def job(eng, e, n, m):
                if eng == "vector":
                    q_ev.at(e, n, 2 * w + 2)
                    tab_ev.at(e, n)
                    rt_ev.at(e, n - 1, w + 1)
                    s3 = raw[:, w * INNER:(w + 1) * INNER].rearrange("p (h t d) -> p h t d", h=H, t=2)
                    d3 = sw[:, w * INNER:(w + 1) * INNER].rearrange("p (h t d) -> p h t d", h=H, t=2)
                    for half in range(2):
                        ins = e.tensor_tensor(d3[:, :, half, :], s3[:, :, 1 - half, :],
                                              over(tab[:, m, 2 * w + 1, half * 32:(half + 1) * 32], H), ALU.mult)
                    ins.then_inc(rsw_ev.sem, 1)
            return job

        def straight(w):
            def job(eng, e, n, m):
                if eng == ("gpsimd", "vector")[w]:
                    q_ev.at(e, n, 2 * w + 2)
                    tab_ev.at(e, n)
                    T_mm.at(e, n - 1, 3 + w)
                    e.tensor_tensor(rt[:, w * INNER:(w + 1) * INNER].rearrange("p (h d) -> p h d", d=D),
                                    raw[:, w * INNER:(w + 1) * INNER].rearrange("p (h d) -> p h d", d=D),
                                    over(tab[:, m, 2 * w, :], H), ALU.mult).then_inc(rc_ev[w].sem, 1)
            return job

        def rotated(w):
            def job(eng, e, n, m):
                if eng == "gpsimd":
                    dst = rt[:, w * INNER:(w + 1) * INNER]
                    rsw_ev.at(e, n, w + 1)
                    rc_ev[w].at(e, n)
                    e.tensor_tensor(dst, dst, sw[:, w * INNER:(w + 1) * INNER], ALU.add).then_inc(rt_ev.sem, 1)
                    if w:
                        rt_ev.at(e, n, 2)
                        rn_ev.at(e, n)
                        d = dst.rearrange("p (h d) -> p h d", d=D)
                        e.tensor_tensor(d, d, wide(rn[:, m, H:2 * H], D), ALU.mult).then_inc(kn_ev.sem, 1)
            return job

        def carry(eng, e, n, m):
            if eng == "gpsimd":
                T_ev.at(e, n - 1)
                S_mm.at(e, n - RING)
                flag = begins[:, ds(n % TB, 1)].unsqueeze(2).to_broadcast([P, H // 2, WIN])
                e.tensor_tensor(kT[:, m, :, 0:WIN], kT[:, (m - 1) % RING, :, P:KW], flag, ALU.mult)\
                    .then_inc(kc_ev.sem, 1)

        def turn_qk(u):
            w, half = u % 2, u // 2
            def job(eng, e, n, m):
                if eng == "tensor":
                    kn_ev.at(e, n) if w else rt_ev.at(e, n, 1)
                    T_ev.at(e, *((n, u) if u else (n - 1, 4)))
                    for j in range(4):
                        c = w * INNER + (4 * half + j) * P
                        mm = e.transpose(ps[:, BANK_T, j * P:(j + 1) * P], rt[:, c:c + P], ident[:])
                    mm.then_inc(T_mm.sem, 1)
                if eng == "scalar":
                    T_mm.at(e, n, u + 1)
                    pairs = slice(4 * half, 4 * half + 4)
                    src = ps[:, BANK_T, :].rearrange("p (j t) -> p j t", j=4)
                    if w:
                        S_mm.at(e, n - RING)
                        e.activation(kT[:, m, pairs, WIN:KW], src, ACT.Copy).then_inc(T_ev.sem, 1)
                    else:
                        S_mm.at(e, n - 1, 4 * half + 4)
                        e.activation(qT[0:D, pairs, 0, :], src[0:D], ACT.Copy)
                        e.activation(qT[D:P, pairs, 1, :], src[D:P], ACT.Copy).then_inc(T_ev.sem, 1)
            return job

        def scores(p):
            bank = 2 + p % 2
            def job(eng, e, n, m):
                both = ps[:, bank, 0:2 * KW].rearrange("p (h k) -> p h k", h=2)
                if eng == "tensor":
                    e_ev.at(e, *((n, p - 1) if p >= 2 else (n - 1, p + 7)))
                    T_ev.at(e, n, 2 + 2 * (p // 4))
                    if p == 0:
                        kc_ev.at(e, n)
                    e.matmul(both, identb[:], mask[:, ds(n % TB, 1), :].to_broadcast([P, 2, KW]),
                             start=True, stop=True)
                    for h in range(2):
                        mm = e.matmul(both[:, h, :], qT[:, p, h, :], kT[:, m, p, :], start=False, stop=True,
                                      skip_group_check=True)
                    mm.then_inc(S_mm.sem, 1)
                if eng == "vector":
                    S_mm.at(e, n, p + 1)
                    c_nb.start(e, n, p)
                    if p == 0:
                        rq_ev.at(e, n)
                    hs = slice(2 * p, 2 * p + 2)
                    c_nb.link(e.tensor_reduce(rmax[:, hs], both, AX.X, ALU.max, negate=True))
                    e_ev.at(e, n - 1, p + 1)
                    e.tensor_tensor(nb[:, hs], rmax[:, hs], rq[:, m, hs], ALU.mult).then_inc(m_ev.sem, 1)
                if eng == "scalar":
                    m_ev.at(e, n, p + 1)
                    nm_ev.at(e, n - 1, p // 2 + 1)
                    pt_mm.at(e, n - 1, p // 2 + 1)
                    pp_ev.at(e, n - 1, p // 2 + 1)
                    for h in range(2):
                        hh = 2 * p + h
                        ins = e.activation(pr[:, hh, :], both[:, h, :], ACT.Exp, bias=nb[:, hh:hh + 1],
                                           scale=rq[:, m, hh:hh + 1], accum_out=rs[:, hh:hh + 1])
                    ins.then_inc(e_ev.sem, 1)
            return job

        def over_sum(u):
            hs = slice(4 * u, 4 * u + 4)
            def job(eng, e, n, m):
                if eng == "vector":
                    e_ev.at(e, n, 2 * u + 2)
                    c_rc.start(e, n, u)
                    c_rc.link(e.reciprocal(rc[:, hs], rs[:, hs]))
                    e.tensor_tensor(pr[:, hs, :], pr[:, hs, :], wide(rc[:, hs], KW), ALU.mult)\
                        .then_inc(nm_ev.sem, 1)
                    nm_ev.at(e, n, u + 1)
                    pv_mm.at(e, n - 1, u // 2 + 1)
                    e.transpose(pTp[P - WIN:P, hs, :], pr[0:WIN, hs, 0:WIN]).then_inc(pp_ev.sem, 1)
            return job

        def turn_p(u):
            hs = slice(4 * u, 4 * u + 4)
            def job(eng, e, n, m):
                if eng == "tensor":
                    nm_ev.at(e, n, u + 1)
                    pt_ev.at(e, n, u) if u % 2 else oT_ev.at(e, *((n, 1) if u else (n - 1, 2)))
                    for j in range(4):
                        mm = e.transpose(ps[:, BANK_O, j * P:(j + 1) * P], pr[:, 4 * u + j, WIN:KW], ident[:])
                    mm.then_inc(pt_mm.sem, 1)
                if eng == "vector":
                    pt_mm.at(e, n, u + 1)
                    pv_mm.at(e, n - 1, u // 2 + 1)
                    e.tensor_copy(pT[:, hs, :], ps[:, BANK_O, :].rearrange("p (j t) -> p j t", j=4))\
                        .then_inc(pt_ev.sem, 1)
            return job

        def values(u):
            def job(eng, e, n, m):
                if eng == "tensor":
                    pt_ev.at(e, n, 2 * u + 2)
                    pp_ev.at(e, n, 2 * u + 2)
                    q_ev.at(e, n)
                    for before in range(2):
                        for j in range(8):
                            h = 8 * u + j
                            row, col = h % 2 * D, j // 2 * P
                            src, p = ((m - 1) % RING, pTp) if before else (m, pT)
                            mm = e.matmul(ps[row:row + D, BANK_O, col:col + (WIN if before else P)],
                                          v[:, src, h * D:(h + 1) * D], p[:, h, :],
                                          start=(not before and j < 2), stop=True, skip_group_check=True)
                    mm.then_inc(pv_mm.sem, 1)
                if eng == "scalar":
                    pv_mm.at(e, n, u + 1)
                    if u == 0:
                        wo_mm.at(e, n - 1)
                    e.activation(oT[:, 4 * u:4 * u + 4, :], ps[:, BANK_O, :].rearrange("p (j t) -> p j t", j=4),
                                 ACT.Copy).then_inc(oT_ev.sem, 1)
            return job

        def project(eng, e, n, m):
            cur = slot(n % NT)
            if eng == "tensor":
                oT_ev.at(e, n)
                w_o.at(e, layer(n))
                nT_ev.at(e, n - 1)
                for j in range(8):
                    mm = e.matmul(ps[:, BANK_Y, 0:E], oT[:, j, :], Wo[:, j, :], start=(j == 0), stop=(j == 7))
                mm.then_inc(wo_mm.sem, 1)
            if eng == "vector":
                wo_mm.at(e, n)
                e.tensor_tensor(Y[:, ds(cur, 1), :], ps[:, BANK_Y, 0:E], X[:, ds(cur, 1), :], ALU.add)\
                    .then_inc(y_ev.sem, 1)

        def shift_y(eng, e, n, m):
            cur = slot(n % NT)
            out = ps[:, BANK_Y, 0:E // 2]
            if eng == "tensor":
                y_ev.at(e, n)
                e.matmul(out, shift[:], Y[:, ds(cur, 1), E // 2:E], start=True, stop=False)
                e.matmul(out, last[:], Y[:, ds(cur - 1, 1), E // 2:E], start=False, stop=True)\
                    .then_inc(s2_mm.sem, 1)
            if eng == "scalar":
                s2_mm.at(e, n)
                yn_ev.at(e, n - 1)
                e.activation(ys[:, E // 2:E], out, ACT.Copy).then_inc(s2_ev.sem, 1)
            if eng == "gpsimd":
                y_ev.at(e, n)
                yn_ev.at(e, n - 1)
                e.tensor_copy(ys[:, 0:E // 2], Y[:, ds(cur, 1), 0:E // 2]).then_inc(yl_ev.sem, 1)

        def residual(eng, e, n, m):
            if eng == "gpsimd":
                y_ev.at(e, n)
                x_ev.at(e, n - RING)
                e.tensor_tensor(yb[:, m, :], Y[:, ds(slot(n % NT), 1), :], b2[:, ds(layer(n), 1), :], ALU.add)\
                    .then_inc(yb_ev.sem, 1)

        def statistics(eng, e, n, m):
            if eng == "vector":
                s2_ev.at(e, n)
                yl_ev.at(e, n)
                ln.chain.start(e, n)
                ln.stats(e, [ys[:]])
            if eng == "gpsimd":
                ln.rstd(e, 1, n)

        def normalize(eng, e, n, m):
            if eng == "vector":
                nT_mm.at(e, n - 1)
                ln.apply(e, [ys[:]], [yn[:]], n).then_inc(yn_ev.sem, 1)

        def turn_y(eng, e, n, m):
            if eng == "tensor":
                yn_ev.at(e, n)
                e.transpose(ps[:, BANK_Y, 0:E], yn[:], ident[:]).then_inc(nT_mm.sem, 1)
            if eng == "scalar":
                nT_mm.at(e, n)
                a_mm.at(e, n - RING)
                e.activation(ynT[:, m, :], ps[:, BANK_Y, 0:E], ACT.Identity, bias=lnb[:, ds(layer(n), 1)],
                             scale=lng[:, ds(layer(n), 1)]).then_inc(nT_ev.sem, 1)

        def gate(eng, e, n, m):
            if eng == "tensor":
                nT_ev.at(e, n)
                w_1.at(e, layer(n))
                x_ev.at(e, n - 1)
                for j, (c, w) in enumerate(PIECES):
                    mm = e.matmul(ps[0:w, BANK_G, j * P:(j + 1) * P], W1[:, HID + c:HID + c + w], ynT[:, m, :],
                                  start=True, stop=True)
                mm.then_inc(g_mm.sem, 1)
            if eng == "scalar":
                g_mm.at(e, n)
                a_ev.at(e, n - 1)
                for j, (c, w) in enumerate(PIECES):
                    ins = e.activation(gl[0:w, j, :], ps[0:w, BANK_G, j * P:(j + 1) * P], ACT.Gelu,
                                       bias=b1[0:w, 3 + j, ds(layer(n), 1)])
                ins.then_inc(g_ev.sem, 1)

        def gated(eng, e, n, m):
            if eng == "tensor":
                g_ev.at(e, n)
                for j, (c, w) in enumerate(PIECES):
                    mm = e.matmul(ps[0:w, BANK_G, j * P:(j + 1) * P], W1[:, c:c + w], ynT[:, m, :],
                                  start=True, stop=True)
                mm.then_inc(a_mm.sem, 1)
            if eng == "vector":
                a_mm.at(e, n)
                g_ev.at(e, n)
                f_mm.at(e, n - 1)
                for j, (c, w) in enumerate(PIECES):
                    ins = e.scalar_tensor_tensor(gT[0:w, j, :], ps[0:w, BANK_G, j * P:(j + 1) * P],
                                                 b1[0:w, j, ds(layer(n), 1)], gl[0:w, j, :], ALU.add, ALU.mult)
                ins.then_inc(a_ev.sem, 1)

        def down(eng, e, n, m):
            if eng == "tensor":
                a_ev.at(e, n)
                w_2.at(e, layer(n))
                for j, (c, w) in enumerate(PIECES):
                    mm = e.matmul(ps[:, BANK_G, 0:E], gT[0:w, j, :], W2[0:w, j, :], start=(j == 0), stop=(j == 2))
                mm.then_inc(f_mm.sem, 1)
            if eng == "vector":
                f_mm.at(e, n)
                yb_ev.at(e, n)
                if not isinstance(n, int) or n < TILES - 1:
                    sh_mm.at(e, n + 1)
                e.tensor_tensor(X[:, ds(slot(n % NT), 1), :], ps[:, BANK_G, 0:E], yb[:, m, :], ALU.add)\
                    .then_inc(x_ev.sem, 1)

        JOBS = {"carry": carry, "tables": tables, "shift_in": shift_in, "turn_in": turn_in, "norms": norms,
                "scale_q": scale_q, "project": project, "shift_y": shift_y, "residual": residual,
                "statistics": statistics, "normalize": normalize, "turn_y": turn_y, "gate": gate,
                "gated": gated, "down": down}
        for kind, count in ((qkv, 6), (swap, 2), (straight, 2), (rotated, 2), (turn_qk, 4), (scores, 8),
                            (over_sum, 4), (turn_p, 4), (values, 2)):
            for c in range(count):
                JOBS[f"{kind.__name__}{c}"] = kind(c)

        def tiles(eng, e):
            rounds(eng, e, ORDER, JOBS, TILES, RING)

        N_IN, N_TAB = 8, 3

        @block.sync
        def _(e):
            def qkv_in(l):
                e.dma_start(Wqkv[:, ds(l % 2, 1), :], a["L0_ffn_Wqkv"][ds(l, 1)].rearrange("l p n -> p l n"))\
                    .then_inc(w_qkv.sem, 16)
            def o_in(l):
                e.dma_start(Wo[:], a["L0_ffn_Wo"][ds(l, 1)].rearrange("l (c p) d -> p (l c) d", p=P))\
                    .then_inc(w_o.sem, 16)
            def w1_in(l):
                e.dma_start(W1[:], a["L0_ffn_W1"][ds(l, 1)].rearrange("l p n -> p (l n)")).then_inc(w_1.sem, 16)
            def w2_in(l):
                w2 = a["L0_ffn_W2"][ds(l, 1)]
                e.dma_start(W2[:, 0:2, :], w2[:, 0:2 * P, :].rearrange("l (c p) d -> p (l c) d", p=P))\
                    .then_inc(w_2.sem, 16)
                e.dma_start(W2[0:HID - 2 * P, 2, :], w2[:, 2 * P:HID, :].rearrange("l p d -> p (l d)"))\
                    .then_inc(w_2.sem, 16)
            for dst, src in ((lng, "lngT"), (lnb, "lnbT"), (b1, "b1T"), (shift, "c_shift"), (last, "c_last"),
                             (begins, "c_begins"), (mask32, "c_mask")):
                e.dma_start(dst[:], a[src]).then_inc(s_in, 16)
            e.dma_start(sq[:, 0, 0:P], a["c_ident"]).then_inc(s_in, 16)
            e.dma_start(rot[:], a["c_rot"]).then_inc(s_tab, 16)
            e.dma_start(scales[:], a["scales"].partition_broadcast(P)).then_inc(s_tab, 16)
            qkv_in(0)
            e.dma_start(b2[:], a["L0_ffn_b2"].partition_broadcast(P)).then_inc(s_tab, 16)
            o_in(0)
            w1_in(0)
            w2_in(0)
            qkv_in(1)

            def refill(l):
                wo_mm.at(e, l * NT - 1)
                o_in(l)
                a_mm.at(e, l * NT - 1)
                w1_in(l)
                f_mm.at(e, l * NT - 1)
                w2_in(l)
            with e.Fori(1, DEPTH - 1) as l:
                refill(l)
                qkv_in(l + 1)
            refill(DEPTH - 1)

        @block.gpsimd
        def _(e):
            xl_ev.open(e)
            rc_ev[0].open(e)
            rt_ev.open(e)
            kn_ev.open(e)
            yl_ev.open(e)
            yb_ev.open(e)
            rn_ev.open(e)
            for b in range(B):
                e.memset(Y[:, b * ZERO_SLOT, :], 0.0)
            ln.open(e)
            e.memset(power[:], -0.5)
            e.memset(pTp[:].rearrange("p a b -> p (a b)"), 0.0).then_inc(s_set, 1)
            e.wait_ge(s_in, 16 * N_IN)
            e.wait_ge(s_tab, 16 * N_TAB)
            e.wait_ge(s_set, 2)
            tiles("gpsimd", e)

        @block.vector
        def _(e):
            for ev in (x_ev, q_ss, rq_ev, rc_ev[1], rsw_ev, m_ev, pt_ev, pp_ev, y_ev, yn_ev, a_ev, nm_ev):
                ev.open(e)
            e.memset(qT[:].rearrange("p a b c -> p (a b c)"), 0.0)
            e.memset(kT[:, RING - 1, :, :], 0.0)
            e.memset(v[:, RING - 1, :], 0.0).then_inc(s_set, 1)
            e.wait_ge(s_in, 16 * N_IN)
            e.tensor_copy(mask[:, 0, :], mask32[:, 0, :])
            for i in range(1, TB):
                e.tensor_copy(mask[:, i, :], mask32[:, 1, :])
            e.tensor_copy(identb[:], sq[:, 0, 0:P]).then_inc(s_mask, 1)
            e.wait_ge(s_mask, 1)
            e.wait_ge(s_set, 2)
            tiles("vector", e)

        @block.scalar
        def _(e):
            for ev in (sh_ev, xT_ev, q_ev, q_sq, T_ev, e_ev, oT_ev, s2_ev, nT_ev, g_ev):
                ev.open(e)
            e.wait_ge(s_in, 16 * N_IN)
            e.wait_ge(s_set, 2)
            e.wait_ge(s_mask, 1)
            tiles("scalar", e)

        @block.tensor
        def _(e):
            for ev in (xT_mm, q_mm, T_mm, S_mm, pt_mm, pv_mm, wo_mm, s2_mm, nT_mm, g_mm, a_mm, f_mm):
                ev.open(e)
            e.wait_ge(s_in, 16 * N_IN)
            e.wait_ge(s_set, 2)
            e.wait_ge(s_mask, 1)
            tiles("tensor", e)


def last_output(nc, X, X2, out):
    STEPS = NT // G
    with Part(nc, "fi") as t:
        yn, res = t.sb("yn", [P, G, E]), t.sb("res", [P, 2, G, E])
        yn_ev, res_ev = t.ev("yn"), t.ev("re", 1, 1)
        sent = [t.ev(f"sent{u}", 16, 1) for u in range(2)]
        ln = LayerNorm(t, "ln", G)
        block = t.block()
        rows = out.rearrange("b (t p) d -> p (b t) d", p=P)

        def tiles_of(i):
            first = i * G + i // (TB // G) + 1
            return [X[:, ds(first + g, 1), :] for g in range(G)]

        def stats(eng, e, i, m):
            if eng == "vector":
                ln.chain.start(e, i)
                ln.stats(e, tiles_of(i))
            if eng == "gpsimd":
                ln.rstd(e, G, i)

        def add(eng, e, i, m):
            if eng == "vector":
                ln.apply(e, tiles_of(i), [yn[:, g, :] for g in range(G)], i).then_inc(yn_ev.sem, 1)
                yn_ev.at(e, i)
                sent[m].at(e, i // 2 - 1)
                e.tensor_tensor(res[:, m, :, :], X2[:, ds(i * G, G), :], yn[:], ALU.add)\
                    .then_inc(res_ev.sem, 1)
            if eng == "sync":
                res_ev.at(e, i)
                e.dma_start(rows[:, ds(i * G, G), :], res[:, m, :, :]).then_inc(sent[m].sem, 16)

        order = {"gpsimd": [("stats", 0)], "vector": [("add", 1), ("stats", 0)], "sync": [("add", 1)]}

        def steps(eng, e):
            rounds(eng, e, order, {"stats": stats, "add": add}, STEPS, 2)

        @block.vector
        def _(e):
            res_ev.open(e)
            steps("vector", e)

        @block.gpsimd
        def _(e):
            ln.open(e)
            steps("gpsimd", e)

        @block.sync
        def _(e):
            for u in range(2):
                sent[u].open(e)
            steps("sync", e)
            for u in range(2):
                sent[u].at(e, STEPS // 2 - 1)


def constants():
    r = np.arange(P)
    half = np.arange(0, D, 2, dtype=np.float32)
    inv_freq = (1.0 / np.float32(10000.0) ** (half / np.float32(D))).astype(np.float32)
    pos = np.arange(S, dtype=np.float32)
    freqs = pos[:, None] * inv_freq[None, :]
    base = (half + np.float32(0.4 * D)) / np.float32(1.4 * D)
    scale = base[None, :] ** ((pos - S // 2) / np.float32(WIN // 2))[:, None]
    cos, sin = np.cos(freqs), np.sin(freqs)
    tabs = []
    for s in (scale, 1.0 / scale):
        tabs += [np.concatenate([cos * s, cos * s], 1), np.concatenate([-sin * s, sin * s], 1)]
    rot = np.stack(tabs, 1).astype(np.float32)
    q, k = WIN + r[:, None], np.arange(KW)[None, :]
    seen = (k <= q) & (q - k <= WIN) & (k // WIN >= q // WIN - 1)
    masks = np.where(np.stack([seen & (k >= WIN), seen], 1), 0.0, NEG).astype(np.float32)
    begins = np.ones((P, TB), np.float32)
    begins[:, 0] = 0.0
    sel = np.zeros((P, D_A + 1), np.float32)
    for c in range(G):
        sel[WIN * c + np.arange(D_A + 1), np.arange(D_A + 1)] = 1.0
    return {
        "c_ident": np.eye(P, dtype=np.float32),
        "c_shift": np.eye(P, k=1, dtype=np.float32),
        "c_last": ((r[:, None] == P - 1) & (r[None, :] == 0)).astype(np.float32),
        "c_rot": np.ascontiguousarray(rot.reshape(TB, P, 4 * D).transpose(1, 0, 2)),
        "c_mask": np.ascontiguousarray(masks), "c_begins": begins, "c_sel": sel,
    }


_INS = ["L0_attn_x", "L0_attn_Wq", "L0_attn_bq", "L0_attn_Wk", "L0_attn_bk", "L0_attn_Wv", "L0_attn_bv",
        "L0_attn_Wo", "L0_attn_bo", "L0_ffn_Wqkv", "L0_ffn_Wo", "L0_ffn_W1", "L0_ffn_W2", "L0_ffn_b2"]


def layout(x):
    arrays = {n: np.ascontiguousarray(x[n]) for n in _INS}
    rel = np.asarray(x["L0_attn_rel_key"])
    arrays["relT"] = np.ascontiguousarray(rel.T)
    arrays["rel0"] = np.ascontiguousarray(np.tile(rel[0], H_A))
    qs, ks = np.asarray(x["L0_ffn_q_scale"]), np.asarray(x["L0_ffn_k_scale"])
    swap = lambda s: np.concatenate([s[:, D // 2:], s[:, :D // 2]], 1)
    arrays["scales"] = np.ascontiguousarray(np.concatenate([qs, swap(qs), ks, swap(ks)], 1))
    arrays["lngT"] = np.ascontiguousarray(np.asarray(x["L0_ffn_ln_g"]).T)
    arrays["lnbT"] = np.ascontiguousarray(np.asarray(x["L0_ffn_ln_b"]).T)
    b1 = np.asarray(x["L0_ffn_b1"])
    b1t = np.zeros((P, 2 * len(PIECES), DEPTH), b1.dtype)
    for half in range(2):
        for j, (c, w) in enumerate(PIECES):
            b1t[0:w, half * len(PIECES) + j, :] = b1[:, half * HID + c:half * HID + c + w].T
    arrays["b1T"] = b1t
    arrays.update(constants())
    return arrays


def kernel(**inputs):
    import concourse.bacc as bacc
    from concourse.bass_utils import run_bass_kernel_spmd

    nc = bacc.Bacc("TRN2", target_bir_lowering=False, num_devices=1)
    arrays = layout(inputs)
    aps = {n: nc.dram_tensor(f"in_{n}", v.shape, mybir.dt.from_np(v.dtype), kind="ExternalInput").ap()
           for n, v in arrays.items()}
    out = nc.dram_tensor("out", (B, S, E), F32, kind="ExternalOutput").ap()
    build(nc, aps, out)
    r = run_bass_kernel_spmd(nc, [{f"in_{n}": v for n, v in arrays.items()}], core_ids=[0])
    return r.results[0]["out"]
```
